# Optimizing a Trainium2 kernel written in Bass

```python
import numpy as np
import jax
import jax.numpy as jnp

def _softmax(x, axis=-1):
    return jax.nn.softmax(x, axis=axis)

def _gelu(x):
    return jax.nn.gelu(x, approximate=True)

def _silu(x):
    return jax.nn.silu(x)

def _sigmoid(x):
    return jax.nn.sigmoid(x)

def _layernorm(x, axis=-1, eps=1e-05):
    m = jnp.mean(x, axis=axis, keepdims=True)
    v = jnp.var(x, axis=axis, keepdims=True)
    return (x - m) / jnp.sqrt(v + eps)

def _scatter_add(tgt, idx, src, axis=0):
    return tgt.at[idx].add(src)

def _segment_sum(src, seg, n):
    return jax.ops.segment_sum(src, seg, n)
kernel_name = 'mk_gnn_resnorm_d4_gnn_r32_00016c'

def setup_inputs(seed: int=0):
    np.random.seed(seed)
    _w = jnp.asarray

    def _rec_inputs():
        import jax
        import jax.numpy as jnp
        _gk = jax.random.key(seed)
        x = -0.0003713 + 1 * jax.random.normal(jax.random.fold_in(_gk, 1), (3125, 128), jnp.float32)
        src = jax.random.randint(jax.random.fold_in(_gk, 2), (100000,), 0, 3125, jnp.int32)
        dst = jnp.minimum((3125 * jax.random.uniform(jax.random.fold_in(_gk, 3), (100000,)) ** 2.0).astype(jnp.int32), 99999)
        _o = jnp.argsort(dst, stable=True)
        src = src[_o]
        dst = dst[_o]
        edge_weight = jax.random.uniform(jax.random.fold_in(_gk, 13), (100000,), jnp.float32, 0.0, 1)
        return (x, src, dst, edge_weight)
    x, src, dst, edge_weight = _rec_inputs()

    def _L0_gnn_setup():
        import jax, jax.numpy as jnp
        import numpy as np
        N_NODES = 3125
        HOP = 3

        def _spmm(edge_row, edge_col, edge_vals, emb):
            msgs = edge_vals[:, None] * emb[edge_col]
            return jax.ops.segment_sum(msgs, edge_row, num_segments=N_NODES)
        key = jax.random.key(seed)
        k1, k2, k3, k4 = jax.random.split(key, 4)
        n_edges = 100000
        users_emb = jax.random.normal(k1, (N_NODES, 128), dtype=jnp.float32)
        edge_row = jax.random.randint(k2, (n_edges,), 0, N_NODES, dtype=jnp.int64)
        edge_col = jax.random.randint(k3, (n_edges,), 0, N_NODES, dtype=jnp.int64)
        edge_vals = jax.random.uniform(k4, (n_edges,), dtype=jnp.float32)
        return {'users_emb': users_emb, 'edge_row': edge_row, 'edge_col': edge_col, 'edge_vals': edge_vals}
    _L0_gnn_all = _L0_gnn_setup()
    _L0_gnn_in = {k: v for k, v in _L0_gnn_all.items() if k in ()}
    del _L0_gnn_all

    def _L1_gnn_setup():
        import jax, jax.numpy as jnp
        import numpy as np
        N = 3125
        E = 50000
        IN_D = 128
        OUT_D = 32
        H = 4
        NEG_SLOPE = 0.2
        key = jax.random.key(seed)
        k0, k1, k2, k3, k4 = jax.random.split(key, 5)
        features = jax.random.normal(k0, (N, IN_D), dtype=jnp.float32)
        edge_index = jax.random.randint(k1, (2, E), 0, N, dtype=jnp.int32)
        W = jax.random.normal(k2, (OUT_D, IN_D), dtype=jnp.float32) * 0.05
        b = jnp.zeros((OUT_D,), dtype=jnp.float32)
        att_src = jax.random.normal(k3, (H, OUT_D), dtype=jnp.float32) * 0.05
        att_dst = jax.random.normal(k4, (H, OUT_D), dtype=jnp.float32) * 0.05
        return {'features': features, 'W': W, 'b': b, 'att_src': att_src, 'att_dst': att_dst, 'edge_index': edge_index}
    _L1_gnn_all = _L1_gnn_setup()
    _L1_gnn_in = {k: v for k, v in _L1_gnn_all.items() if k in ('W', 'b', 'att_src', 'att_dst')}
    del _L1_gnn_all

    def _L2_gnn_setup():
        import jax, jax.numpy as jnp
        import numpy as np
        N_NODES = 3125
        IN_DIM = 128
        HID_DIM = 128
        N_EDGES = 25000
        BN_EPS = 1e-05
        key = jax.random.key(seed)
        ks = jax.random.split(key, 8)
        x = jax.random.normal(ks[0], (N_NODES, IN_DIM), dtype=jnp.float32)
        edge_index = jax.random.randint(ks[1], (2, N_EDGES), 0, N_NODES, dtype=jnp.int64)
        s1 = 1.0 / np.sqrt(IN_DIM)
        W1 = jax.random.uniform(ks[2], (IN_DIM, HID_DIM), jnp.float32, -s1, s1)
        b1 = jax.random.uniform(ks[3], (HID_DIM,), jnp.float32, -s1, s1)
        gamma = jnp.ones((HID_DIM,), jnp.float32)
        beta = jnp.zeros((HID_DIM,), jnp.float32)
        s2 = 1.0 / np.sqrt(HID_DIM)
        W2 = jax.random.uniform(ks[4], (HID_DIM, HID_DIM), jnp.float32, -s2, s2)
        b2 = jax.random.uniform(ks[5], (HID_DIM,), jnp.float32, -s2, s2)
        return {'x': x, 'edge_index': edge_index, 'W1': W1, 'b1': b1, 'gamma': gamma, 'beta': beta, 'W2': W2, 'b2': b2}
    _L2_gnn_all = _L2_gnn_setup()
    _L2_gnn_in = {k: v for k, v in _L2_gnn_all.items() if k in ('W1', 'b1', 'gamma', 'beta', 'W2', 'b2')}
    del _L2_gnn_all

    def _L3_gnn_setup():
        import jax, jax.numpy as jnp
        import numpy as np
        N_NODES = 50000
        N_EDGES = 12500
        D = 128
        NUM_LAYERS = 3
        DELTA = 4.0
        BN_EPS = 1e-05
        LN_EPS = 1e-05
        STD_EPS = 1e-30
        N_AGG = 4
        N_SCAL = 3

        def _pna_layer(h, src, dst, Mw, Mb, Uw, Ub, bn_g, bn_b, mix_w, mix_b):
            N = h.shape[0]
            msg = jnp.concatenate([h[src], h[dst]], axis=-1) @ Mw.T + Mb
            deg = jax.ops.segment_sum(jnp.ones((msg.shape[0],), msg.dtype), dst, num_segments=N)
            s1 = jax.ops.segment_sum(msg, dst, num_segments=N)
            s2 = jax.ops.segment_sum(msg * msg, dst, num_segments=N)
            mx = jax.ops.segment_max(msg, dst, num_segments=N)
            mn = jax.ops.segment_min(msg, dst, num_segments=N)
            degc = deg[:, None]
            mean = s1 / degc
            var = jax.nn.relu(s2 / degc - mean * mean)
            std = jnp.sqrt(var + STD_EPS)
            agg = jnp.concatenate([mx, mn, std, var], axis=-1)
            logd = jnp.log(deg + 1.0)[:, None]
            h_neigh = jnp.concatenate([agg, agg * (logd / DELTA), agg * (DELTA / logd)], axis=-1)
            u = jnp.concatenate([h, h_neigh], axis=-1) @ Uw.T + Ub
            u = u * jnp.sqrt(1.0 / N)
            mu = jnp.mean(u, axis=0)
            v = jnp.mean((u - mu) ** 2, axis=0)
            u = (u - mu) / jnp.sqrt(v + BN_EPS) * bn_g + bn_b
            out = jax.nn.leaky_relu(u @ mix_w.T + mix_b, 0.01)
            return out + h
        key = jax.random.key(seed)
        ks = jax.random.split(key, 8)
        L = NUM_LAYERS
        s = 0.05
        feat = jax.random.normal(ks[0], (N_NODES, D), jnp.float32)
        src = jax.random.randint(ks[1], (N_EDGES,), 0, N_NODES, dtype=jnp.int32)
        dst = jax.random.randint(ks[2], (N_EDGES,), 0, N_NODES, dtype=jnp.int32)
        u_in = (N_AGG * N_SCAL + 1) * D
        Mw = jax.random.normal(ks[3], (L, D, 2 * D), jnp.float32) * s
        Mb = jnp.zeros((L, D), jnp.float32)
        Uw = jax.random.normal(ks[4], (L, D, u_in), jnp.float32) * s
        Ub = jnp.zeros((L, D), jnp.float32)
        bn_g = jnp.ones((L, D), jnp.float32)
        bn_b = jnp.zeros((L, D), jnp.float32)
        mix_w = jax.random.normal(ks[5], (L, D, D), jnp.float32) * s
        mix_b = jnp.zeros((L, D), jnp.float32)
        ln_g = jnp.ones((L, D), jnp.float32)
        ln_b = jnp.zeros((L, D), jnp.float32)
        return dict(feat=feat, src=src, dst=dst, Mw=Mw, Mb=Mb, Uw=Uw, Ub=Ub, bn_g=bn_g, bn_b=bn_b, mix_w=mix_w, mix_b=mix_b, ln_g=ln_g, ln_b=ln_b)
    _L3_gnn_all = _L3_gnn_setup()
    _L3_gnn_in = {k: v for k, v in _L3_gnn_all.items() if k in ('Mw', 'Mb', 'Uw', 'Ub', 'bn_g', 'bn_b', 'mix_w', 'mix_b', 'ln_g', 'ln_b')}
    del _L3_gnn_all
    return {'x': x, 'src': src, 'dst': dst, 'edge_weight': edge_weight, 'L1_gnn_W': _L1_gnn_in['W'], 'L1_gnn_b': _L1_gnn_in['b'], 'L1_gnn_att_src': _L1_gnn_in['att_src'], 'L1_gnn_att_dst': _L1_gnn_in['att_dst'], 'L2_gnn_W1': _L2_gnn_in['W1'], 'L2_gnn_b1': _L2_gnn_in['b1'], 'L2_gnn_gamma': _L2_gnn_in['gamma'], 'L2_gnn_beta': _L2_gnn_in['beta'], 'L2_gnn_W2': _L2_gnn_in['W2'], 'L2_gnn_b2': _L2_gnn_in['b2'], 'L3_gnn_Mw': _L3_gnn_in['Mw'], 'L3_gnn_Mb': _L3_gnn_in['Mb'], 'L3_gnn_Uw': _L3_gnn_in['Uw'], 'L3_gnn_Ub': _L3_gnn_in['Ub'], 'L3_gnn_bn_g': _L3_gnn_in['bn_g'], 'L3_gnn_bn_b': _L3_gnn_in['bn_b'], 'L3_gnn_mix_w': _L3_gnn_in['mix_w'], 'L3_gnn_mix_b': _L3_gnn_in['mix_b'], 'L3_gnn_ln_g': _L3_gnn_in['ln_g'], 'L3_gnn_ln_b': _L3_gnn_in['ln_b']}

def reference(x, src, dst, edge_weight, L1_gnn_W, L1_gnn_b, L1_gnn_att_src, L1_gnn_att_dst, L2_gnn_W1, L2_gnn_b1, L2_gnn_gamma, L2_gnn_beta, L2_gnn_W2, L2_gnn_b2, L3_gnn_Mw, L3_gnn_Mb, L3_gnn_Uw, L3_gnn_Ub, L3_gnn_bn_g, L3_gnn_bn_b, L3_gnn_mix_w, L3_gnn_mix_b, L3_gnn_ln_g, L3_gnn_ln_b):
    import jax
    import jax.numpy as jnp

    def _L0_gnn_ref(users_emb, edge_row, edge_col, edge_vals):
        import jax, jax.numpy as jnp
        import numpy as np
        N_NODES = 3125
        HOP = 3

        def _spmm(edge_row, edge_col, edge_vals, emb):
            msgs = edge_vals[:, None] * emb[edge_col]
            return jax.ops.segment_sum(msgs, edge_row, num_segments=N_NODES)
        acc = users_emb
        emb = users_emb
        for _ in range(HOP):
            emb = _spmm(edge_row, edge_col, edge_vals, emb)
            acc = acc + emb
        return acc / jnp.asarray(HOP + 1, dtype=users_emb.dtype)

    def _L1_gnn_ref(features, W, b, att_src, att_dst, edge_index):
        import jax, jax.numpy as jnp
        import numpy as np
        N = 3125
        E = 50000
        IN_D = 128
        OUT_D = 32
        H = 4
        NEG_SLOPE = 0.2
        src = edge_index[0]
        dst = edge_index[1]
        Wh = features @ W.T + b
        a_src = Wh @ att_src.T
        a_dst = Wh @ att_dst.T
        e = a_src[src] + a_dst[dst]
        e = jnp.where(e > 0, e, NEG_SLOPE * e)
        e = e - jnp.max(e)
        exp_e = jnp.exp(e)
        denom = jax.ops.segment_sum(exp_e, src, num_segments=N)
        alpha = exp_e / (denom[src] + 1e-16)
        msg = Wh[src][:, None, :] * alpha[:, :, None]
        out = jax.ops.segment_sum(msg, dst, num_segments=N)
        return out.reshape(N, H * OUT_D)

    def _L2_gnn_ref(x, edge_index, W1, b1, gamma, beta, W2, b2):
        import jax, jax.numpy as jnp
        import numpy as np
        N_NODES = 3125
        IN_DIM = 128
        HID_DIM = 128
        N_EDGES = 25000
        BN_EPS = 1e-05
        src = edge_index[0]
        dst = edge_index[1]
        agg = jax.ops.segment_sum(x[src], dst, num_segments=x.shape[0])
        h = agg + x
        h = h @ W1 + b1
        mean = jnp.mean(h, axis=0)
        var = jnp.var(h, axis=0)
        h = (h - mean) * jax.lax.rsqrt(var + BN_EPS) * gamma + beta
        h = jax.nn.relu(h)
        h = h @ W2 + b2
        return jax.nn.relu(h)

    def _L3_gnn_ref(feat, src, dst, Mw, Mb, Uw, Ub, bn_g, bn_b, mix_w, mix_b, ln_g, ln_b):
        import jax, jax.numpy as jnp
        import numpy as np
        N_NODES = 50000
        N_EDGES = 12500
        D = 128
        NUM_LAYERS = 3
        DELTA = 4.0
        BN_EPS = 1e-05
        LN_EPS = 1e-05
        STD_EPS = 1e-30
        N_AGG = 4
        N_SCAL = 3

        def _pna_layer(h, src, dst, Mw, Mb, Uw, Ub, bn_g, bn_b, mix_w, mix_b):
            N = h.shape[0]
            msg = jnp.concatenate([h[src], h[dst]], axis=-1) @ Mw.T + Mb
            deg = jax.ops.segment_sum(jnp.ones((msg.shape[0],), msg.dtype), dst, num_segments=N)
            s1 = jax.ops.segment_sum(msg, dst, num_segments=N)
            s2 = jax.ops.segment_sum(msg * msg, dst, num_segments=N)
            mx = jax.ops.segment_max(msg, dst, num_segments=N)
            mn = jax.ops.segment_min(msg, dst, num_segments=N)
            degc = deg[:, None]
            mean = s1 / degc
            var = jax.nn.relu(s2 / degc - mean * mean)
            std = jnp.sqrt(var + STD_EPS)
            agg = jnp.concatenate([mx, mn, std, var], axis=-1)
            logd = jnp.log(deg + 1.0)[:, None]
            h_neigh = jnp.concatenate([agg, agg * (logd / DELTA), agg * (DELTA / logd)], axis=-1)
            u = jnp.concatenate([h, h_neigh], axis=-1) @ Uw.T + Ub
            u = u * jnp.sqrt(1.0 / N)
            mu = jnp.mean(u, axis=0)
            v = jnp.mean((u - mu) ** 2, axis=0)
            u = (u - mu) / jnp.sqrt(v + BN_EPS) * bn_g + bn_b
            out = jax.nn.leaky_relu(u @ mix_w.T + mix_b, 0.01)
            return out + h
        N = feat.shape[0]
        loops = jnp.arange(N, dtype=src.dtype)
        src_sl = jnp.concatenate([src, loops])
        dst_sl = jnp.concatenate([dst, loops])
        h = feat
        for l in range(NUM_LAYERS):
            h = _pna_layer(h, src_sl, dst_sl, Mw[l], Mb[l], Uw[l], Ub[l], bn_g[l], bn_b[l], mix_w[l], mix_b[l])
            mu = jnp.mean(h, axis=-1, keepdims=True)
            v = jnp.mean((h - mu) ** 2, axis=-1, keepdims=True)
            h = (h - mu) / jnp.sqrt(v + LN_EPS) * ln_g[l] + ln_b[l]
            h = jax.nn.elu(h)
        return h
    edge_index = jnp.stack([src, dst])
    x = _layernorm(x + _L0_gnn_ref(x, src, dst, edge_weight), axis=-1)
    x = _layernorm(x + _L1_gnn_ref(x, L1_gnn_W, L1_gnn_b, L1_gnn_att_src, L1_gnn_att_dst, edge_index), axis=-1)
    x = _layernorm(x + _L2_gnn_ref(x, edge_index, L2_gnn_W1, L2_gnn_b1, L2_gnn_gamma, L2_gnn_beta, L2_gnn_W2, L2_gnn_b2), axis=-1)
    x = _layernorm(x + _L3_gnn_ref(x, src, dst, L3_gnn_Mw, L3_gnn_Mb, L3_gnn_Uw, L3_gnn_Ub, L3_gnn_bn_g, L3_gnn_bn_b, L3_gnn_mix_w, L3_gnn_mix_b, L3_gnn_ln_g, L3_gnn_ln_b), axis=-1)
    return x

_drawn_inputs = setup_inputs


def setup_inputs(seed=0):
    import zlib

    import numpy as np

    out = dict(_drawn_inputs(seed))
    spreads = {'L1_gnn_b': (0.0, 0.1),
     'L2_gnn_gamma': (1.0, 0.2),
     'L2_gnn_beta': (0.0, 0.1),
     'L3_gnn_Mb': (0.0, 0.537),
     'L3_gnn_Ub': (0.0, 0.8),
     'L3_gnn_bn_g': (1.0, 0.2),
     'L3_gnn_bn_b': (0.0, 0.1),
     'L3_gnn_mix_b': (0.0, 0.1),
     'L3_gnn_ln_g': (1.0, 0.2),
     'L3_gnn_ln_b': (0.0, 0.1)}
    factors = {'L1_gnn_att_src': 5.232, 'L2_gnn_b1': 8.0}
    for name, (base, spread) in spreads.items():
        noise = np.random.default_rng([zlib.crc32(name.encode()), seed]).standard_normal(out[name].shape)
        drawn = base * np.exp(spread * noise) if base else spread * noise
        out[name] = jnp.asarray(drawn.astype(out[name].dtype))
    for name, factor in factors.items():
        out[name] = (out[name] * factor).astype(out[name].dtype)
    return out
```

```python
import concourse.bass as bass
from concourse import mybir
from contextlib import ExitStack

FP32 = mybir.dt.float32
BF16 = mybir.dt.bfloat16
FP16 = mybir.dt.float16
INT32 = mybir.dt.int32
ALU = mybir.AluOpType
ACT = mybir.ActivationFunctionType
AX = mybir.AxisListType

P = 128
N_NODES = 3125
FEAT = 128
NT = -(-N_NODES // P)
NP = NT * P
N_EDGES = 100000
EI = 512
EP = -(-N_EDGES // EI) * EI
ET = EP // P
WIN = 16
CELLS = WIN * NT
NWIN = NP // WIN
PER = P // WIN
STEPS = N_EDGES // P + NWIN
SG = -(-STEPS // P)
CHUNK = 400
NC = NP // CHUNK
BIG = 1e30


class Chain:

    def __init__(self, eng, sem, base=0):
        self.eng, self.sem, self.n = eng, sem, base

    def __call__(self, ins):
        ins.then_inc(self.sem, 1)
        self.n = self.n + 1
        self.eng.wait_ge(self.sem, self.n)


def windows_and_steps(nc, io, st):
    with ExitStack() as ctx:
        def sb(name, shape, dt):
            return ctx.enter_context(nc.sbuf_tensor(name, shape, dt))

        def sem(name):
            return ctx.enter_context(nc.semaphore(name))

        last_i = sb("last_i", [P, ET], INT32)
        last_f = sb("last_f", [P, ET], FP32)
        junk = sb("cmp_junk", [P, ET], FP32)
        node_p1_i = sb("node_p1_i", [P, NT], INT32)
        node_p1 = sb("node_p1", [P, NT], FP32)
        step_i = sb("step_i", [P, SG], INT32)
        step_f = sb("step_f", [P, SG], FP32)
        win_thr_i = sb("win_thr_i", [P, 2], INT32)
        win_thr = sb("win_thr", [P, 2], FP32)
        win_tile = sb("win_tile", [P, 2], FP32)
        win_end_i = sb("win_end_i", [P, 2], INT32)
        ends_bi = sb("ends_bi", [P, NWIN], INT32)
        ends_b = sb("ends_b", [P, NWIN], FP32)
        node_tile = sb("node_tile", [P, NT], FP32)
        node_tile_i = sb("node_tile_i", [P, NT], INT32)
        node_rows_i = sb("node_rows_i", [P, NT, P], INT32)
        node_rows = sb("node_rows", [P, P], FP32)
        node_cnt = sb("node_cnt", [P, NT], FP32)
        end_f = sb("end_f", [P, NT], FP32)
        win_of = sb("win_of", [P, SG], FP32)
        tile_of = sb("tile_of", [P, SG], FP32)
        tile_of_i = sb("tile_of_i", [P, SG], INT32)
        src_s = sb("src_s", [P, SG, P], INT32)
        dst_s = sb("dst_s", [P, SG, P], INT32)
        wgt_s = sb("wgt_s", [P, SG, P], FP32)
        shi_i = sb("shi_i", [P, SG, P], INT32)
        slo_i = sb("slo_i", [P, SG, P], INT32)
        part_b = sb("part_b", [P, SG, P], BF16)
        tabs = [sb(f"step_tab{i}", [P, SG, P], FP32) for i in range(5)]
        key_f, slo_f, whi_f, wmid_f, wlo_f = tabs
        dst_cur = sb("dst_cur", [P, EP // P], INT32)
        dst_prev = sb("dst_prev", [P, EP // P], INT32)
        differs = sb("differs", [P, EP // P], FP32)
        pens = sb("start_pens", [P, 2, EP // P], BF16)
        zero_row = sb("zero_row", [1, P], FP32)
        psT = [ctx.enter_context(nc.psum_tensor(f"psT{i}", [P, 512], FP32)) for i in range(2)]

        s_const = sem("p0_const")
        s_last = sem("p0_last")
        s_dst = sem("p0_dst")
        s_chain = sem("p0_chain")
        s_wend = sem("p0_wend")
        s_wout = sem("p0_wout")
        s_wback = sem("p0_wback")
        s_nidx = sem("p0_nidx")
        s_ngat = sem("p0_ngat")
        s_sidx = sem("p0_sidx")
        s_sgat = sem("p0_sgat")
        s_end = sem("p0_end")
        s_eout = sem("p0_eout")
        s_pen = sem("p0_pen")
        s_pout = sem("p0_pout")
        s_tabs = sem("p0_tabs")
        s_tr = sem("p0_tr")
        s_ev = sem("p0_ev")
        s_zout = sem("p0_zero_out")

        with nc.Block() as block:
            @block.sync
            def _(sp):
                sp.dma_start(last_i[:, :], io["dst_last"].to_broadcast((P, ET))).then_inc(s_last, 16)
                sp.dma_start(dst_cur[:, :], io["dst_pad"][1:EP + 1].rearrange("(p c) -> p c", p=P)).then_inc(s_dst, 16)
                sp.dma_start(dst_prev[:, :], io["dst_pad"][0:EP].rearrange("(p c) -> p c", p=P)).then_inc(s_dst, 16)
                sp.wait_ge(s_wend, 1)
                with nc.allow_non_contiguous_dma(reason="256 words"):
                    sp.dma_start(st["win_ends"][0:2 * P].rearrange("(j p) -> p j", p=P), win_end_i[:, :]).then_inc(s_wout, 16)
                sp.wait_ge(s_wout, 16)
                sp.dma_start(ends_bi[:, :], st["win_ends"][0:NWIN].rearrange("(a n) -> a n", a=1).to_broadcast((P, NWIN))).then_inc(s_wback, 16)
                sp.dma_start(st["ends_row"][0:1, 1:NWIN + 1], st["win_ends"][0:NWIN].rearrange("(a n) -> a n", a=1)).then_inc(s_wback, 16)
                sp.wait_ge(s_pen, 2)
                for i in range(2):
                    sp.dma_start(st["pens"][i, :].rearrange("(p c) -> p c", p=P), pens[:, i, :]).then_inc(s_pout, 16)
                sp.wait_ge(s_end, 1)
                with nc.allow_non_contiguous_dma(reason="3200 words"):
                    sp.dma_start(st["node_ends"][P:P + NP].rearrange("(g p) -> p g", p=P), end_f[:, :]).then_inc(s_eout, 16)
                sp.wait_ge(s_eout, 16)
                sp.wait_ge(s_pout, 32)
                sp.wait_ge(s_wback, 32)

            @block.gpsimd
            def _(pool):
                pool.iota(node_p1_i[:, :], pattern=[[P, NT]], base=1, channel_multiplier=1).then_inc(s_const, 1)
                pool.iota(step_i[:, :], pattern=[[P, SG]], base=0, channel_multiplier=1).then_inc(s_const, 1)
                pool.iota(win_thr_i[:, :], pattern=[[P * WIN, 2]], base=WIN, channel_multiplier=WIN).then_inc(s_const, 1)
                pool.memset(st["ident"][:, :], 0.0).then_inc(s_const, 1)
                pool.wait_ge(s_const, 4)
                pool.affine_select(out=st["ident"][:, :], in_=st["ident"][:, :], compare_op=ALU.not_equal, fill=1.0,
                                   base=0, pattern=[[-1, P]], channel_multiplier=1).then_inc(s_const, 1)
                pool.iota(st["cell_iota"][:, :], pattern=[[1, CELLS]], base=0, channel_multiplier=0,
                          allow_small_or_imprecise_dtypes=True).then_inc(s_const, 1)
                pool.memset(st["ends_row"][0:1, 0:1], 0).then_inc(s_const, 1)
                pool.memset(zero_row[:, :], 0.0).then_inc(s_const, 1)
                pool.wait_ge(s_nidx, 1)
                for g in range(NT):
                    pool.indirect_dma_start(out=node_rows_i[:, g, :], out_offset=None, in_=io["dst_tiles"],
                                            in_offset=bass.IndirectOffsetOnAxis(ap=node_tile_i[:, g:g + 1], axis=0)).then_inc(s_ngat, 16)
                pool.wait_ge(s_sidx, 1)
                for g in range(SG):
                    for table, rows in ((io["src_tiles"], src_s), (io["dst_tiles"], dst_s), (io["wgt_tiles"], wgt_s)):
                        pool.indirect_dma_start(out=rows[:, g, :], out_offset=None, in_=table,
                                                in_offset=bass.IndirectOffsetOnAxis(ap=tile_of_i[:, g:g + 1], axis=0)).then_inc(s_sgat, 16)

            @block.vector
            def _(dve):
                link = Chain(dve, s_chain)
                dve.wait_ge(s_const, 7)
                link(dve.tensor_copy(node_p1[:, :], node_p1_i[:, :]))
                link(dve.tensor_copy(step_f[:, :], step_i[:, :]))
                link(dve.tensor_copy(win_thr[:, :], win_thr_i[:, :]))
                dve.wait_ge(s_last, 16)
                link(dve.tensor_copy(last_f[:, :], last_i[:, :]))
                for j in range(2):
                    link(dve.tensor_scalar(junk[:, :], last_f[:, :], win_thr[:, j:j + 1], 0.0, ALU.is_lt, ALU.add,
                                           accum_out=win_tile[:, j:j + 1]))
                dve.scalar_tensor_tensor(win_end_i[:, :], win_thr[:, :], 1.0 / WIN, win_tile[:, :], ALU.mult, ALU.add).then_inc(s_wend, 1)
                for g in range(NT):
                    link(dve.tensor_scalar(junk[:, :], last_f[:, :], node_p1[:, g:g + 1], 0.0, ALU.is_lt, ALU.add,
                                           accum_out=node_tile[:, g:g + 1]))
                dve.tensor_copy(node_tile_i[:, :], node_tile[:, :]).then_inc(s_nidx, 1)
                dve.wait_ge(s_wback, 32)
                link(dve.tensor_copy(ends_b[:, :], ends_bi[:, :]))
                for g in range(SG):
                    link(dve.tensor_scalar(junk[:, 0:NWIN], ends_b[:, :], step_f[:, g:g + 1], 0.0, ALU.is_le, ALU.add,
                                           accum_out=win_of[:, g:g + 1]))
                link(dve.tensor_tensor(tile_of[:, :], step_f[:, :], win_of[:, :], ALU.subtract))
                dve.tensor_scalar(tile_of_i[:, :], tile_of[:, :], float(ET - 1), None, ALU.min).then_inc(s_sidx, 1)
                dve.wait_ge(s_dst, 32)
                link(dve.tensor_tensor(differs[:, :], dst_cur[:, :], dst_prev[:, :], ALU.not_equal))
                dve.tensor_scalar(pens[:, 0, :], differs[:, :], -BIG, None, ALU.mult).then_inc(s_pen, 1)
                dve.tensor_scalar(pens[:, 1, :], differs[:, :], BIG, None, ALU.mult).then_inc(s_pen, 1)
                for g in range(NT):
                    dve.wait_ge(s_ngat, 16 * NT)
                    link(dve.tensor_copy(node_rows[:, :], node_rows_i[:, g, :]))
                    link(dve.tensor_scalar(junk[:, 0:P], node_rows[:, :], node_p1[:, g:g + 1], 0.0, ALU.is_lt, ALU.add,
                                           accum_out=node_cnt[:, g:g + 1]))
                link(dve.scalar_tensor_tensor(end_f[:, :], node_tile[:, :], float(P), node_cnt[:, :], ALU.mult, ALU.add))
                dve.tensor_scalar(st["last_edge"][:, :], end_f[:, :], -1.0, 0.0, ALU.add, ALU.max).then_inc(s_end, 1)
                dve.wait_ge(s_sgat, 16 * 3 * SG)
                link(dve.tensor_scalar(shi_i[:, :, :], src_s[:, :, :], 7, None, ALU.arith_shift_right))
                link(dve.tensor_scalar(slo_i[:, :, :], src_s[:, :, :], P - 1, None, ALU.bitwise_and))
                link(dve.tensor_copy(slo_f[:, :, :], slo_i[:, :, :]))
                link(dve.scalar_tensor_tensor(key_f[:, :, :], dst_s[:, :, :], float(NT), shi_i[:, :, :], ALU.mult, ALU.add))
                link(dve.tensor_scalar(win_of[:, :], win_of[:, :], -float(CELLS), None, ALU.mult))
                for g in range(SG):
                    link(dve.tensor_scalar(key_f[:, g, :], key_f[:, g, :], win_of[:, g:g + 1], None, ALU.add))
                link(dve.tensor_copy(part_b[:, :, :], wgt_s[:, :, :]))
                link(dve.tensor_copy(whi_f[:, :, :], part_b[:, :, :]))
                link(dve.tensor_tensor(wgt_s[:, :, :], wgt_s[:, :, :], whi_f[:, :, :], ALU.subtract))
                link(dve.tensor_copy(part_b[:, :, :], wgt_s[:, :, :]))
                link(dve.tensor_copy(wmid_f[:, :, :], part_b[:, :, :]))
                dve.tensor_tensor(wlo_f[:, :, :], wgt_s[:, :, :], wmid_f[:, :, :], ALU.subtract).then_inc(s_tabs, 1)

            @block.tensor
            def _(pe):
                pe.wait_ge(s_const, 5)
                pe.wait_ge(s_tabs, 1)
                for n in range(5 * SG // 4):
                    if n >= 2:
                        pe.wait_ge(s_ev, n - 1)
                    for q in range(4):
                        i, g = divmod(4 * n + q, SG)
                        last = pe.transpose(psT[n % 2][:, q * P:(q + 1) * P], tabs[i][:, g, :], st["ident"][:, :])
                    last.then_inc(s_tr, 1)

            @block.scalar
            def _(act):
                act.wait_ge(s_const, 8)
                act.dma_start(st["node_ends"][0:P].rearrange("(a n) -> a n", a=1), zero_row[:, :]).then_inc(s_zout, 16)
                for n in range(5 * SG // 4):
                    i, g = divmod(4 * n, SG)
                    act.wait_ge(s_tr, n + 1)
                    act.copy(st["steps"][:, i, g * P:(g + 4) * P], psT[n % 2][:, :]).then_inc(s_ev, 1)
                act.wait_ge(s_zout, 16)


def build_adjacency(nc, st):
    RING = 8
    with ExitStack() as ctx:
        def sb(name, shape, dt):
            return ctx.enter_context(nc.sbuf_tensor(name, shape, dt))

        def sem(name):
            return ctx.enter_context(nc.semaphore(name))

        cells = sb("cells", [P, RING, CELLS], BF16)
        rows = sb("rows", [P, RING, 4 * P], BF16)
        stage_c = sb("stage_c", [P, 2, NT, P], FP32)
        stage_a = sb("stage_a", [P, 2, NT, P], FP32)
        stage_t = sb("stage_t", [P, 2, NP], FP32)
        zero_b = sb("zero_b", [P, P], BF16)
        ps_c = [ctx.enter_context(nc.psum_tensor(f"ps_c{i}", [P, 512], FP32)) for i in range(2)]
        ps_a = [ctx.enter_context(nc.psum_tensor(f"ps_a{i}", [P, 512], FP32)) for i in range(2)]
        ps_t = [ctx.enter_context(nc.psum_tensor(f"ps_t{i}", [P, 512], FP32)) for i in range(2)]
        s_zero = sem("p1_zero")
        s_made = sem("p1_made")
        s_used = sem("p1_used")
        s_win = sem("p1_window_summed")
        s_free = sem("p1_window_copied")
        s_tr = sem("p1_transposed")
        s_trc = sem("p1_transpose_copied")
        s_cout = [sem(f"p1_c_out{i}") for i in range(2)]
        s_tout = [sem(f"p1_t_out{i}") for i in range(2)]
        TB = -(-NT // 4)

        def over_tiles(eng, body):
            with eng.Fori(0, NT // 2) as half:
                body(half * 2, 0)
                body(half * 2 + 1, 1)
            body(NT - 1, 0)

        with nc.Block() as block:
            @block.vector
            def _(dve):
                dve.memset(zero_b[:, :], 0.0).then_inc(s_zero, 1)

                def make(k, slot):
                    steps = st["steps"]
                    dve.tensor_scalar(cells[:, slot, :], st["cell_iota"][:, :], steps[:, 0, bass.ds(k, 1)], None, ALU.is_equal)
                    dve.tensor_scalar(rows[:, slot, 0:P], st["cell_iota"][:, 0:P], steps[:, 1, bass.ds(k, 1)], None, ALU.is_equal)
                    for i in range(3):
                        last = dve.tensor_scalar(rows[:, slot, (i + 1) * P:(i + 2) * P], st["cell_iota"][:, 0:P],
                                                 steps[:, 1, bass.ds(k, 1)], steps[:, 2 + i, bass.ds(k, 1)],
                                                 ALU.is_equal, ALU.mult)
                    last.then_inc(s_made, 1)

                for slot in range(RING):
                    make(slot, slot)
                with dve.Fori(1, STEPS // RING) as turn:
                    for slot in range(RING):
                        dve.wait_ge(s_used, (turn - 1) * RING + slot + 1)
                        make(turn * RING + slot, slot)
                for k in range(STEPS // RING * RING, STEPS):
                    dve.wait_ge(s_used, k - RING + 1)
                    make(k, k % RING)

            @block.tensor
            def _(pe):
                def window(w, half):
                    if not isinstance(w, int) or w >= 2:
                        pe.wait_ge(s_free, 2 * (w - 1))
                    for ps in (ps_c, ps_a):
                        pe.matmul(ps[half][:, CELLS:CELLS + 1], zero_b[:, :], zero_b[:, 0:1], start=True, stop=False, skip_group_check=True)
                    first = pe.value_load(st["ends_row"][0:1, bass.ds(w, 1)], min_val=0, max_val=STEPS)
                    after = pe.value_load(st["ends_row"][0:1, bass.ds(w + 1, 1)], min_val=1, max_val=STEPS)
                    with pe.Fori(first, after) as k:
                        pe.wait_ge(s_made, k + 1)
                        slot = k % RING
                        moving = cells[:, bass.ds(slot, 1), :].rearrange("p a c -> p (a c)")
                        for i in range(4):
                            ps = ps_c if i == 0 else ps_a
                            stat = rows[:, bass.ds(slot, 1), i * P:(i + 1) * P].rearrange("p a c -> p (a c)")
                            last = pe.matmul(ps[half][:, 0:CELLS], stat, moving, start=False, stop=False, skip_group_check=True)
                        last.then_inc(s_used, 1)
                    for ps in (ps_c, ps_a):
                        last = pe.matmul(ps[half][:, CELLS:CELLS + 1], zero_b[:, :], zero_b[:, 0:1], start=False, stop=True, skip_group_check=True)
                    last.then_inc(s_win, 1)

                def transposes(tile, parity, copied):
                    pe.wait_ge(s_free, (tile + 1) * PER * 2)
                    for b in range(TB):
                        n = tile * TB + b
                        if not isinstance(n, int) or n >= 2:
                            pe.wait_ge(s_trc, n - 1)
                        for q in range(min(4, NT - 4 * b)):
                            last = pe.transpose(ps_t[b % 2][:, q * P:(q + 1) * P], stage_a[:, parity, 4 * b + q, :], st["ident"][:, :])
                        last.then_inc(s_tr, 1)

                pe.wait_ge(s_zero, 1)

                def tile(t, parity, first=False):
                    for j in range(PER):
                        window(t * PER + j, j % 2)
                    transposes(t, parity, None)

                tile(0, 0)
                with pe.Fori(0, (NT - 1) // 2) as half:
                    tile(half * 2 + 1, 1)
                    tile(half * 2 + 2, 0)

            @block.scalar
            def _(act):
                def tile(t, parity, first=False):
                    for j in range(PER):
                        w = t * PER + j
                        act.wait_ge(s_win, w + 1)
                        if j == 0 and not first:
                            act.wait_ge(s_cout[parity], ((t - parity) // 2) * 16)
                        for ps, stage in ((ps_c, stage_c), (ps_a, stage_a)):
                            act.copy(stage[:, parity, :, j * WIN:(j + 1) * WIN],
                                     ps[j % 2][:, 0:CELLS].rearrange("p (d s) -> p s d", s=NT)).then_inc(s_free, 1)
                    if not first:
                        act.wait_ge(s_tout[parity], ((t - parity) // 2) * 16)
                    for b in range(TB):
                        act.wait_ge(s_tr, t * TB + b + 1)
                        n = min(4, NT - 4 * b) * P
                        act.copy(stage_t[:, parity, 4 * b * P:4 * b * P + n], ps_t[b % 2][:, 0:n]).then_inc(s_trc, 1)

                tile(0, 0, True)
                tile(1, 1, True)
                with act.Fori(1, (NT - 1) // 2) as half:
                    tile(half * 2, 0)
                    tile(half * 2 + 1, 1)
                tile(NT - 1, 0)

            @block.sync
            def _(sp):
                def tile(t, parity):
                    sp.wait_ge(s_free, (t + 1) * PER * 2)
                    sp.dma_start(st["C"][:, :, bass.ds(t * P, P)].rearrange("s p d -> p s d"), stage_c[:, parity, :, :]).then_inc(s_cout[parity], 16)
                    sp.wait_ge(s_trc, (t + 1) * TB)
                    sp.dma_start(st["AT"][bass.ds(t, 1), :, :].rearrange("a p s -> p (a s)"), stage_t[:, parity, :]).then_inc(s_tout[parity], 16)

                over_tiles(sp, tile)
                for i in range(2):
                    sp.wait_ge(s_cout[i], 16 * ((NT + 1 - i) // 2))
                    sp.wait_ge(s_tout[i], 16 * ((NT + 1 - i) // 2))


class Signal:

    def __init__(self, sem):
        self.sem, self.base = sem, 0

    def at(self, n):
        return n + self.base

    def passed(self, n):
        self.base += n


class Steps(Chain):

    def __init__(self, eng, kept):
        super().__init__(eng, kept.sem, kept.base)
        self.kept = kept

    def done(self):
        self.kept.base = self.n


def in_ring(eng, ring, body, first_turn=0):
    for slot in range(ring):
        body(slot, slot, 0)
    with eng.Fori(1, NT // ring) as turn:
        for slot in range(ring):
            body(turn * ring + slot, slot, turn)
    for t in range(NT // ring * ring, NT):
        body(t, t % ring, NT // ring)


def banks(st):
    return st["ps"][:, :, 0:CHUNK]


def chunk(buf, c, rows=P):
    return buf[0:rows, c * CHUNK:(c + 1) * CHUNK]


def tile(buf, t, width=P, rows=P):
    return buf[0:rows, t * width:(t + 1) * width]


def dyn_tile(buf, t, width=P, rows=P):
    return buf[0:rows, bass.ds(t * width, width)]


def empty_banks(nc, block, st, out, ready, count):
    sig = st["sig"]

    def half(h):
        return (out[:, h * NP // 2:(h + 1) * NP // 2].rearrange("p (c n) -> p c n", n=CHUNK),
                banks(st)[:, h * NC // 2:(h + 1) * NC // 2, :])

    def scalar(act):
        if count:
            act.wait_ge(ready.sem, ready.at(count))
        act.copy(*half(0)).then_inc(sig["out"].sem, 1)

    @block.vector
    def _(dve):
        if count:
            dve.wait_ge(ready.sem, ready.at(count))
        dve.tensor_copy(*half(1)).then_inc(sig["out"].sem, 1)

    return scalar


def spread(nc, st, matrix, xn, out):
    sig, ring, stat = st["sig"], st["ring"], st["stat"]
    loaded, used, picked = sig["loaded"], sig["used"], sig["picked"]
    with nc.Block() as block:
        @block.sync
        def _(sp):
            def load(t, slot, turn):
                if not isinstance(t, int) or t >= RING:
                    sp.wait_ge(used.sem, used.at(t - RING + 1))
                sp.dma_start(ring[:, slot, :], matrix[bass.ds(t, 1), :, :].rearrange("a p n -> p (a n)")).then_inc(loaded[slot].sem, 16)
            in_ring(sp, RING, load)

        @block.tensor
        def _(pe):
            def multiply(t, slot, turn):
                pe.wait_ge(loaded[slot].sem, loaded[slot].at((turn + 1) * 16))
                pe.wait_ge(picked.sem, picked.at(t + 1))
                for c in range(NC):
                    last = pe.matmul(banks(st)[:, c, :], stat[:, slot, :], ring[:, slot, c * CHUNK:(c + 1) * CHUNK],
                                     start=isinstance(t, int) and t == 0, stop=isinstance(t, int) and t == NT - 1)
                last.then_inc(used.sem, 1)
            in_ring(pe, RING, multiply)

        empty = empty_banks(nc, block, st, out, used, NT)

        @block.scalar
        def _(act):
            def pick(t, slot, turn):
                if not isinstance(t, int) or t >= RING:
                    act.wait_ge(used.sem, used.at(t - RING + 1))
                act.copy(stat[:, slot, :], dyn_tile(xn, t)).then_inc(picked.sem, 1)
            in_ring(act, RING, pick)
            empty(act)
    for slot in range(RING):
        loaded[slot].passed(16 * len(range(slot, NT, RING)))
    used.passed(NT)
    picked.passed(NT)
    sig["out"].passed(2)


def flip(nc, st, source, out):
    sig, ident = st["sig"], st["ident"]
    turned, copied = sig["turned"], sig["out"]
    nb = -(-NT // 4)
    with nc.Block() as block:
        @block.tensor
        def _(pe):
            for b in range(nb):
                for q in range(min(4, NT - 4 * b)):
                    last = pe.transpose(st["ps"][:, b, q * P:(q + 1) * P], tile(source, 4 * b + q), ident[:, :])
                last.then_inc(turned.sem, 1)

        def copy_bank(eng, copy, b):
            n = min(4, NT - 4 * b) * P
            eng.wait_ge(turned.sem, turned.at(b + 1))
            copy(out[:, 4 * b * P:4 * b * P + n], st["ps"][:, b, 0:n]).then_inc(copied.sem, 1)

        @block.scalar
        def _(act):
            for b in range(0, nb, 2):
                copy_bank(act, act.copy, b)

        @block.vector
        def _(dve):
            for b in range(1, nb, 2):
                copy_bank(dve, dve.tensor_copy, b)
    turned.passed(nb)
    copied.passed(nb)


def empty_alone(nc, st, out):
    with nc.Block() as block:
        empty = empty_banks(nc, block, st, out, None, 0)

        @block.scalar
        def _(act):
            empty(act)
    st["sig"]["out"].passed(2)


def linear(nc, st, terms, out, bias=None, func=None, rows=P):
    sig = st["sig"]
    multiplied, copied = sig["used"], sig["out"]
    with nc.Block() as block:
        @block.tensor
        def _(pe):
            for c in range(NC):
                for i, (weight, x, k) in enumerate(terms):
                    last = pe.matmul(banks(st)[0:rows, c, :], weight, chunk(x, c, k), start=i == 0, stop=i == len(terms) - 1)
                last.then_inc(multiplied.sem, 1)

        @block.scalar
        def _(act):
            for c in range(NC):
                act.wait_ge(multiplied.sem, multiplied.at(c + 1))
                if bias is None:
                    act.copy(chunk(out, c, rows), banks(st)[0:rows, c, :]).then_inc(copied.sem, 1)
                else:
                    act.activation(chunk(out, c, rows), banks(st)[0:rows, c, :], func or ACT.Identity, bias=bias).then_inc(copied.sem, 1)
    multiplied.passed(NC)
    copied.passed(NC)


def over_features(buf):
    return buf[:, :].rearrange("p (t f) -> p t f", f=FEAT)


def norm_rows(nc, st, x, gain=None, shift=None):
    sig, work = st["sig"], st["norm_work"]
    mean, var = st["norm_mean"], st["norm_var"]
    ready, rooted = sig["to_act"], sig["from_act"]
    x3, w3 = over_features(x), over_features(work)

    def wide(col):
        return col[:, :].unsqueeze(2).to_broadcast((P, NT, FEAT))

    with nc.Block() as block:
        @block.vector
        def _(dve):
            link = Steps(dve, sig["dve"])
            link(dve.tensor_reduce(mean[:, :], x3, AX.X, ALU.add))
            link(dve.tensor_scalar(mean[:, :], mean[:, :], 1.0 / FEAT, None, ALU.mult))
            link(dve.tensor_tensor(x3, x3, wide(mean), ALU.subtract))
            link(dve.tensor_tensor(w3, x3, x3, ALU.mult))
            link(dve.tensor_reduce(var[:, :], w3, AX.X, ALU.add))
            dve.tensor_scalar(var[:, :], var[:, :], 1.0 / FEAT, 1e-5, ALU.mult, ALU.add).then_inc(ready.sem, 1)
            dve.wait_ge(rooted.sem, rooted.at(1))
            link(dve.reciprocal(var[:, :], var[:, :]))
            link(dve.tensor_tensor(x3, x3, wide(var), ALU.mult))
            if gain is not None:
                link(dve.tensor_tensor(x3, x3, gain.unsqueeze(1).to_broadcast((P, NT, FEAT)), ALU.mult))
                link(dve.tensor_tensor(x3, x3, shift.unsqueeze(1).to_broadcast((P, NT, FEAT)), ALU.add))
            link.done()

        @block.scalar
        def _(act):
            act.wait_ge(ready.sem, ready.at(1))
            act.sqrt(var[:, :], var[:, :]).then_inc(rooted.sem, 1)
    ready.passed(1)
    rooted.passed(1)


def norm_nodes(nc, st, x, gain, shift):
    sig, work, cols = st["sig"], st["norm_work"], st["node_cols"]
    ready, rooted = sig["to_act"], sig["from_act"]
    real = x[:, 0:N_NODES]
    with nc.Block() as block:
        @block.vector
        def _(dve):
            link = Steps(dve, sig["dve"])
            link(dve.tensor_reduce(cols[:, 0:1], real, AX.X, ALU.add))
            link(dve.tensor_scalar(cols[:, 0:1], cols[:, 0:1], 1.0 / N_NODES, None, ALU.mult))
            dve.tensor_scalar(x[:, :], x[:, :], cols[:, 0:1], None, ALU.subtract).then_inc(ready.sem, 1)
            dve.wait_ge(rooted.sem, rooted.at(1))
            dve.tensor_scalar(cols[:, 2:3], cols[:, 1:2], 1.0 / N_NODES, 1e-5, ALU.mult, ALU.add).then_inc(ready.sem, 1)
            dve.wait_ge(rooted.sem, rooted.at(2))
            link(dve.reciprocal(cols[:, 4:5], cols[:, 3:4]))
            link(dve.tensor_scalar(x[:, :], x[:, :], cols[:, 4:5], gain, ALU.mult, ALU.mult))
            link(dve.tensor_scalar(x[:, :], x[:, :], shift, None, ALU.add))
            link.done()

        @block.scalar
        def _(act):
            act.wait_ge(ready.sem, ready.at(1))
            act.activation(work[:, 0:N_NODES], real, ACT.Square, accum_out=cols[:, 1:2]).then_inc(rooted.sem, 1)
            act.wait_ge(ready.sem, ready.at(2))
            act.sqrt(cols[:, 3:4], cols[:, 2:3]).then_inc(rooted.sem, 1)
    ready.passed(2)
    rooted.passed(2)


def on_vector(nc, st, program):
    with nc.Block() as block:
        @block.vector
        def _(dve):
            link = Steps(dve, st["sig"]["dve"])
            program(dve, link)
            link.done()


def light_hops(nc, io, st):
    sig, x, en, et, acc = st["sig"], st["x"], st["buf_a"], st["buf_b"], st["buf_c"]
    with nc.Block() as block:
        @block.sync
        def _(sp):
            sp.dma_start(over_features(x), io["x_pad"].rearrange("(t p) f -> p t f", p=P)).then_inc(sig["params"].sem, 16)
            sp.wait_ge(sig["params"].sem, sig["params"].at(16))
    sig["params"].passed(16)
    for hop in range(3):
        spread(nc, st, st["AT"], x if hop == 0 else en, et)
        if hop == 0:
            on_vector(nc, st, lambda dve, link: link(dve.tensor_copy(acc[:, :], et[:, :])))
        else:
            on_vector(nc, st, lambda dve, link: link(dve.tensor_tensor(acc[:, :], acc[:, :], et[:, :], ALU.add)))
        if hop < 2:
            flip(nc, st, et, en)
    flip(nc, st, acc, en)

    def combine(dve, link):
        link(dve.tensor_tensor(en[:, :], en[:, :], x[:, :], ALU.add))
        link(dve.scalar_tensor_tensor(x[:, :], en[:, :], 0.25, x[:, :], ALU.mult, ALU.add))
    on_vector(nc, st, combine)
    norm_rows(nc, st, x)


HEADS = 4
HD = 32


def attention(nc, io, st):
    sig, x, xt = st["sig"], st["x"], st["buf_a"]
    out = st["buf_b"]
    flip(nc, st, x, xt)
    with ExitStack() as ctx:
        def sb(name, shape, dt=FP32):
            return ctx.enter_context(nc.sbuf_tensor(name, shape, dt))
        w = sb("gat_w", [HD, FEAT])
        att = sb("gat_att", [2 * HEADS, HD])
        bias = sb("gat_b", [HD, 1])
        wt = sb("gat_wt", [P, HD])
        att_t = sb("gat_att_t", [HD, 2 * HEADS])
        att_wide = sb("gat_att_wide", [HD, HEADS, P])
        wh = sb("gat_wh", [P, NT * HD])
        a_src = sb("gat_a_src", [P, NT * HEADS])
        a_dst = sb("gat_a_dst", [P, HEADS, NP])
        best = sb("gat_best", [P, HEADS])
        now = sb("gat_best_now", [P, 2, HEADS])
        best_all = sb("gat_best_all", [P, 4])
        bias_up = sb("gat_bias_up", [P, NT * HEADS])
        bias_down = sb("gat_bias_down", [P, NT * HEADS])
        params, turned, copied, used, ready, back = (sig[k] for k in ("params", "turned", "out", "used", "to_act", "from_act"))
        with nc.Block() as block:
            @block.sync
            def _(sp):
                sp.dma_start(w[:, :], io["L1_gnn_W"]).then_inc(params.sem, 16)
                sp.dma_start(att[0:HEADS, :], io["L1_gnn_att_src"]).then_inc(params.sem, 16)
                sp.dma_start(att[HEADS:2 * HEADS, :], io["L1_gnn_att_dst"]).then_inc(params.sem, 16)
                sp.dma_start(bias[:, :], io["L1_gnn_b"].rearrange("(p a) -> p a", a=1)).then_inc(params.sem, 16)

            @block.tensor
            def _(pe):
                pe.wait_ge(params.sem, params.at(64))
                pe.transpose(st["ps"][0:P, 0, 0:HD], w[:, :], st["ident"][0:HD, 0:HD]).then_inc(turned.sem, 1)
                pe.transpose(st["ps"][0:HD, 1, 0:2 * HEADS], att[:, :], st["ident"][0:2 * HEADS, 0:2 * HEADS]).then_inc(turned.sem, 1)

            @block.vector
            def _(dve):
                link = Steps(dve, sig["dve"])
                dve.wait_ge(turned.sem, turned.at(2))
                link(dve.tensor_copy(wt[:, :], st["ps"][0:P, 0, 0:HD]))
                link(dve.tensor_copy(att_t[:, :], st["ps"][0:HD, 1, 0:2 * HEADS]))
                link(dve.tensor_copy(att_wide[:, :, :], att_t[:, HEADS:2 * HEADS].unsqueeze(2).to_broadcast((HD, HEADS, P))))
                link.done()
        params.passed(64)
        turned.passed(2)
        with nc.sbuf_tensor("gat_wh_t", [HD, NP], FP32) as wh_t:
            linear(nc, st, [(wt[:, :], xt, P)], wh_t, bias=bias[:, 0:1], rows=HD)
            with nc.Block() as block:
                @block.tensor
                def _(pe):
                    for t in range(NT):
                        pe.transpose(st["ps"][:, t // 16, t % 16 * HD:(t % 16 + 1) * HD], tile(wh_t, t, rows=HD), st["ident"][0:HD, 0:HD])
                        last = pe.matmul(st["ps"][:, 2, t * HEADS:(t + 1) * HEADS], tile(wh_t, t, rows=HD), att_t[:, 0:HEADS], start=True, stop=True)
                    last.then_inc(turned.sem, 1)
                    for n in range(HEADS * NC):
                        h, c = divmod(n, NC)
                        if n >= 4:
                            pe.wait_ge(copied.sem, copied.at(n - 3))
                        pe.matmul(st["ps"][:, 4 + n % 4, 0:CHUNK], att_wide[:, h, :], chunk(wh_t, c, HD), start=True, stop=True).then_inc(used.sem, 1)

                @block.scalar
                def _(act):
                    for n in range(HEADS * NC):
                        h, c = divmod(n, NC)
                        act.wait_ge(used.sem, used.at(n + 1))
                        act.copy(a_dst[:, h, c * CHUNK:(c + 1) * CHUNK], st["ps"][:, 4 + n % 4, 0:CHUNK]).then_inc(copied.sem, 1)

                @block.vector
                def _(dve):
                    link = Steps(dve, sig["dve"])
                    dve.wait_ge(turned.sem, turned.at(1))
                    link(dve.tensor_copy(wh[:, 0:16 * HD], st["ps"][:, 0, :]))
                    link(dve.tensor_copy(wh[:, 16 * HD:NT * HD], st["ps"][:, 1, 0:(NT - 16) * HD]))
                    link(dve.tensor_copy(a_src[:, :], st["ps"][:, 2, 0:NT * HEADS]))
                    link.done()
            turned.passed(1)
            used.passed(HEADS * NC)
            copied.passed(HEADS * NC)

        R = 2
        loaded, made, seen = sig["loaded"], sig["picked"], sig["used"]
        with nc.sbuf_tensor("gat_pen", [P, R, NP], FP32) as pen, nc.sbuf_tensor("gat_best_junk", [P, HEADS, NP], BF16) as junk, nc.sbuf_tensor("gat_carrier", [P, 1], FP32) as carrier:
            ring = st["ring"]
            with nc.Block() as block:
                @block.sync
                def _(sp):
                    def load(t, slot, turn):
                        if not isinstance(t, int) or t >= R:
                            sp.wait_ge(made.sem, made.at(t - R + 1))
                        sp.dma_start(ring[:, slot, :], st["C"][bass.ds(t, 1), :, :].rearrange("a p n -> p (a n)")).then_inc(loaded[slot].sem, 16)
                    in_ring(sp, R, load)

                @block.scalar
                def _(act):
                    def penalise(t, slot, turn):
                        act.wait_ge(loaded[slot].sem, loaded[slot].at((turn + 1) * 16))
                        if not isinstance(t, int) or t >= R:
                            act.wait_ge(seen.sem, seen.at((t - R + 1) * HEADS))
                        act.activation(pen[:, slot, :], ring[:, slot, :], ACT.Relu, bias=st["big_col"][:, 0:1], scale=-BIG).then_inc(made.sem, 1)
                    in_ring(act, R, penalise)

                @block.vector
                def _(dve):
                    def largest(t, slot, turn):
                        dve.wait_ge(made.sem, made.at(t + 1))
                        if not isinstance(t, int) or t >= 1:
                            dve.wait_ge(sig["dve"].sem, sig["dve"].at(3 * t))
                        dve.memset(carrier[:, :], 0.0).then_inc(sig["dve"].sem, 1)
                        for h in range(HEADS):
                            dve.tensor_tensor_reduce(out=junk[:, h, :], in0=a_dst[:, h, :], in1=pen[:, slot, :], scale=1.0, scalar=-3e38,
                                                            op0=ALU.subtract, op1=ALU.max, accum_out=now[:, slot, h:h + 1]).then_inc(seen.sem, 1)
                        dve.wait_ge(seen.sem, seen.at(t * HEADS + HEADS))
                        dve.tensor_tensor(now[:, slot, :], now[:, slot, :], dyn_tile(a_src, t, HEADS), ALU.add).then_inc(sig["dve"].sem, 1)
                        dve.wait_ge(sig["dve"].sem, sig["dve"].at(3 * t + 2))
                        dve.tensor_tensor(best[:, :], now[:, slot, :], now[:, slot, :] if isinstance(t, int) and t == 0 else best[:, :],
                                          ALU.max).then_inc(sig["dve"].sem, 1)
                    in_ring(dve, R, largest)
            for slot in range(R):
                loaded[slot].passed(16 * len(range(slot, NT, R)))
            made.passed(NT)
            seen.passed(NT * HEADS)
            sig["dve"].passed(3 * NT)

        pooled = sig["pooled"]
        with nc.Block() as block:
            @block.vector
            def _(dve):
                link = Steps(dve, sig["dve"])
                dve.tensor_reduce(best_all[:, 0:1], best[:, :], AX.X, ALU.max).then_inc(ready.sem, 1)
                dve.wait_ge(pooled.sem, pooled.at(1))
                link(dve.tensor_scalar(best_all[:, 2:3], best_all[:, 1:2], 0.2, None, ALU.mult))
                link(dve.tensor_tensor(best_all[:, 3:4], best_all[:, 1:2], best_all[:, 2:3], ALU.max))
                link(dve.tensor_scalar(bias_up[:, :], a_src[:, :], best_all[:, 3:4], None, ALU.subtract))
                link(dve.tensor_scalar(bias_down[:, :], a_src[:, :], 0.2, best_all[:, 3:4], ALU.mult, ALU.subtract))
                link.done()

            @block.gpsimd
            def _(pool):
                pool.wait_ge(ready.sem, ready.at(1))
                pool.partition_all_reduce(best_all[:, 1:2], best_all[:, 0:1], P, bass.bass_isa.ReduceOp.max).then_inc(pooled.sem, 1)
        ready.passed(1)
        pooled.passed(1)

        R = 3
        down = (xt, st["norm_work"])
        with (nc.sbuf_tensor("gat_exp", [P, 2, NP], FP32) as expd,
              nc.sbuf_tensor("gat_share", [P, 2, NP], FP32) as share, nc.sbuf_tensor("gat_den", [P, 2, 2], FP32) as den,
              nc.sbuf_tensor("gat_message", [P, 2, HD], FP32) as message):
            ring = st["ring"]
            exped, shared, scaled, spent = sig["from_act"], sig["shared"], sig["scaled"], sig["used"]
            with nc.Block() as block:
                @block.sync
                def _(sp):
                    def load(t, slot, turn):
                        if not isinstance(t, int) or t >= R:
                            sp.wait_ge(shared.sem, shared.at((t - R + 1) * HEADS))
                        sp.dma_start(ring[:, slot, :], st["C"][bass.ds(t, 1), :, :].rearrange("a p n -> p (a n)")).then_inc(loaded[slot].sem, 16)
                    in_ring(sp, R, load)

                @block.scalar
                def _(act):
                    def exps(t, slot, turn):
                        for h in range(HEADS):
                            n = t * HEADS + h
                            if not isinstance(n, int) or n >= 2:
                                act.wait_ge(shared.sem, shared.at(n - 1))
                            act.activation(expd[:, h % 2, :], a_dst[:, h, :], ACT.Exp, bias=bias_up[:, bass.ds(n, 1)])
                            act.activation(down[h % 2][:, :], a_dst[:, h, :], ACT.Exp, bias=bias_down[:, bass.ds(n, 1)], scale=0.2).then_inc(exped.sem, 1)
                    in_ring(act, R, exps)

                @block.vector
                def _(dve):
                    def shares(t, slot, turn):
                        dve.wait_ge(loaded[slot].sem, loaded[slot].at((turn + 1) * 16))
                        for h in range(HEADS):
                            n = t * HEADS + h
                            par = h % 2
                            dve.wait_ge(exped.sem, exped.at(n + 1))
                            if not isinstance(n, int) or n >= 2:
                                dve.wait_ge(spent.sem, spent.at(n - 1))
                            dve.tensor_tensor(expd[:, par, :], expd[:, par, :], down[par][:, :], ALU.max).then_inc(sig["dve"].sem, 1)
                            dve.wait_ge(sig["dve"].sem, sig["dve"].at(3 * n + 1))
                            dve.scalar_tensor_tensor(share[:, par, :], expd[:, par, :], 1.0, ring[:, slot, :], ALU.min, ALU.mult,
                                                     accum_out=den[:, par, 0:1]).then_inc(shared.sem, 1)
                            dve.wait_ge(shared.sem, shared.at(n + 1))
                            dve.tensor_scalar(den[:, par, 0:1], den[:, par, 0:1], 1e-16, None, ALU.add).then_inc(sig["dve"].sem, 1)
                            dve.wait_ge(sig["dve"].sem, sig["dve"].at(3 * n + 2))
                            dve.reciprocal(den[:, par, 1:2], den[:, par, 0:1]).then_inc(sig["dve"].sem, 1)
                            dve.wait_ge(sig["dve"].sem, sig["dve"].at(3 * n + 3))
                            dve.tensor_scalar(message[:, par, :], dyn_tile(wh, t, HD), den[:, par, 1:2], None, ALU.mult).then_inc(scaled.sem, 1)
                    in_ring(dve, R, shares)

                @block.tensor
                def _(pe):
                    def sums(t, slot, turn):
                        for h in range(HEADS):
                            n = t * HEADS + h
                            pe.wait_ge(scaled.sem, scaled.at(n + 1))
                            for c in range(NC):
                                last = pe.matmul(banks(st)[h * HD:(h + 1) * HD, c, :], message[:, h % 2, :], share[:, h % 2, c * CHUNK:(c + 1) * CHUNK],
                                                 start=isinstance(t, int) and t == 0, stop=isinstance(t, int) and t == NT - 1)
                            last.then_inc(spent.sem, 1)
                    in_ring(pe, R, sums)

            for slot in range(R):
                loaded[slot].passed(16 * len(range(slot, NT, R)))
            for s, n in ((exped, NT * HEADS), (shared, NT * HEADS), (scaled, NT * HEADS), (spent, NT * HEADS), (sig["dve"], 3 * NT * HEADS)):
                s.passed(n)
    empty_alone(nc, st, out)
    flip(nc, st, out, xt)
    on_vector(nc, st, lambda dve, link: link(dve.tensor_tensor(x[:, :], x[:, :], xt[:, :], ALU.add)))
    norm_rows(nc, st, x)


def isomorphism(nc, io, st):
    sig, x = st["sig"], st["x"]
    agg, ht = st["buf_a"], st["buf_b"]
    with nc.sbuf_tensor("gin_w", [P, 2, P], FP32) as w, nc.sbuf_tensor("gin_vecs", [P, 4], FP32) as vecs:
        params = sig["params"]
        with nc.Block() as block:
            @block.sync
            def _(sp):
                sp.dma_start(w[:, 0, :], io["L2_gnn_W1"]).then_inc(params.sem, 16)
                sp.dma_start(w[:, 1, :], io["L2_gnn_W2"]).then_inc(params.sem, 16)
                for i, name in enumerate(("L2_gnn_b1", "L2_gnn_gamma", "L2_gnn_beta", "L2_gnn_b2")):
                    sp.dma_start(vecs[:, i:i + 1], io[name].rearrange("(p a) -> p a", a=1)).then_inc(params.sem, 16)
                sp.wait_ge(params.sem, params.at(96))
        params.passed(96)
        spread(nc, st, st["C"], x, agg)
        flip(nc, st, x, ht)
        on_vector(nc, st, lambda dve, link: link(dve.tensor_tensor(agg[:, :], agg[:, :], ht[:, :], ALU.add)))
        linear(nc, st, [(w[:, 0, :], agg, P)], ht, bias=vecs[:, 0:1])
        norm_nodes(nc, st, ht, vecs[:, 1:2], vecs[:, 2:3])
        on_vector(nc, st, lambda dve, link: link(dve.tensor_scalar(ht[:, :], ht[:, :], 0.0, None, ALU.max)))
        linear(nc, st, [(w[:, 1, :], ht, P)], agg, bias=vecs[:, 3:4], func=ACT.Relu)
        flip(nc, st, agg, ht)
        on_vector(nc, st, lambda dve, link: link(dve.tensor_tensor(x[:, :], x[:, :], ht[:, :], ALU.add)))
        norm_rows(nc, st, x)


LAYERS = 3
UB = 13
WB = 2 + UB + 1


def degrees(nc, st):
    sig = st["sig"]
    recip, amp, att = st["recip_deg"], st["amplify"], st["attenuate"]
    ends = st["node_ends"]
    with nc.sbuf_tensor("ends_now", [P, NP], FP32) as now, nc.sbuf_tensor("ends_before", [P, NP], FP32) as before, \
            nc.sbuf_tensor("ends_cols", [P, 2, NT], FP32) as cols:
        params, ready, back = sig["params"], sig["to_act"], sig["from_act"]
        with nc.Block() as block:
            @block.sync
            def _(sp):
                for row, lo in ((now, P), (before, P - 1)):
                    sp.dma_start(row[:, :], ends[lo:lo + NP].rearrange("(a n) -> a n", a=1).to_broadcast((P, NP))).then_inc(params.sem, 16)
                with nc.allow_non_contiguous_dma(reason="3200 words"):
                    for i, lo in enumerate((P, P - 1)):
                        sp.dma_start(cols[:, i, :], ends[lo:lo + NP].rearrange("(t p) -> p t", p=P)).then_inc(params.sem, 16)

            @block.vector
            def _(dve):
                link = Steps(dve, sig["dve"])
                dve.wait_ge(params.sem, params.at(64))
                link(dve.tensor_tensor(now[:, :], now[:, :], before[:, :], ALU.subtract))
                dve.tensor_scalar(now[:, :], now[:, :], 1.0, None, ALU.add).then_inc(ready.sem, 1)
                dve.wait_ge(ready.sem, ready.at(1))
                link(dve.reciprocal(recip[:, :], now[:, :]))
                dve.wait_ge(back.sem, back.at(1))
                link(dve.tensor_scalar(amp[:, :], amp[:, :], 0.25, None, ALU.mult))
                link(dve.reciprocal(att[:, :], amp[:, :]))
                link(dve.tensor_tensor(cols[:, 0, :], cols[:, 0, :], cols[:, 1, :], ALU.is_equal))
                link(dve.tensor_scalar(st["no_edge"][:, :], cols[:, 0, :], -BIG, None, ALU.mult))
                link.done()

            @block.scalar
            def _(act):
                act.wait_ge(ready.sem, ready.at(1))
                act.activation(amp[:, :], now[:, :], ACT.Ln, bias=1.0).then_inc(back.sem, 1)
        params.passed(64)
        ready.passed(1)
        back.passed(1)


def load_layer(nc, io, st, layer, wt, vecs, rows):
    sig = st["sig"]
    params, turned, copied = sig["params"], sig["turned"], sig["out"]
    with nc.sbuf_tensor(f"raw_w{layer}", [P, WB * P], FP32) as raw:
        with nc.Block() as block:
            @block.sync
            def _(sp):
                sp.dma_start(raw[:, 0:2 * P], io["L3_gnn_Mw"][layer, :, :]).then_inc(params.sem, 16)
                sp.dma_start(raw[:, 2 * P:(2 + UB) * P], io["L3_gnn_Uw"][layer, :, :]).then_inc(params.sem, 16)
                sp.dma_start(raw[:, (2 + UB) * P:WB * P], io["L3_gnn_mix_w"][layer, :, :]).then_inc(params.sem, 16)
                for i, name in enumerate(("Mb", "Ub", "bn_g", "bn_b", "mix_b")):
                    sp.dma_start(vecs[:, i:i + 1], io["L3_gnn_" + name][layer, :].rearrange("(p a) -> p a", a=1)).then_inc(params.sem, 16)
                for i, name in enumerate(("ln_g", "ln_b")):
                    sp.dma_start(rows[:, i, :], io["L3_gnn_" + name][layer:layer + 1, :].to_broadcast((P, P))).then_inc(params.sem, 16)
                sp.wait_ge(params.sem, params.at(160))

            @block.tensor
            def _(pe):
                pe.wait_ge(params.sem, params.at(160))
                for b in range(WB // 4):
                    for q in range(4):
                        last = pe.transpose(st["ps"][:, b, q * P:(q + 1) * P], raw[:, (4 * b + q) * P:(4 * b + q + 1) * P], st["ident"][:, :])
                    last.then_inc(turned.sem, 1)

            @block.scalar
            def _(act):
                for b in range(WB // 4):
                    act.wait_ge(turned.sem, turned.at(b + 1))
                    act.copy(wt[:, 4 * b * P:4 * (b + 1) * P], st["ps"][:, b, :]).then_inc(copied.sem, 1)
        params.passed(160)
        turned.passed(WB // 4)
        copied.passed(WB // 4)


TILES_IN = EI // P
GSTEPS = EP // EI
GU = 4
PEN_STEPS = 4


def running_extremes(nc, st, layer):
    sig = st["sig"]
    with ExitStack() as ctx:
        def sb(name, shape, dt=FP32):
            return ctx.enter_context(nc.sbuf_tensor(f"{name}{layer}", shape, dt))

        def sem(name):
            return ctx.enter_context(nc.semaphore(f"g{layer}_{name}"))
        idx = sb("gather_idx", [P, GU, TILES_IN], INT32)
        got = sb("gathered", [P, GU, TILES_IN, FEAT])
        spare = sb("spare", [P, 1])
        zeros = sb("spare_zeros", [P, 1])
        pen = sb("pen_rows", [P, 2, 2, EI * PEN_STEPS // 2], BF16)
        run = sb("running", [P, 2, 2, EI])
        rows = sb("run_rows", [P, 2, TILES_IN, 2, FEAT])
        ps = st["ps"]
        s_idx, s_scan, s_turn, s_back, s_rows, s_zero = (sem(n) for n in ("idx", "scanned", "turned", "turned_back", "rows", "zeroed"))
        s_got = [sem(f"gathered{i}") for i in range(GU)]
        s_pen = [sem(f"pen{i}") for i in range(2)]
        s_out = [sem(f"stored{i}") for i in range(2)]

        def turns(eng, body):
            for u in range(GU):
                body(u, u, 0)
            with eng.Fori(1, GSTEPS // GU) as turn:
                for u in range(GU):
                    body(turn * GU + u, u, turn)

        with nc.Block() as block:
            @block.gpsimd
            def _(pool):
                pool.memset(zeros[:, :], 0.0).then_inc(s_zero, 1)
                pool.wait_ge(s_zero, 1)

                def gather(step, u, turn):
                    if not (isinstance(step, int) and step < GU):
                        pool.wait_ge(s_turn, step - GU + 1)
                    pool.wait_ge(st["sig"]["src_in"].sem, 16)
                    pool.tensor_copy(idx[:, u, :], st["src_cols"][:, bass.ds(step * TILES_IN, TILES_IN)]).then_inc(s_idx, 1)
                    pool.wait_ge(s_idx, 2 * step + 1)
                    pool.tensor_tensor(spare[:, :], zeros[:, :], zeros[:, :], ALU.add).then_inc(s_idx, 1)
                    for q in range(TILES_IN):
                        pool.indirect_dma_start(out=got[:, u, q, :], out_offset=None, in_=st["P"],
                                                in_offset=bass.IndirectOffsetOnAxis(ap=idx[:, u, q:q + 1], axis=0)).then_inc(s_got[u], 16)
                turns(pool, gather)

            @block.tensor
            def _(pe):
                def turn_in(step, u, turn):
                    pe.wait_ge(s_got[u], (turn + 1) * 16 * TILES_IN)
                    if not (isinstance(step, int) and step < 2):
                        pe.wait_ge(s_scan, step - 1)
                    for q in range(TILES_IN):
                        last = pe.transpose(ps[:, u % 2, q * P:(q + 1) * P], got[:, u, q, :], st["ident"][:, :])
                    last.then_inc(s_turn, 1)

                def turn_back(step, u, turn):
                    pe.wait_ge(s_scan, step + 1)
                    if not (isinstance(step, int) and step < 2):
                        pe.wait_ge(s_rows, 2 * (step - 1))
                    for i in range(2):
                        for q in range(TILES_IN):
                            last = pe.transpose(ps[:, 2 + 2 * (u % 2) + i, q * P:(q + 1) * P], run[:, u % 2, i, q * P:(q + 1) * P], st["ident"][:, :])
                    last.then_inc(s_back, 1)

                turn_in(0, 0, 0)
                for u in range(1, GU):
                    turn_in(u, u, 0)
                    turn_back(u - 1, u - 1, 0)
                with pe.Fori(1, GSTEPS // GU) as turn:
                    for u in range(GU):
                        turn_in(turn * GU + u, u, turn)
                        turn_back(turn * GU + u - 1, (u - 1) % GU, turn)
                turn_back(GSTEPS - 1, GU - 1, 0)

            @block.vector
            def _(dve):
                def scan(step, u, turn):
                    half = u // 2
                    if u % 2 == 0:
                        dve.wait_ge(s_pen[half], (turn + 1) * 16)
                    dve.wait_ge(s_turn, step + 1)
                    if not (isinstance(step, int) and step < 2):
                        dve.wait_ge(s_back, step - 1)
                    for i, op in ((0, ALU.max), (1, ALU.min)):
                        if isinstance(step, int) and step == 0:
                            start = 0.0
                        else:
                            dve.wait_ge(s_scan, step)
                            start = run[:, (u + 1) % 2, i, EI - 1:EI]
                        last = dve.tensor_tensor_scan(run[:, u % 2, i, :], pen[:, half, i, u % 2 * EI:(u % 2 + 1) * EI],
                                                      ps[:, u % 2, :], start, ALU.add, op)
                    last.then_inc(s_scan, 1)
                turns(dve, scan)

            @block.scalar
            def _(act):
                def rows_out(step, u, turn):
                    act.wait_ge(s_back, step + 1)
                    if not (isinstance(step, int) and step < 2):
                        act.wait_ge(s_out[u % 2], (turn * (GU // 2) + u // 2) * 16)
                    for i in range(2):
                        act.copy(rows[:, u % 2, :, i, :], ps[:, 2 + 2 * (u % 2) + i, :].rearrange("p (q f) -> p q f", f=FEAT)).then_inc(s_rows, 1)
                turns(act, rows_out)

            @block.sync
            def _(sp):
                def load_pens(half, turn):
                    if not isinstance(turn, int) or turn >= 1:
                        sp.wait_ge(s_scan, (turn - 1) * GU + 2 * half + 2)
                    sp.dma_start(pen[:, half, :, :], st["pens"][:, bass.ds((turn * GU + 2 * half) * EI, 2 * EI)].unsqueeze(0).to_broadcast((P, 2, 2 * EI))).then_inc(s_pen[half], 16)

                def store(step, u, turn):
                    sp.wait_ge(s_rows, 2 * (step + 1))
                    sp.dma_start(st["extremes"][bass.ds(step * EI, EI), :].rearrange("(q p) w -> p q w", p=P),
                                 rows[:, u % 2, :, :, :].rearrange("p q i f -> p q (i f)")).then_inc(s_out[u % 2], 16)
                for half in range(2):
                    load_pens(half, 0)
                TURNS = GSTEPS // GU
                with sp.Fori(0, TURNS - 1) as turn:
                    store(turn * GU, 0, turn)
                    store(turn * GU + 1, 1, turn)
                    load_pens(0, turn + 1)
                    store(turn * GU + 2, 2, turn)
                    store(turn * GU + 3, 3, turn)
                    load_pens(1, turn + 1)
                for u in range(GU):
                    store((TURNS - 1) * GU + u, u, TURNS - 1)
                for i in range(2):
                    sp.wait_ge(s_out[i], 16 * GSTEPS // 2)


def extremes_of_nodes(nc, st, layer, mx, mn):
    sig = st["sig"]
    HB = 5
    with nc.sbuf_tensor(f"end_rows{layer}", [P, NT, 2, FEAT], FP32) as rows, nc.semaphore(f"e{layer}_rows") as s_rows:
        turned, copied, fixed = sig["turned"], sig["out"], sig["shared"]
        with nc.Block() as block:
            @block.gpsimd
            def _(pool):
                for t in range(NT):
                    pool.indirect_dma_start(out=rows[:, t, :, :].rearrange("p i f -> p (i f)"), out_offset=None, in_=st["extremes"],
                                            in_offset=bass.IndirectOffsetOnAxis(ap=st["last_edge"][:, t:t + 1], axis=0)).then_inc(s_rows, 16)

            @block.vector
            def _(dve):
                dve.wait_ge(s_rows, 16 * NT)
                for i, op in enumerate((ALU.add, ALU.subtract)):
                    dve.tensor_tensor(rows[:, :, i, :], rows[:, :, i, :], st["no_edge"][:, :].unsqueeze(2).to_broadcast((P, NT, FEAT)), op).then_inc(fixed.sem, 1)

            @block.tensor
            def _(pe):
                n = 0
                for i in range(2):
                    pe.wait_ge(fixed.sem, fixed.at(i + 1))
                    for b in range(-(-NT // 4)):
                        if n >= 8:
                            pe.wait_ge(copied.sem, copied.at(n - 7))
                        for q in range(min(4, NT - 4 * b)):
                            last = pe.transpose(st["ps"][:, n % 8, q * P:(q + 1) * P], rows[:, 4 * b + q, i, :], st["ident"][:, :])
                        last.then_inc(turned.sem, 1)
                        n += 1

            @block.scalar
            def _(act):
                n = 0
                for out in (mx, mn):
                    for b in range(-(-NT // 4)):
                        w = min(4, NT - 4 * b) * P
                        act.wait_ge(turned.sem, turned.at(n + 1))
                        act.copy(out[:, 4 * b * P:4 * b * P + w], st["ps"][:, n % 8, 0:w]).then_inc(copied.sem, 1)
                        n += 1
        turned.passed(2 * -(-NT // 4))
        copied.passed(2 * -(-NT // 4))
        fixed.passed(2)


def principal_layer(nc, io, st, layer, h, ht):
    sig = st["sig"]
    with ExitStack() as ctx:
        def sb(name, shape, dt=FP32):
            return ctx.enter_context(nc.sbuf_tensor(f"{name}{layer}", shape, dt))
        wt = sb("layer_w", [P, WB * P])
        vecs = sb("layer_vecs", [P, 5])
        lnrow = sb("layer_rows", [P, 2, P])
        load_layer(nc, io, st, layer, wt, vecs, lnrow)

        def w(i):
            return wt[:, i * P:(i + 1) * P]
        pt = sb("p_t", [P, NP])
        std = sb("std_t", [P, NP])
        var = sb("var_t", [P, NP])
        with nc.sbuf_tensor(f"p_n{layer}", [P, NP], FP32) as pn:
            linear(nc, st, [(w(0), ht, P)], pt)
            flip(nc, st, pt, pn)
            with nc.Block() as block:
                @block.sync
                def _(sp):
                    sp.dma_start(st["P"].rearrange("(t p) f -> p t f", p=P), over_features(pn)).then_inc(sig["params"].sem, 16)
                    sp.wait_ge(sig["params"].sem, sig["params"].at(16))
            sig["params"].passed(16)
            with nc.sbuf_tensor(f"ring{layer}", [P, RING, NP], FP32) as ring:
                st["ring"] = ring
                spread(nc, st, st["C"], pn, std)
                on_vector(nc, st, lambda dve, link: link(dve.tensor_tensor(pn[:, :], pn[:, :], pn[:, :], ALU.mult)))
                spread(nc, st, st["C"], pn, var)
        mx = sb("max_t", [P, NP])
        running_extremes(nc, st, layer)
        mn = sb("min_t", [P, NP])
        extremes_of_nodes(nc, st, layer, mx, mn)
        ready, back = sig["to_act"], sig["from_act"]
        qt = st["norm_work"]
        linear(nc, st, [(w(1), ht, P)], qt, bias=vecs[:, 0:1])
        with nc.sbuf_tensor(f"square{layer}", [P, NP], FP32) as sq:
            with nc.Block() as block:
                @block.vector
                def _(dve):
                    link = Steps(dve, sig["dve"])
                    recip = st["recip_deg"]
                    link(dve.tensor_tensor(std[:, :], std[:, :], pt[:, :], ALU.add))
                    link(dve.tensor_tensor(std[:, :], std[:, :], recip[:, :], ALU.mult))
                    link(dve.tensor_tensor(std[:, :], std[:, :], std[:, :], ALU.mult))
                    link(dve.tensor_tensor(sq[:, :], pt[:, :], pt[:, :], ALU.mult))
                    link(dve.tensor_tensor(var[:, :], var[:, :], sq[:, :], ALU.add))
                    link(dve.tensor_tensor(var[:, :], var[:, :], recip[:, :], ALU.mult))
                    link(dve.tensor_tensor(var[:, :], var[:, :], std[:, :], ALU.subtract))
                    link(dve.tensor_scalar(var[:, :], var[:, :], 0.0, None, ALU.max))
                    dve.tensor_scalar(sq[:, :], var[:, :], 1e-30, None, ALU.add).then_inc(ready.sem, 1)
                    link(dve.tensor_tensor(mx[:, :], mx[:, :], pt[:, :], ALU.max))
                    link(dve.tensor_tensor(mx[:, :], mx[:, :], qt[:, :], ALU.add))
                    link(dve.tensor_tensor(mn[:, :], mn[:, :], pt[:, :], ALU.min))
                    link(dve.tensor_tensor(mn[:, :], mn[:, :], qt[:, :], ALU.add))
                    link.done()

                @block.scalar
                def _(act):
                    act.wait_ge(ready.sem, ready.at(1))
                    act.wait_ge(sig["dve"].sem, sig["dve"].base)
                    act.sqrt(std[:, :], sq[:, :]).then_inc(back.sem, 1)
            ready.passed(1)
            back.passed(1)
            aggs = (mx, mn, std, var)
            u, scaled = sq, pt
            linear(nc, st, [(w(2), ht, P)] + [(w(3 + i), a, P) for i, a in enumerate(aggs)], u, bias=vecs[:, 1:2])
            for s, scaler in enumerate((st["amplify"], st["attenuate"])):
                linear(nc, st, [(w(7 + 4 * s + i), a, P) for i, a in enumerate(aggs)], scaled)

                def add_scaled(dve, link):
                    link(dve.tensor_tensor(scaled[:, :], scaled[:, :], scaler[:, :], ALU.mult))
                    link(dve.tensor_tensor(u[:, :], u[:, :], scaled[:, :], ALU.add))
                on_vector(nc, st, add_scaled)
            on_vector(nc, st, lambda dve, link: link(dve.tensor_scalar(u[:, :], u[:, :], (1.0 / N_NODES) ** 0.5, None, ALU.mult)))
            norm_nodes(nc, st, u, vecs[:, 2:3], vecs[:, 3:4])
            mixed = scaled
            linear(nc, st, [(w(WB - 1), u, P)], mixed, bias=vecs[:, 4:5])

            def residual(dve, link):
                link(dve.scalar_tensor_tensor(mixed[:, :], mixed[:, :], 0.01, mixed[:, :], ALU.mult, ALU.max))
                link(dve.tensor_tensor(ht[:, :], ht[:, :], mixed[:, :], ALU.add))
            on_vector(nc, st, residual)
            flip(nc, st, ht, h)
            norm_rows(nc, st, h, lnrow[:, 0, :], lnrow[:, 1, :])
            with nc.Block() as block:
                @block.vector
                def _(dve):
                    link = Steps(dve, sig["dve"])
                    dve.tensor_scalar(u[:, :], h[:, :], 0.0, None, ALU.min).then_inc(ready.sem, 1)
                    dve.wait_ge(back.sem, back.at(1))
                    link(dve.tensor_scalar(u[:, :], u[:, :], -1.0, None, ALU.add))
                    link(dve.scalar_tensor_tensor(h[:, :], h[:, :], 0.0, u[:, :], ALU.max, ALU.add))
                    link.done()

                @block.scalar
                def _(act):
                    act.wait_ge(ready.sem, ready.at(1))
                    act.activation(u[:, :], u[:, :], ACT.Exp).then_inc(back.sem, 1)
            ready.passed(1)
            back.passed(1)
            if layer < LAYERS - 1:
                flip(nc, st, h, ht)


RING = 3


def program(nc, io, out, kind="Internal"):
    st = {}

    def dram(name, shape, dt=FP32):
        st[name] = nc.dram_tensor(name, shape, dt, kind=kind).ap()
    dram("win_ends", [2 * P], INT32)
    dram("node_ends", [P + NP])
    dram("pens", [2, EP], BF16)
    dram("C", [NT, P, NP])
    dram("AT", [NT, P, NP])
    dram("P", [NP, FEAT])
    dram("extremes", [EP, 2 * FEAT])
    with ExitStack() as ctx:
        def sb(name, shape, dt=FP32):
            st[name] = ctx.enter_context(nc.sbuf_tensor(name, shape, dt))
        sb("ident", [P, P])
        sb("cell_iota", [P, CELLS], FP16)
        sb("last_edge", [P, NT], INT32)
        sb("ends_row", [1, NWIN + 1], INT32)
        sb("big_col", [P, 1])
        with nc.sbuf_tensor("steps", [P, 5, SG * P], FP32) as steps:
            st["steps"] = steps
            windows_and_steps(nc, io, st)
            build_adjacency(nc, st)
        for name, shape in (("x", [P, NP]), ("norm_work", [P, NP]), ("norm_mean", [P, NT]), ("norm_var", [P, NT]), ("node_cols", [P, 5])):
            sb(name, shape)
        sb("stat", [P, RING, P])
        st["ps"] = ctx.enter_context(nc.psum_tensor("ps", [P, 8, 512], FP32))
        sig = st["sig"] = {k: Signal(ctx.enter_context(nc.semaphore("sig_" + k))) for k in
                           ("used", "picked", "out", "turned", "to_act", "from_act", "params", "dve", "act", "pooled", "shared", "scaled", "src_in")}
        sig["loaded"] = [Signal(ctx.enter_context(nc.semaphore(f"sig_loaded{i}"))) for i in range(RING)]
        on_vector(nc, st, lambda dve, link: link(dve.memset(st["big_col"][:, :], BIG)))
        with nc.sbuf_tensor("buf_a", [P, NP], FP32) as a, nc.sbuf_tensor("buf_b", [P, NP], FP32) as b, nc.sbuf_tensor("ring", [P, RING, NP], FP32) as ring:
            st["buf_a"], st["buf_b"], st["ring"] = a, b, ring
            with nc.sbuf_tensor("buf_c", [P, NP], FP32) as c:
                st["buf_c"] = c
                light_hops(nc, io, st)
            attention(nc, io, st)
            isomorphism(nc, io, st)
        for name, shape in (("recip_deg", [P, NP]), ("amplify", [P, NP]), ("attenuate", [P, NP]), ("no_edge", [P, NT]), ("h", [P, NP]), ("h_t", [P, NP])):
            sb(name, shape)
        st["src_cols"] = ctx.enter_context(nc.sbuf_tensor("src_cols", [P, ET], INT32))
        degrees(nc, st)
        h, ht, x = st["h"], st["h_t"], st["x"]
        with nc.Block() as block:
            @block.sync
            def _(sp):
                with nc.allow_non_contiguous_dma(reason="each edge tile's indices become a column"):
                    sp.dma_start(st["src_cols"][:, :], io["src_cols"]).then_inc(sig["src_in"].sem, 16)
                sp.wait_ge(sig["src_in"].sem, 16)
        flip(nc, st, x, ht)
        for layer in range(LAYERS):
            principal_layer(nc, io, st, layer, h, ht)
        on_vector(nc, st, lambda dve, link: link(dve.tensor_tensor(x[:, :], x[:, :], h[:, :], ALU.add)))
        norm_rows(nc, st, x)
        with nc.Block() as block:
            @block.sync
            def _(sp):
                full = N_NODES // P
                sp.dma_start(out[0:full * P, :].rearrange("(t p) f -> p t f", p=P), over_features(x)[:, 0:full, :]).then_inc(sig["params"].sem, 16)
                sp.dma_start(out[full * P:N_NODES, :], x[0:N_NODES - full * P, full * P:NP]).then_inc(sig["params"].sem, 16)
                sp.wait_ge(sig["params"].sem, sig["params"].at(32))


_PARAMS = ["L1_gnn_W", "L1_gnn_b", "L1_gnn_att_src", "L1_gnn_att_dst", "L2_gnn_W1", "L2_gnn_b1", "L2_gnn_gamma", "L2_gnn_beta",
           "L2_gnn_W2", "L2_gnn_b2", "L3_gnn_Mw", "L3_gnn_Mb", "L3_gnn_Uw", "L3_gnn_Ub", "L3_gnn_bn_g", "L3_gnn_bn_b",
           "L3_gnn_mix_w", "L3_gnn_mix_b", "L3_gnn_ln_g", "L3_gnn_ln_b"]


def layouts(inputs):
    import numpy as np
    pad = EP - N_EDGES
    src = np.concatenate([np.asarray(inputs["src"]), np.zeros(pad, np.int32)])
    dst = np.concatenate([np.asarray(inputs["dst"]), np.full(pad, NP, np.int32)])
    weight = np.concatenate([np.asarray(inputs["edge_weight"]), np.zeros(pad, np.float32)])
    x = np.concatenate([np.asarray(inputs["x"]), np.zeros((NP - N_NODES, FEAT), np.float32)])
    arrays = {
        "x_pad": x,
        "dst_pad": np.concatenate([np.full(1, -1, np.int32), dst]),
        "dst_last": np.ascontiguousarray(dst.reshape(ET, P)[:, P - 1:].reshape(1, ET)),
        "dst_tiles": dst.reshape(ET, P),
        "src_tiles": src.reshape(ET, P),
        "src_cols": np.ascontiguousarray(src.reshape(ET, P).T),
        "wgt_tiles": weight.reshape(ET, P),
    }
    for name in _PARAMS:
        arrays[name] = np.ascontiguousarray(inputs[name])
    return arrays


def kernel(**inputs):
    import concourse.bacc as _bacc
    from concourse.bass_utils import run_bass_kernel_spmd as _run

    nc = _bacc.Bacc("TRN2", target_bir_lowering=False, num_devices=1)
    arrays = layouts(inputs)
    io = {name: nc.dram_tensor("in_" + name, list(a.shape), mybir.dt.from_np(a.dtype), kind="ExternalInput").ap() for name, a in arrays.items()}
    out = nc.dram_tensor("out", [N_NODES, FEAT], FP32, kind="ExternalOutput").ap()
    program(nc, io, out)
    r = _run(nc, [{"in_" + name: a for name, a in arrays.items()}], core_ids=[0])
    return r.results[0]["out"]
```

```python
import concourse.bass as bass
from concourse import mybir
from contextlib import ExitStack

FP32 = mybir.dt.float32
BF16 = mybir.dt.bfloat16
FP16 = mybir.dt.float16
INT32 = mybir.dt.int32
ALU = mybir.AluOpType
ACT = mybir.ActivationFunctionType
AX = mybir.AxisListType

P = 128
N_NODES = 3125
FEAT = 128
NT = -(-N_NODES // P)
NP = NT * P
N_EDGES = 100000
EI = 512
EP = -(-N_EDGES // EI) * EI
ET = EP // P
WIN = 16
CELLS = WIN * NT
NWIN = NP // WIN
PER = P // WIN
STEPS = N_EDGES // P + NWIN
SG = -(-STEPS // P)
CHUNK = 400
NC = NP // CHUNK
BIG = 1e30


class Chain:

    def __init__(self, eng, sem, base=0):
        self.eng, self.sem, self.n = eng, sem, base

    def __call__(self, ins):
        ins.then_inc(self.sem, 1)
        self.n = self.n + 1
        self.eng.wait_ge(self.sem, self.n)


def windows_and_steps(nc, io, st):
    with ExitStack() as ctx:
        def sb(name, shape, dt):
            return ctx.enter_context(nc.sbuf_tensor(name, shape, dt))

        def sem(name):
            return ctx.enter_context(nc.semaphore(name))

        last_i = sb("last_i", [P, ET], INT32)
        last_f = sb("last_f", [P, ET], FP32)
        junk = sb("cmp_junk", [P, ET], FP32)
        node_p1_i = sb("node_p1_i", [P, NT], INT32)
        node_p1 = sb("node_p1", [P, NT], FP32)
        step_i = sb("step_i", [P, SG], INT32)
        step_f = sb("step_f", [P, SG], FP32)
        win_thr_i = sb("win_thr_i", [P, 2], INT32)
        win_thr = sb("win_thr", [P, 2], FP32)
        win_tile = sb("win_tile", [P, 2], FP32)
        win_end_i = sb("win_end_i", [P, 2], INT32)
        ends_bi = sb("ends_bi", [P, NWIN], INT32)
        ends_b = sb("ends_b", [P, NWIN], FP32)
        node_tile = sb("node_tile", [P, NT], FP32)
        node_tile_i = sb("node_tile_i", [P, NT], INT32)
        node_rows_i = sb("node_rows_i", [P, NT, P], INT32)
        node_rows = sb("node_rows", [P, P], FP32)
        node_cnt = sb("node_cnt", [P, NT], FP32)
        end_f = sb("end_f", [P, NT], FP32)
        win_of = sb("win_of", [P, SG], FP32)
        tile_of = sb("tile_of", [P, SG], FP32)
        tile_of_i = sb("tile_of_i", [P, SG], INT32)
        src_s = sb("src_s", [P, SG, P], INT32)
        dst_s = sb("dst_s", [P, SG, P], INT32)
        wgt_s = sb("wgt_s", [P, SG, P], FP32)
        shi_i = sb("shi_i", [P, SG, P], INT32)
        slo_i = sb("slo_i", [P, SG, P], INT32)
        key_f = sb("key_f", [P, SG, P], FP32)
        slo_f = sb("slo_f", [P, SG, P], FP32)
        tabs = (key_f, slo_f, wgt_s)
        dst_cur = sb("dst_cur", [P, EP // P], INT32)
        dst_prev = sb("dst_prev", [P, EP // P], INT32)
        differs = sb("differs", [P, EP // P], FP32)
        pens = sb("start_pens", [P, 2, EP // P], BF16)
        zero_row = sb("zero_row", [1, P], FP32)
        psT = [ctx.enter_context(nc.psum_tensor(f"psT{i}", [P, 512], FP32)) for i in range(2)]

        s_const = sem("p0_const")
        s_last = sem("p0_last")
        s_dst = sem("p0_dst")
        s_chain = sem("p0_chain")
        s_wend = sem("p0_wend")
        s_wout = sem("p0_wout")
        s_wback = sem("p0_wback")
        s_nidx = sem("p0_nidx")
        s_ngat = sem("p0_ngat")
        s_sidx = sem("p0_sidx")
        s_sgat = sem("p0_sgat")
        s_end = sem("p0_end")
        s_eout = sem("p0_eout")
        s_pen = sem("p0_pen")
        s_pout = sem("p0_pout")
        s_tabs = sem("p0_tabs")
        s_tr = sem("p0_tr")
        s_ev = sem("p0_ev")
        s_zout = sem("p0_zero_out")

        with nc.Block() as block:
            @block.sync
            def _(sp):
                sp.dma_start(last_i[:, :], io["dst_last"].to_broadcast((P, ET))).then_inc(s_last, 16)
                sp.dma_start(dst_cur[:, :], io["dst_pad"][1:EP + 1].rearrange("(p c) -> p c", p=P)).then_inc(s_dst, 16)
                sp.dma_start(dst_prev[:, :], io["dst_pad"][0:EP].rearrange("(p c) -> p c", p=P)).then_inc(s_dst, 16)
                sp.wait_ge(s_wend, 1)
                with nc.allow_non_contiguous_dma(reason="256 words"):
                    sp.dma_start(st["win_ends"][0:2 * P].rearrange("(j p) -> p j", p=P), win_end_i[:, :]).then_inc(s_wout, 16)
                sp.wait_ge(s_wout, 16)
                sp.dma_start(ends_bi[:, :], st["win_ends"][0:NWIN].rearrange("(a n) -> a n", a=1).to_broadcast((P, NWIN))).then_inc(s_wback, 16)
                sp.dma_start(st["ends_row"][0:1, 1:NWIN + 1], st["win_ends"][0:NWIN].rearrange("(a n) -> a n", a=1)).then_inc(s_wback, 16)
                sp.wait_ge(s_pen, 2)
                for i in range(2):
                    sp.dma_start(st["pens"][i, :].rearrange("(p c) -> p c", p=P), pens[:, i, :]).then_inc(s_pout, 16)
                sp.wait_ge(s_end, 1)
                with nc.allow_non_contiguous_dma(reason="3200 words"):
                    sp.dma_start(st["node_ends"][P:P + NP].rearrange("(g p) -> p g", p=P), end_f[:, :]).then_inc(s_eout, 16)
                sp.wait_ge(s_eout, 16)
                sp.wait_ge(s_pout, 32)
                sp.wait_ge(s_wback, 32)

            @block.gpsimd
            def _(pool):
                pool.iota(node_p1_i[:, :], pattern=[[P, NT]], base=1, channel_multiplier=1).then_inc(s_const, 1)
                pool.iota(step_i[:, :], pattern=[[P, SG]], base=0, channel_multiplier=1).then_inc(s_const, 1)
                pool.iota(win_thr_i[:, :], pattern=[[P * WIN, 2]], base=WIN, channel_multiplier=WIN).then_inc(s_const, 1)
                pool.memset(st["ident"][:, :], 0.0).then_inc(s_const, 1)
                pool.wait_ge(s_const, 4)
                pool.affine_select(out=st["ident"][:, :], in_=st["ident"][:, :], compare_op=ALU.not_equal, fill=1.0,
                                   base=0, pattern=[[-1, P]], channel_multiplier=1).then_inc(s_const, 1)
                pool.iota(st["cell_iota"][:, :], pattern=[[1, CELLS]], base=0, channel_multiplier=0,
                          allow_small_or_imprecise_dtypes=True).then_inc(s_const, 1)
                pool.memset(st["ends_row"][0:1, NWIN + 1:NWIN + 2], 0).then_inc(s_const, 1)
                pool.memset(zero_row[:, :], 0.0).then_inc(s_const, 1)
                pool.wait_ge(s_nidx, 1)
                for g in range(NT):
                    pool.indirect_dma_start(out=node_rows_i[:, g, :], out_offset=None, in_=io["dst_tiles"],
                                            in_offset=bass.IndirectOffsetOnAxis(ap=node_tile_i[:, g:g + 1], axis=0)).then_inc(s_ngat, 16)
                pool.wait_ge(s_sidx, 1)
                for g in range(SG):
                    for table, rows in ((io["src_tiles"], src_s), (io["dst_tiles"], dst_s), (io["wgt_tiles"], wgt_s)):
                        pool.indirect_dma_start(out=rows[:, g, :], out_offset=None, in_=table,
                                                in_offset=bass.IndirectOffsetOnAxis(ap=tile_of_i[:, g:g + 1], axis=0)).then_inc(s_sgat, 16)

            @block.vector
            def _(dve):
                link = Chain(dve, s_chain)
                dve.wait_ge(s_const, 7)
                link(dve.tensor_copy(node_p1[:, :], node_p1_i[:, :]))
                link(dve.tensor_copy(step_f[:, :], step_i[:, :]))
                link(dve.tensor_copy(win_thr[:, :], win_thr_i[:, :]))
                dve.wait_ge(s_last, 16)
                link(dve.tensor_copy(last_f[:, :], last_i[:, :]))
                for j in range(2):
                    link(dve.tensor_scalar(junk[:, :], last_f[:, :], win_thr[:, j:j + 1], 0.0, ALU.is_lt, ALU.add,
                                           accum_out=win_tile[:, j:j + 1]))
                dve.scalar_tensor_tensor(win_end_i[:, :], win_thr[:, :], 1.0 / WIN, win_tile[:, :], ALU.mult, ALU.add).then_inc(s_wend, 1)
                for g in range(NT):
                    link(dve.tensor_scalar(junk[:, :], last_f[:, :], node_p1[:, g:g + 1], 0.0, ALU.is_lt, ALU.add,
                                           accum_out=node_tile[:, g:g + 1]))
                dve.tensor_copy(node_tile_i[:, :], node_tile[:, :]).then_inc(s_nidx, 1)
                dve.wait_ge(s_wback, 32)
                link(dve.tensor_copy(ends_b[:, :], ends_bi[:, :]))
                for g in range(SG):
                    link(dve.tensor_scalar(junk[:, 0:NWIN], ends_b[:, :], step_f[:, g:g + 1], 0.0, ALU.is_le, ALU.add,
                                           accum_out=win_of[:, g:g + 1]))
                link(dve.tensor_tensor(tile_of[:, :], step_f[:, :], win_of[:, :], ALU.subtract))
                dve.tensor_scalar(tile_of_i[:, :], tile_of[:, :], float(ET - 1), None, ALU.min).then_inc(s_sidx, 1)
                dve.wait_ge(s_dst, 32)
                link(dve.tensor_tensor(differs[:, :], dst_cur[:, :], dst_prev[:, :], ALU.not_equal))
                dve.tensor_scalar(pens[:, 0, :], differs[:, :], -BIG, None, ALU.mult).then_inc(s_pen, 1)
                dve.tensor_scalar(pens[:, 1, :], differs[:, :], BIG, None, ALU.mult).then_inc(s_pen, 1)
                for g in range(NT):
                    dve.wait_ge(s_ngat, 16 * NT)
                    link(dve.tensor_copy(node_rows[:, :], node_rows_i[:, g, :]))
                    link(dve.tensor_scalar(junk[:, 0:P], node_rows[:, :], node_p1[:, g:g + 1], 0.0, ALU.is_lt, ALU.add,
                                           accum_out=node_cnt[:, g:g + 1]))
                link(dve.scalar_tensor_tensor(end_f[:, :], node_tile[:, :], float(P), node_cnt[:, :], ALU.mult, ALU.add))
                dve.tensor_scalar(st["last_edge"][:, :], end_f[:, :], -1.0, 0.0, ALU.add, ALU.max).then_inc(s_end, 1)
                dve.wait_ge(s_sgat, 16 * 3 * SG)
                link(dve.tensor_scalar(shi_i[:, :, :], src_s[:, :, :], 7, None, ALU.arith_shift_right))
                link(dve.tensor_scalar(slo_i[:, :, :], src_s[:, :, :], P - 1, None, ALU.bitwise_and))
                link(dve.tensor_copy(slo_f[:, :, :], slo_i[:, :, :]))
                link(dve.scalar_tensor_tensor(key_f[:, :, :], dst_s[:, :, :], float(NT), shi_i[:, :, :], ALU.mult, ALU.add))
                link(dve.tensor_scalar(win_of[:, :], win_of[:, :], -float(CELLS), None, ALU.mult))
                for g in range(SG):
                    last = dve.tensor_scalar(key_f[:, g, :], key_f[:, g, :], win_of[:, g:g + 1], None, ALU.add)
                last.then_inc(s_tabs, 1)

            @block.tensor
            def _(pe):
                pe.wait_ge(s_const, 5)
                pe.wait_ge(s_tabs, 1)
                for n in range(3 * SG // 4):
                    if n >= 2:
                        pe.wait_ge(s_ev, n - 1)
                    for q in range(4):
                        i, g = divmod(4 * n + q, SG)
                        last = pe.transpose(psT[n % 2][:, q * P:(q + 1) * P], tabs[i][:, g, :], st["ident"][:, :])
                    last.then_inc(s_tr, 1)

            @block.scalar
            def _(act):
                act.wait_ge(s_const, 8)
                act.dma_start(st["node_ends"][0:P].rearrange("(a n) -> a n", a=1), zero_row[:, :]).then_inc(s_zout, 16)
                for n in range(3 * SG // 4):
                    i, g = divmod(4 * n, SG)
                    act.wait_ge(s_tr, n + 1)
                    act.copy(st["steps"][:, i, g * P:(g + 4) * P], psT[n % 2][:, :]).then_inc(s_ev, 1)
                act.wait_ge(s_zout, 16)


def build_adjacency(nc, st):
    RING = 8
    with ExitStack() as ctx:
        def sb(name, shape, dt):
            return ctx.enter_context(nc.sbuf_tensor(name, shape, dt))

        def sem(name):
            return ctx.enter_context(nc.semaphore(name))

        cells_c = sb("cells_c", [P, RING, CELLS], BF16)
        cells_a = sb("cells_a", [P, RING, CELLS], FP32)
        rows_c = sb("rows_c", [P, RING, P], BF16)
        rows_a = sb("rows_a", [P, RING, P], FP32)
        now = sb("step_now", [P, 3, RING], FP32)
        now_spare = sb("ahead_spare", [P, 1], FP32)
        now_spare2 = sb("ahead_spare2", [P, 1], FP32)
        stage_c = sb("stage_c", [P, 2, NT, P], FP32)
        stage_a = sb("stage_a", [P, NT, P], FP32)
        stage_t = sb("stage_t", [P, 2, NP], FP32)
        zero_b = sb("zero_b", [P, P], BF16)
        iota_f = sb("cell_iota_f", [P, CELLS], FP32)
        ps = ctx.enter_context(nc.psum_tensor("ps_windows", [P, 4 * 512], FP32))
        ps_t = [ctx.enter_context(nc.psum_tensor(f"ps_t{i}", [P, 512], FP32)) for i in range(2)]
        SUMS = 2 * 512
        s_zero = sem("p1_zero")
        s_made = sem("p1_made")
        s_now = sem("p1_columns")
        s_used = sem("p1_used")
        s_win = sem("p1_window_summed")
        s_free = sem("p1_window_copied")
        s_tr = sem("p1_transposed")
        s_trc = sem("p1_transpose_copied")
        s_cout = [sem(f"p1_c_out{i}") for i in range(2)]
        s_tout = [sem(f"p1_t_out{i}") for i in range(2)]
        TB = -(-NT // 4)
        AHEAD = 2

        def over_tiles(eng, body):
            with eng.Fori(0, NT // 2) as half:
                body(half * 2, 0)
                body(half * 2 + 1, 1)
            body(NT - 1, 0)

        with nc.Block() as block:
            @block.vector
            def _(dve):
                dve.memset(zero_b[:, :], 0.0).then_inc(s_zero, 1)
                dve.tensor_copy(iota_f[:, :], st["cell_iota"][:, :]).then_inc(s_zero, 1)
                dve.wait_ge(s_zero, 2)

                def columns(turn):
                    dve.tensor_copy(now[:, :, :], st["steps"][:, :, bass.ds(turn * RING, RING)]).then_inc(s_now, 1)
                    dve.wait_ge(s_now, turn + 1)

                def make(slot):
                    def col(i):
                        return now[:, i, slot:slot + 1]
                    dve.tensor_scalar(cells_c[:, slot, :], st["cell_iota"][:, :], col(0), None, ALU.is_equal)
                    dve.tensor_scalar(cells_a[:, slot, :], iota_f[:, :], col(0), None, ALU.is_equal)
                    dve.tensor_scalar(rows_c[:, slot, :], st["cell_iota"][:, 0:P], col(1), None, ALU.is_equal)
                    dve.tensor_scalar(rows_a[:, slot, :], iota_f[:, 0:P], col(1), col(2), ALU.is_equal, ALU.mult).then_inc(s_made, 1)

                columns(0)
                for slot in range(RING):
                    make(slot)
                with dve.Fori(1, STEPS // RING) as turn:
                    dve.wait_ge(s_made, turn * RING)
                    columns(turn)
                    for slot in range(RING):
                        dve.wait_ge(s_used, (turn - 1) * RING + slot + 1)
                        make(slot)
                dve.wait_ge(s_made, STEPS // RING * RING)
                columns(STEPS // RING)
                for k in range(STEPS // RING * RING, STEPS):
                    dve.wait_ge(s_used, k - RING + 1)
                    make(k % RING)

            @block.tensor
            def _(pe):
                half = pe.alloc_register("window_half")
                window = pe.alloc_register("window")
                left = pe.alloc_register("windows_left_in_tile")
                tile_no = pe.alloc_register("tile_no")
                ends_at = pe.alloc_register("window_ends_at")

                def mark(at, start):
                    for off in (0, SUMS):
                        last = pe.matmul(ps[:, bass.ds(at + (off + CELLS), 1)], zero_b[:, :], zero_b[:, 0:1], start=start, stop=not start, skip_group_check=True)
                    return last

                def transposes():
                    t = pe.snap(tile_no)
                    pe.wait_ge(s_free, (t + 1) * PER * 2 + AHEAD)
                    for b in range(TB):
                        pe.wait_ge(s_trc, t * TB + b + 1)
                        for q in range(min(4, NT - 4 * b)):
                            last = pe.transpose(ps_t[b % 2][:, q * P:(q + 1) * P], stage_a[:, 4 * b + q, :], st["ident"][:, :])
                        last.then_inc(s_tr, 1)
                    pe.reg_add(tile_no, tile_no, 1)
                    pe.reg_mov(left, PER)

                def step(k, slot):
                    pe.wait_ge(s_made, k + 1)
                    at = pe.snap(half, min_val=0, max_val=512)
                    pe.matmul(ps[:, bass.ds(at, CELLS)], rows_c[:, slot, :], cells_c[:, slot, :], start=False, stop=False, skip_group_check=True)
                    pe.matmul(ps[:, bass.ds(at + SUMS, CELLS)], rows_a[:, slot, :], cells_a[:, slot, :],
                              start=False, stop=False, skip_group_check=True).then_inc(s_used, 1)
                    with pe.If_eq(ends_at, k + 1):
                        mark(at, False).then_inc(s_win, 1)
                        pe.reg_add(window, window, 1)
                        pe.reg_alu(half, half, 512, ALU.bitwise_xor)
                        pe.reg_add(left, left, -1)
                        with pe.If_eq(left, 0):
                            transposes()
                        w = pe.snap(window, min_val=1, max_val=NWIN)
                        pe.load(ends_at, st["ends_row"][0:1, bass.ds(w + 1, 1)])
                        pe.wait_ge(s_free, w * 2)
                        mark(pe.snap(half, min_val=0, max_val=512), True)

                pe.wait_ge(s_zero, 1)
                pe.reg_mov(half, 0)
                pe.reg_mov(window, 0)
                pe.reg_mov(left, PER)
                pe.reg_mov(tile_no, 0)
                pe.load(ends_at, st["ends_row"][0:1, 1:2])
                mark(pe.snap(half, min_val=0, max_val=512), True)
                with pe.Fori(0, STEPS // RING) as turn:
                    for slot in range(RING):
                        step(turn * RING + slot, slot)
                for k in range(STEPS // RING * RING, STEPS):
                    step(k, k % RING)

            @block.scalar
            def _(act):
                act.copy(now_spare[:, :], st["cell_iota"][:, 0:1]).then_inc(s_free, AHEAD)
                act.copy(now_spare2[:, :], st["cell_iota"][:, 0:1]).then_inc(s_trc, 2)

                def tile(t, parity, first=False):
                    for j in range(PER):
                        w = t * PER + j
                        act.wait_ge(s_win, w + 1)
                        if j == 0 and not first:
                            act.wait_ge(s_cout[parity], ((t - parity) // 2) * 16)
                        for bank, stage in ((0, stage_c[:, parity, :, j * WIN:(j + 1) * WIN]), (2, stage_a[:, :, j * WIN:(j + 1) * WIN])):
                            at = (bank + j % 2) * 512
                            act.copy(stage, ps[:, at:at + CELLS].rearrange("p (d s) -> p s d", s=NT)).then_inc(s_free, 1)
                    if not first:
                        act.wait_ge(s_tout[parity], ((t - parity) // 2) * 16)
                    for b in range(TB):
                        act.wait_ge(s_tr, t * TB + b + 1)
                        n = min(4, NT - 4 * b) * P
                        act.copy(stage_t[:, parity, 4 * b * P:4 * b * P + n], ps_t[b % 2][:, 0:n]).then_inc(s_trc, 1)

                tile(0, 0, True)
                tile(1, 1, True)
                with act.Fori(1, (NT - 1) // 2) as half:
                    tile(half * 2, 0)
                    tile(half * 2 + 1, 1)
                tile(NT - 1, 0)

            @block.sync
            def _(sp):
                def tile(t, parity):
                    sp.wait_ge(s_free, (t + 1) * PER * 2 + AHEAD)
                    sp.dma_start(st["C"][:, :, bass.ds(t * P, P)].rearrange("s p d -> p s d"), stage_c[:, parity, :, :]).then_inc(s_cout[parity], 16)
                    sp.wait_ge(s_trc, (t + 1) * TB + 2)
                    sp.dma_start(st["AT"][bass.ds(t, 1), :, :].rearrange("a p s -> p (a s)"), stage_t[:, parity, :]).then_inc(s_tout[parity], 16)

                over_tiles(sp, tile)
                for i in range(2):
                    sp.wait_ge(s_cout[i], 16 * ((NT + 1 - i) // 2))
                    sp.wait_ge(s_tout[i], 16 * ((NT + 1 - i) // 2))


class Signal:

    def __init__(self, sem):
        self.sem, self.base = sem, 0

    def at(self, n):
        return n + self.base

    def passed(self, n):
        self.base += n


class Steps(Chain):

    def __init__(self, eng, kept):
        super().__init__(eng, kept.sem, kept.base)
        self.kept = kept

    def done(self):
        self.kept.base = self.n


def in_ring(eng, ring, body, first_turn=0):
    for slot in range(ring):
        body(slot, slot, 0)
    with eng.Fori(1, NT // ring) as turn:
        for slot in range(ring):
            body(turn * ring + slot, slot, turn)
    for t in range(NT // ring * ring, NT):
        body(t, t % ring, NT // ring)


def banks(st):
    return st["ps"][:, :, 0:CHUNK]


def chunk(buf, c, rows=P):
    return buf[0:rows, c * CHUNK:(c + 1) * CHUNK]


def tile(buf, t, width=P, rows=P):
    return buf[0:rows, t * width:(t + 1) * width]


def dyn_tile(buf, t, width=P, rows=P):
    return buf[0:rows, bass.ds(t * width, width)]


def empty_banks(nc, block, st, out, ready, count):
    sig = st["sig"]

    def half(h):
        return (out[:, h * NP // 2:(h + 1) * NP // 2].rearrange("p (c n) -> p c n", n=CHUNK),
                banks(st)[:, h * NC // 2:(h + 1) * NC // 2, :])

    def scalar(act):
        if count:
            act.wait_ge(ready.sem, ready.at(count))
        act.copy(*half(0)).then_inc(sig["out"].sem, 1)

    @block.vector
    def _(dve):
        if count:
            dve.wait_ge(ready.sem, ready.at(count))
        dve.tensor_copy(*half(1)).then_inc(sig["out"].sem, 1)

    return scalar


def spread(nc, st, matrix, xn, out):
    sig, ring, stat = st["sig"], st["ring"], st["stat"]
    loaded, used, picked = sig["loaded"], sig["used"], sig["picked"]
    with nc.Block() as block:
        @block.sync
        def _(sp):
            def load(t, slot, turn):
                if not isinstance(t, int) or t >= RING:
                    sp.wait_ge(used.sem, used.at(t - RING + 1))
                sp.dma_start(ring[:, slot, :], matrix[bass.ds(t, 1), :, :].rearrange("a p n -> p (a n)")).then_inc(loaded[slot].sem, 16)
            in_ring(sp, RING, load)

        @block.tensor
        def _(pe):
            def multiply(t, slot, turn):
                pe.wait_ge(loaded[slot].sem, loaded[slot].at((turn + 1) * 16))
                pe.wait_ge(picked.sem, picked.at(t + 1))
                for c in range(NC):
                    last = pe.matmul(banks(st)[:, c, :], stat[:, slot, :], ring[:, slot, c * CHUNK:(c + 1) * CHUNK],
                                     start=isinstance(t, int) and t == 0, stop=isinstance(t, int) and t == NT - 1)
                last.then_inc(used.sem, 1)
            in_ring(pe, RING, multiply)

        empty = empty_banks(nc, block, st, out, used, NT)

        @block.scalar
        def _(act):
            def pick(t, slot, turn):
                if not isinstance(t, int) or t >= RING:
                    act.wait_ge(used.sem, used.at(t - RING + 1))
                act.copy(stat[:, slot, :], dyn_tile(xn, t)).then_inc(picked.sem, 1)
            in_ring(act, RING, pick)
            empty(act)
    for slot in range(RING):
        loaded[slot].passed(16 * len(range(slot, NT, RING)))
    used.passed(NT)
    picked.passed(NT)
    sig["out"].passed(2)


def flip(nc, st, source, out):
    sig, ident = st["sig"], st["ident"]
    turned, copied = sig["turned"], sig["out"]
    nb = -(-NT // 4)
    with nc.Block() as block:
        @block.tensor
        def _(pe):
            for b in range(nb):
                for q in range(min(4, NT - 4 * b)):
                    last = pe.transpose(st["ps"][:, b, q * P:(q + 1) * P], tile(source, 4 * b + q), ident[:, :])
                last.then_inc(turned.sem, 1)

        def copy_bank(eng, copy, b):
            n = min(4, NT - 4 * b) * P
            eng.wait_ge(turned.sem, turned.at(b + 1))
            copy(out[:, 4 * b * P:4 * b * P + n], st["ps"][:, b, 0:n]).then_inc(copied.sem, 1)

        @block.scalar
        def _(act):
            for b in range(0, nb, 2):
                copy_bank(act, act.copy, b)

        @block.vector
        def _(dve):
            for b in range(1, nb, 2):
                copy_bank(dve, dve.tensor_copy, b)
    turned.passed(nb)
    copied.passed(nb)


def empty_alone(nc, st, out):
    with nc.Block() as block:
        empty = empty_banks(nc, block, st, out, None, 0)

        @block.scalar
        def _(act):
            empty(act)
    st["sig"]["out"].passed(2)


def linear(nc, st, terms, out, bias=None, func=None, rows=P):
    sig = st["sig"]
    multiplied, copied = sig["used"], sig["out"]
    with nc.Block() as block:
        @block.tensor
        def _(pe):
            for c in range(NC):
                for i, (weight, x, k) in enumerate(terms):
                    last = pe.matmul(banks(st)[0:rows, c, :], weight, chunk(x, c, k), start=i == 0, stop=i == len(terms) - 1)
                last.then_inc(multiplied.sem, 1)

        @block.scalar
        def _(act):
            for c in range(NC):
                act.wait_ge(multiplied.sem, multiplied.at(c + 1))
                if bias is None:
                    act.copy(chunk(out, c, rows), banks(st)[0:rows, c, :]).then_inc(copied.sem, 1)
                else:
                    act.activation(chunk(out, c, rows), banks(st)[0:rows, c, :], func or ACT.Identity, bias=bias).then_inc(copied.sem, 1)
    multiplied.passed(NC)
    copied.passed(NC)


def over_features(buf):
    return buf[:, :].rearrange("p (t f) -> p t f", f=FEAT)


def norm_rows(nc, st, x, gain=None, shift=None):
    sig, work = st["sig"], st["norm_work"]
    mean, var = st["norm_mean"], st["norm_var"]
    ready, rooted = sig["to_act"], sig["from_act"]
    x3, w3 = over_features(x), over_features(work)

    def wide(col):
        return col[:, :].unsqueeze(2).to_broadcast((P, NT, FEAT))

    with nc.Block() as block:
        @block.vector
        def _(dve):
            link = Steps(dve, sig["dve"])
            link(dve.tensor_reduce(mean[:, :], x3, AX.X, ALU.add))
            link(dve.tensor_scalar(mean[:, :], mean[:, :], 1.0 / FEAT, None, ALU.mult))
            link(dve.tensor_tensor(x3, x3, wide(mean), ALU.subtract))
            link(dve.tensor_tensor(w3, x3, x3, ALU.mult))
            link(dve.tensor_reduce(var[:, :], w3, AX.X, ALU.add))
            dve.tensor_scalar(var[:, :], var[:, :], 1.0 / FEAT, 1e-5, ALU.mult, ALU.add).then_inc(ready.sem, 1)
            dve.wait_ge(rooted.sem, rooted.at(1))
            link(dve.reciprocal(var[:, :], var[:, :]))
            link(dve.tensor_tensor(x3, x3, wide(var), ALU.mult))
            if gain is not None:
                link(dve.tensor_tensor(x3, x3, gain.unsqueeze(1).to_broadcast((P, NT, FEAT)), ALU.mult))
                link(dve.tensor_tensor(x3, x3, shift.unsqueeze(1).to_broadcast((P, NT, FEAT)), ALU.add))
            link.done()

        @block.scalar
        def _(act):
            act.wait_ge(ready.sem, ready.at(1))
            act.sqrt(var[:, :], var[:, :]).then_inc(rooted.sem, 1)
    ready.passed(1)
    rooted.passed(1)


def norm_nodes(nc, st, x, gain, shift):
    sig, work, cols = st["sig"], st["norm_work"], st["node_cols"]
    ready, rooted = sig["to_act"], sig["from_act"]
    real = x[:, 0:N_NODES]
    with nc.Block() as block:
        @block.vector
        def _(dve):
            link = Steps(dve, sig["dve"])
            link(dve.tensor_reduce(cols[:, 0:1], real, AX.X, ALU.add))
            link(dve.tensor_scalar(cols[:, 0:1], cols[:, 0:1], 1.0 / N_NODES, None, ALU.mult))
            dve.tensor_scalar(x[:, :], x[:, :], cols[:, 0:1], None, ALU.subtract).then_inc(ready.sem, 1)
            dve.wait_ge(rooted.sem, rooted.at(1))
            dve.tensor_scalar(cols[:, 2:3], cols[:, 1:2], 1.0 / N_NODES, 1e-5, ALU.mult, ALU.add).then_inc(ready.sem, 1)
            dve.wait_ge(rooted.sem, rooted.at(2))
            link(dve.reciprocal(cols[:, 4:5], cols[:, 3:4]))
            link(dve.tensor_scalar(x[:, :], x[:, :], cols[:, 4:5], gain, ALU.mult, ALU.mult))
            link(dve.tensor_scalar(x[:, :], x[:, :], shift, None, ALU.add))
            link.done()

        @block.scalar
        def _(act):
            act.wait_ge(ready.sem, ready.at(1))
            act.activation(work[:, 0:N_NODES], real, ACT.Square, accum_out=cols[:, 1:2]).then_inc(rooted.sem, 1)
            act.wait_ge(ready.sem, ready.at(2))
            act.sqrt(cols[:, 3:4], cols[:, 2:3]).then_inc(rooted.sem, 1)
    ready.passed(2)
    rooted.passed(2)


def on_vector(nc, st, program):
    with nc.Block() as block:
        @block.vector
        def _(dve):
            link = Steps(dve, st["sig"]["dve"])
            program(dve, link)
            link.done()


def light_hops(nc, io, st):
    sig, x, en, et, acc = st["sig"], st["x"], st["buf_a"], st["buf_b"], st["buf_c"]
    with nc.Block() as block:
        @block.sync
        def _(sp):
            sp.dma_start(over_features(x), io["x_pad"].rearrange("(t p) f -> p t f", p=P)).then_inc(sig["params"].sem, 16)
            sp.wait_ge(sig["params"].sem, sig["params"].at(16))
    sig["params"].passed(16)
    for hop in range(3):
        spread(nc, st, st["AT"], x if hop == 0 else en, et)
        if hop == 0:
            on_vector(nc, st, lambda dve, link: link(dve.tensor_copy(acc[:, :], et[:, :])))
        else:
            on_vector(nc, st, lambda dve, link: link(dve.tensor_tensor(acc[:, :], acc[:, :], et[:, :], ALU.add)))
        if hop < 2:
            flip(nc, st, et, en)
    flip(nc, st, acc, en)

    def combine(dve, link):
        link(dve.tensor_tensor(en[:, :], en[:, :], x[:, :], ALU.add))
        link(dve.scalar_tensor_tensor(x[:, :], en[:, :], 0.25, x[:, :], ALU.mult, ALU.add))
    on_vector(nc, st, combine)
    norm_rows(nc, st, x)


HEADS = 4
HD = 32


def attention(nc, io, st):
    sig, x, xt = st["sig"], st["x"], st["buf_a"]
    out = st["buf_b"]
    flip(nc, st, x, xt)
    with ExitStack() as ctx:
        def sb(name, shape, dt=FP32):
            return ctx.enter_context(nc.sbuf_tensor(name, shape, dt))
        w = sb("gat_w", [HD, FEAT])
        att = sb("gat_att", [2 * HEADS, HD])
        bias = sb("gat_b", [HD, 1])
        wt = sb("gat_wt", [P, HD])
        att_t = sb("gat_att_t", [HD, 2 * HEADS])
        att_wide = sb("gat_att_wide", [HD, HEADS, P])
        wh = sb("gat_wh", [P, NT * HD])
        a_src = sb("gat_a_src", [P, NT * HEADS])
        a_dst = sb("gat_a_dst", [P, HEADS, NP])
        best = sb("gat_best", [P, HEADS])
        now = sb("gat_best_now", [P, 2, HEADS])
        best_all = sb("gat_best_all", [P, 4])
        bias_up = sb("gat_bias_up", [P, NT * HEADS])
        bias_down = sb("gat_bias_down", [P, NT * HEADS])
        params, turned, copied, used, ready, back = (sig[k] for k in ("params", "turned", "out", "used", "to_act", "from_act"))
        with nc.Block() as block:
            @block.sync
            def _(sp):
                sp.dma_start(w[:, :], io["L1_gnn_W"]).then_inc(params.sem, 16)
                sp.dma_start(att[0:HEADS, :], io["L1_gnn_att_src"]).then_inc(params.sem, 16)
                sp.dma_start(att[HEADS:2 * HEADS, :], io["L1_gnn_att_dst"]).then_inc(params.sem, 16)
                sp.dma_start(bias[:, :], io["L1_gnn_b"].rearrange("(p a) -> p a", a=1)).then_inc(params.sem, 16)

            @block.tensor
            def _(pe):
                pe.wait_ge(params.sem, params.at(64))
                pe.transpose(st["ps"][0:P, 0, 0:HD], w[:, :], st["ident"][0:HD, 0:HD]).then_inc(turned.sem, 1)
                pe.transpose(st["ps"][0:HD, 1, 0:2 * HEADS], att[:, :], st["ident"][0:2 * HEADS, 0:2 * HEADS]).then_inc(turned.sem, 1)

            @block.vector
            def _(dve):
                link = Steps(dve, sig["dve"])
                dve.wait_ge(turned.sem, turned.at(2))
                link(dve.tensor_copy(wt[:, :], st["ps"][0:P, 0, 0:HD]))
                link(dve.tensor_copy(att_t[:, :], st["ps"][0:HD, 1, 0:2 * HEADS]))
                link(dve.tensor_copy(att_wide[:, :, :], att_t[:, HEADS:2 * HEADS].unsqueeze(2).to_broadcast((HD, HEADS, P))))
                link.done()
        params.passed(64)
        turned.passed(2)
        with nc.sbuf_tensor("gat_wh_t", [HD, NP], FP32) as wh_t:
            linear(nc, st, [(wt[:, :], xt, P)], wh_t, bias=bias[:, 0:1], rows=HD)
            with nc.Block() as block:
                @block.tensor
                def _(pe):
                    for t in range(NT):
                        pe.transpose(st["ps"][:, t // 16, t % 16 * HD:(t % 16 + 1) * HD], tile(wh_t, t, rows=HD), st["ident"][0:HD, 0:HD])
                        last = pe.matmul(st["ps"][:, 2, t * HEADS:(t + 1) * HEADS], tile(wh_t, t, rows=HD), att_t[:, 0:HEADS], start=True, stop=True)
                    last.then_inc(turned.sem, 1)
                    for n in range(HEADS * NC):
                        h, c = divmod(n, NC)
                        if n >= 4:
                            pe.wait_ge(copied.sem, copied.at(n - 3))
                        pe.matmul(st["ps"][:, 4 + n % 4, 0:CHUNK], att_wide[:, h, :], chunk(wh_t, c, HD), start=True, stop=True).then_inc(used.sem, 1)

                @block.scalar
                def _(act):
                    for n in range(HEADS * NC):
                        h, c = divmod(n, NC)
                        act.wait_ge(used.sem, used.at(n + 1))
                        act.copy(a_dst[:, h, c * CHUNK:(c + 1) * CHUNK], st["ps"][:, 4 + n % 4, 0:CHUNK]).then_inc(copied.sem, 1)

                @block.vector
                def _(dve):
                    link = Steps(dve, sig["dve"])
                    dve.wait_ge(turned.sem, turned.at(1))
                    link(dve.tensor_copy(wh[:, 0:16 * HD], st["ps"][:, 0, :]))
                    link(dve.tensor_copy(wh[:, 16 * HD:NT * HD], st["ps"][:, 1, 0:(NT - 16) * HD]))
                    link(dve.tensor_copy(a_src[:, :], st["ps"][:, 2, 0:NT * HEADS]))
                    link.done()
            turned.passed(1)
            used.passed(HEADS * NC)
            copied.passed(HEADS * NC)

        R = 2
        loaded, made, seen = sig["loaded"], sig["picked"], sig["used"]
        with nc.sbuf_tensor("gat_pen", [P, R, NP], FP32) as pen, nc.sbuf_tensor("gat_best_junk", [P, HEADS, NP], BF16) as junk, nc.sbuf_tensor("gat_carrier", [P, 1], FP32) as carrier:
            ring = st["ring"]
            with nc.Block() as block:
                @block.sync
                def _(sp):
                    def load(t, slot, turn):
                        if not isinstance(t, int) or t >= R:
                            sp.wait_ge(made.sem, made.at(t - R + 1))
                        sp.dma_start(ring[:, slot, :], st["C"][bass.ds(t, 1), :, :].rearrange("a p n -> p (a n)")).then_inc(loaded[slot].sem, 16)
                    in_ring(sp, R, load)

                @block.scalar
                def _(act):
                    def penalise(t, slot, turn):
                        act.wait_ge(loaded[slot].sem, loaded[slot].at((turn + 1) * 16))
                        if not isinstance(t, int) or t >= R:
                            act.wait_ge(seen.sem, seen.at((t - R + 1) * HEADS))
                        act.activation(pen[:, slot, :], ring[:, slot, :], ACT.Relu, bias=st["big_col"][:, 0:1], scale=-BIG).then_inc(made.sem, 1)
                    in_ring(act, R, penalise)

                @block.vector
                def _(dve):
                    def largest(t, slot, turn):
                        dve.wait_ge(made.sem, made.at(t + 1))
                        if not isinstance(t, int) or t >= 1:
                            dve.wait_ge(sig["dve"].sem, sig["dve"].at(3 * t))
                        dve.memset(carrier[:, :], 0.0).then_inc(sig["dve"].sem, 1)
                        for h in range(HEADS):
                            dve.tensor_tensor_reduce(out=junk[:, h, :], in0=a_dst[:, h, :], in1=pen[:, slot, :], scale=1.0, scalar=-3e38,
                                                            op0=ALU.subtract, op1=ALU.max, accum_out=now[:, slot, h:h + 1]).then_inc(seen.sem, 1)
                        dve.wait_ge(seen.sem, seen.at(t * HEADS + HEADS))
                        dve.tensor_tensor(now[:, slot, :], now[:, slot, :], dyn_tile(a_src, t, HEADS), ALU.add).then_inc(sig["dve"].sem, 1)
                        dve.wait_ge(sig["dve"].sem, sig["dve"].at(3 * t + 2))
                        dve.tensor_tensor(best[:, :], now[:, slot, :], now[:, slot, :] if isinstance(t, int) and t == 0 else best[:, :],
                                          ALU.max).then_inc(sig["dve"].sem, 1)
                    in_ring(dve, R, largest)
            for slot in range(R):
                loaded[slot].passed(16 * len(range(slot, NT, R)))
            made.passed(NT)
            seen.passed(NT * HEADS)
            sig["dve"].passed(3 * NT)

        pooled = sig["pooled"]
        with nc.Block() as block:
            @block.vector
            def _(dve):
                link = Steps(dve, sig["dve"])
                dve.tensor_reduce(best_all[:, 0:1], best[:, :], AX.X, ALU.max).then_inc(ready.sem, 1)
                dve.wait_ge(pooled.sem, pooled.at(1))
                link(dve.tensor_scalar(best_all[:, 2:3], best_all[:, 1:2], 0.2, None, ALU.mult))
                link(dve.tensor_tensor(best_all[:, 3:4], best_all[:, 1:2], best_all[:, 2:3], ALU.max))
                link(dve.tensor_scalar(bias_up[:, :], a_src[:, :], best_all[:, 3:4], None, ALU.subtract))
                link(dve.tensor_scalar(bias_down[:, :], a_src[:, :], 0.2, best_all[:, 3:4], ALU.mult, ALU.subtract))
                link.done()

            @block.gpsimd
            def _(pool):
                pool.wait_ge(ready.sem, ready.at(1))
                pool.partition_all_reduce(best_all[:, 1:2], best_all[:, 0:1], P, bass.bass_isa.ReduceOp.max).then_inc(pooled.sem, 1)
        ready.passed(1)
        pooled.passed(1)

        R = 3
        down = (xt, st["norm_work"])
        with (nc.sbuf_tensor("gat_exp", [P, 2, NP], FP32) as expd,
              nc.sbuf_tensor("gat_share", [P, 2, NP], FP32) as share, nc.sbuf_tensor("gat_den", [P, 2, 2], FP32) as den,
              nc.sbuf_tensor("gat_message", [P, 2, HD], FP32) as message):
            ring = st["ring"]
            exped, shared, scaled, spent = sig["from_act"], sig["shared"], sig["scaled"], sig["used"]
            with nc.Block() as block:
                @block.sync
                def _(sp):
                    def load(t, slot, turn):
                        if not isinstance(t, int) or t >= R:
                            sp.wait_ge(shared.sem, shared.at((t - R + 1) * HEADS))
                        sp.dma_start(ring[:, slot, :], st["C"][bass.ds(t, 1), :, :].rearrange("a p n -> p (a n)")).then_inc(loaded[slot].sem, 16)
                    in_ring(sp, R, load)

                @block.scalar
                def _(act):
                    def exps(t, slot, turn):
                        for h in range(HEADS):
                            n = t * HEADS + h
                            if not isinstance(n, int) or n >= 2:
                                act.wait_ge(shared.sem, shared.at(n - 1))
                            act.activation(expd[:, h % 2, :], a_dst[:, h, :], ACT.Exp, bias=bias_up[:, bass.ds(n, 1)])
                            act.activation(down[h % 2][:, :], a_dst[:, h, :], ACT.Exp, bias=bias_down[:, bass.ds(n, 1)], scale=0.2).then_inc(exped.sem, 1)
                    in_ring(act, R, exps)

                @block.vector
                def _(dve):
                    def shares(t, slot, turn):
                        dve.wait_ge(loaded[slot].sem, loaded[slot].at((turn + 1) * 16))
                        for h in range(HEADS):
                            n = t * HEADS + h
                            par = h % 2
                            dve.wait_ge(exped.sem, exped.at(n + 1))
                            if not isinstance(n, int) or n >= 2:
                                dve.wait_ge(spent.sem, spent.at(n - 1))
                            dve.tensor_tensor(expd[:, par, :], expd[:, par, :], down[par][:, :], ALU.max).then_inc(sig["dve"].sem, 1)
                            dve.wait_ge(sig["dve"].sem, sig["dve"].at(3 * n + 1))
                            dve.scalar_tensor_tensor(share[:, par, :], expd[:, par, :], 1.0, ring[:, slot, :], ALU.min, ALU.mult,
                                                     accum_out=den[:, par, 0:1]).then_inc(shared.sem, 1)
                            dve.wait_ge(shared.sem, shared.at(n + 1))
                            dve.tensor_scalar(den[:, par, 0:1], den[:, par, 0:1], 1e-16, None, ALU.add).then_inc(sig["dve"].sem, 1)
                            dve.wait_ge(sig["dve"].sem, sig["dve"].at(3 * n + 2))
                            dve.reciprocal(den[:, par, 1:2], den[:, par, 0:1]).then_inc(sig["dve"].sem, 1)
                            dve.wait_ge(sig["dve"].sem, sig["dve"].at(3 * n + 3))
                            dve.tensor_scalar(message[:, par, :], dyn_tile(wh, t, HD), den[:, par, 1:2], None, ALU.mult).then_inc(scaled.sem, 1)
                    in_ring(dve, R, shares)

                @block.tensor
                def _(pe):
                    def sums(t, slot, turn):
                        for h in range(HEADS):
                            n = t * HEADS + h
                            pe.wait_ge(scaled.sem, scaled.at(n + 1))
                            for c in range(NC):
                                last = pe.matmul(banks(st)[h * HD:(h + 1) * HD, c, :], message[:, h % 2, :], share[:, h % 2, c * CHUNK:(c + 1) * CHUNK],
                                                 start=isinstance(t, int) and t == 0, stop=isinstance(t, int) and t == NT - 1)
                            last.then_inc(spent.sem, 1)
                    in_ring(pe, R, sums)

            for slot in range(R):
                loaded[slot].passed(16 * len(range(slot, NT, R)))
            for s, n in ((exped, NT * HEADS), (shared, NT * HEADS), (scaled, NT * HEADS), (spent, NT * HEADS), (sig["dve"], 3 * NT * HEADS)):
                s.passed(n)
    empty_alone(nc, st, out)
    flip(nc, st, out, xt)
    on_vector(nc, st, lambda dve, link: link(dve.tensor_tensor(x[:, :], x[:, :], xt[:, :], ALU.add)))
    norm_rows(nc, st, x)


def isomorphism(nc, io, st):
    sig, x = st["sig"], st["x"]
    agg, ht = st["buf_a"], st["buf_b"]
    with nc.sbuf_tensor("gin_w", [P, 2, P], FP32) as w, nc.sbuf_tensor("gin_vecs", [P, 4], FP32) as vecs:
        params = sig["params"]
        with nc.Block() as block:
            @block.sync
            def _(sp):
                sp.dma_start(w[:, 0, :], io["L2_gnn_W1"]).then_inc(params.sem, 16)
                sp.dma_start(w[:, 1, :], io["L2_gnn_W2"]).then_inc(params.sem, 16)
                for i, name in enumerate(("L2_gnn_b1", "L2_gnn_gamma", "L2_gnn_beta", "L2_gnn_b2")):
                    sp.dma_start(vecs[:, i:i + 1], io[name].rearrange("(p a) -> p a", a=1)).then_inc(params.sem, 16)
                sp.wait_ge(params.sem, params.at(96))
        params.passed(96)
        spread(nc, st, st["C"], x, agg)
        flip(nc, st, x, ht)
        on_vector(nc, st, lambda dve, link: link(dve.tensor_tensor(agg[:, :], agg[:, :], ht[:, :], ALU.add)))
        linear(nc, st, [(w[:, 0, :], agg, P)], ht, bias=vecs[:, 0:1])
        norm_nodes(nc, st, ht, vecs[:, 1:2], vecs[:, 2:3])
        on_vector(nc, st, lambda dve, link: link(dve.tensor_scalar(ht[:, :], ht[:, :], 0.0, None, ALU.max)))
        linear(nc, st, [(w[:, 1, :], ht, P)], agg, bias=vecs[:, 3:4], func=ACT.Relu)
        flip(nc, st, agg, ht)
        on_vector(nc, st, lambda dve, link: link(dve.tensor_tensor(x[:, :], x[:, :], ht[:, :], ALU.add)))
        norm_rows(nc, st, x)


LAYERS = 3
UB = 13
WB = 2 + UB + 1


def degrees(nc, st):
    sig = st["sig"]
    recip, amp, att = st["recip_deg"], st["amplify"], st["attenuate"]
    ends = st["node_ends"]
    with nc.sbuf_tensor("ends_now", [P, NP], FP32) as now, nc.sbuf_tensor("ends_before", [P, NP], FP32) as before, \
            nc.sbuf_tensor("ends_cols", [P, 2, NT], FP32) as cols:
        params, ready, back = sig["params"], sig["to_act"], sig["from_act"]
        with nc.Block() as block:
            @block.sync
            def _(sp):
                for row, lo in ((now, P), (before, P - 1)):
                    sp.dma_start(row[:, :], ends[lo:lo + NP].rearrange("(a n) -> a n", a=1).to_broadcast((P, NP))).then_inc(params.sem, 16)
                with nc.allow_non_contiguous_dma(reason="3200 words"):
                    for i, lo in enumerate((P, P - 1)):
                        sp.dma_start(cols[:, i, :], ends[lo:lo + NP].rearrange("(t p) -> p t", p=P)).then_inc(params.sem, 16)

            @block.vector
            def _(dve):
                link = Steps(dve, sig["dve"])
                dve.wait_ge(params.sem, params.at(64))
                link(dve.tensor_tensor(now[:, :], now[:, :], before[:, :], ALU.subtract))
                dve.tensor_scalar(now[:, :], now[:, :], 1.0, None, ALU.add).then_inc(ready.sem, 1)
                dve.wait_ge(ready.sem, ready.at(1))
                link(dve.reciprocal(recip[:, :], now[:, :]))
                dve.wait_ge(back.sem, back.at(1))
                link(dve.tensor_scalar(amp[:, :], amp[:, :], 0.25, None, ALU.mult))
                link(dve.reciprocal(att[:, :], amp[:, :]))
                link(dve.tensor_tensor(cols[:, 0, :], cols[:, 0, :], cols[:, 1, :], ALU.is_equal))
                link(dve.tensor_scalar(st["no_edge"][:, :], cols[:, 0, :], -BIG, None, ALU.mult))
                link.done()

            @block.scalar
            def _(act):
                act.wait_ge(ready.sem, ready.at(1))
                act.activation(amp[:, :], now[:, :], ACT.Ln, bias=1.0).then_inc(back.sem, 1)
        params.passed(64)
        ready.passed(1)
        back.passed(1)


def load_layer(nc, io, st, layer, wt, vecs, rows):
    sig = st["sig"]
    params, turned, copied = sig["params"], sig["turned"], sig["out"]
    with nc.sbuf_tensor(f"raw_w{layer}", [P, WB * P], FP32) as raw:
        with nc.Block() as block:
            @block.sync
            def _(sp):
                sp.dma_start(raw[:, 0:2 * P], io["L3_gnn_Mw"][layer, :, :]).then_inc(params.sem, 16)
                sp.dma_start(raw[:, 2 * P:(2 + UB) * P], io["L3_gnn_Uw"][layer, :, :]).then_inc(params.sem, 16)
                sp.dma_start(raw[:, (2 + UB) * P:WB * P], io["L3_gnn_mix_w"][layer, :, :]).then_inc(params.sem, 16)
                for i, name in enumerate(("Mb", "Ub", "bn_g", "bn_b", "mix_b")):
                    sp.dma_start(vecs[:, i:i + 1], io["L3_gnn_" + name][layer, :].rearrange("(p a) -> p a", a=1)).then_inc(params.sem, 16)
                for i, name in enumerate(("ln_g", "ln_b")):
                    sp.dma_start(rows[:, i, :], io["L3_gnn_" + name][layer:layer + 1, :].to_broadcast((P, P))).then_inc(params.sem, 16)
                sp.wait_ge(params.sem, params.at(160))

            @block.tensor
            def _(pe):
                pe.wait_ge(params.sem, params.at(160))
                for b in range(WB // 4):
                    for q in range(4):
                        last = pe.transpose(st["ps"][:, b, q * P:(q + 1) * P], raw[:, (4 * b + q) * P:(4 * b + q + 1) * P], st["ident"][:, :])
                    last.then_inc(turned.sem, 1)

            @block.scalar
            def _(act):
                for b in range(WB // 4):
                    act.wait_ge(turned.sem, turned.at(b + 1))
                    act.copy(wt[:, 4 * b * P:4 * (b + 1) * P], st["ps"][:, b, :]).then_inc(copied.sem, 1)
        params.passed(160)
        turned.passed(WB // 4)
        copied.passed(WB // 4)


TILES_IN = EI // P
GSTEPS = EP // EI
GU = 4
SPANS = 7
SPAN = -(-N_NODES // SPANS // 2) * 2
TURNS = GSTEPS // SPANS // GU
assert TURNS * GU * SPANS == GSTEPS and (TURNS - 1) * GU + 1 == NT and SPAN * SPANS <= NP


def extremes_and_sums(nc, st, layer, pn, sum1, sum2):
    with ExitStack() as ctx:
        def sb(name, shape, dt=FP32):
            return ctx.enter_context(nc.sbuf_tensor(f"{name}{layer}", shape, dt))

        def sem(name):
            return ctx.enter_context(nc.semaphore(f"g{layer}_{name}"))
        idx = sb("gather_idx", [P, GU, TILES_IN], INT32)
        got = sb("gathered", [P, GU, TILES_IN, FEAT])
        spare = sb("spare", [P, 1])
        zeros = sb("spare_zeros", [P, 1])
        pen = sb("pen_rows", [P, 2, 2, 2 * EI], BF16)
        run = sb("running", [P, 2, 2, EI])
        rows = sb("run_rows", [P, 2, TILES_IN, 2, FEAT])
        counts = sb("span_counts", [P, GU, SPAN])
        powers = sb("powers", [P, 2, 2, FEAT])
        ps = st["ps"]
        IN, BACK, SUM = 0, 2, 6
        s_idx, s_scan, s_turn, s_back, s_rows, s_zero = (sem(n) for n in ("idx", "scanned", "turned", "turned_back", "rows", "zeroed"))
        s_pow, s_sum, s_span = (sem(n) for n in ("powers", "tile_summed", "span_copied"))
        s_got = [sem(f"gathered{i}") for i in range(GU)]
        s_pen = [sem(f"pen{i}") for i in range(2)]
        s_out = [sem(f"stored{i}") for i in range(2)]
        s_cnt = [sem(f"counts{i}") for i in range(GU)]

        def first(*xs):
            return all(isinstance(x, int) and x == 0 for x in xs)

        def early(x, n):
            return isinstance(x, int) and x < n

        def steps(eng, body):
            def span(s):
                def turn(t):
                    for u in range(GU):
                        body(s, t, u, s * (TURNS * GU) + t * GU + u)
                turn(0)
                with eng.Fori(1, TURNS - 1) as t:
                    turn(t)
                turn(TURNS - 1)
            span(0)
            with eng.Fori(1, SPANS) as s:
                span(s)

        def has_sum(turn, u):
            return not (isinstance(turn, int) and turn == TURNS - 1 and u > 0)

        def slot_loads(span, turn, u):
            return span * (TURNS if u == 0 else TURNS - 1) + turn + 1

        with nc.Block() as block:
            @block.gpsimd
            def _(pool):
                pool.memset(zeros[:, :], 0.0).then_inc(s_zero, 1)
                pool.wait_ge(s_zero, 1)

                def gather(span, turn, u, step):
                    if not early(step, GU):
                        pool.wait_ge(s_turn, step - GU + 1)
                    pool.wait_ge(st["sig"]["src_in"].sem, 16)
                    pool.tensor_copy(idx[:, u, :], st["src_cols"][:, bass.ds(step * TILES_IN, TILES_IN)]).then_inc(s_idx, 1)
                    pool.wait_ge(s_idx, 2 * step + 1)
                    pool.tensor_tensor(spare[:, :], zeros[:, :], zeros[:, :], ALU.add).then_inc(s_idx, 1)
                    for q in range(TILES_IN):
                        pool.indirect_dma_start(out=got[:, u, q, :], out_offset=None, in_=st["P"],
                                                in_offset=bass.IndirectOffsetOnAxis(ap=idx[:, u, q:q + 1], axis=0)).then_inc(s_got[u], 16)
                steps(pool, gather)

            @block.tensor
            def _(pe):
                def turn_back(step, parity):
                    pe.wait_ge(s_scan, step + 1)
                    if not early(step, 2):
                        pe.wait_ge(s_rows, 2 * (step - 1))
                    for i in range(2):
                        for q in range(TILES_IN):
                            last = pe.transpose(ps[:, BACK + 2 * parity + i, q * P:(q + 1) * P], run[:, parity, i, q * P:(q + 1) * P], st["ident"][:, :])
                    last.then_inc(s_back, 1)

                def work(span, turn, u, step):
                    if has_sum(turn, u):
                        n = span * NT + turn * GU + u
                        pe.wait_ge(s_cnt[u], slot_loads(span, turn, u) * 16)
                        pe.wait_ge(s_pow, n + 1)
                        start = isinstance(turn, int) and turn == 0 and u == 0
                        if start and not first(span):
                            pe.wait_ge(s_span, 2 * span)
                        for i in range(2):
                            last = pe.matmul(ps[:, SUM + i, 0:SPAN], powers[:, u % 2, i, :], counts[:, u, :], start=start,
                                             stop=isinstance(turn, int) and turn == TURNS - 1)
                        last.then_inc(s_sum, 1)
                    pe.wait_ge(s_got[u], (span * TURNS + turn + 1) * 16 * TILES_IN)
                    if not early(step, 2):
                        pe.wait_ge(s_scan, step - 1)
                    for q in range(TILES_IN):
                        last = pe.transpose(ps[:, IN + u % 2, q * P:(q + 1) * P], got[:, u, q, :], st["ident"][:, :])
                    last.then_inc(s_turn, 1)
                    if not early(step, 1):
                        turn_back(step - 1, (u - 1) % 2)
                steps(pe, work)
                turn_back(GSTEPS - 1, 1)

            @block.vector
            def _(dve):
                def scan(span, turn, u, step):
                    half = u // 2
                    if u % 2 == 0:
                        dve.wait_ge(s_pen[half], (span * TURNS + turn + 1) * 16)
                    dve.wait_ge(s_turn, step + 1)
                    if not early(step, 2):
                        dve.wait_ge(s_back, step - 1)
                    for i, op in ((0, ALU.max), (1, ALU.min)):
                        if first(step):
                            start = 0.0
                        else:
                            dve.wait_ge(s_scan, step)
                            start = run[:, (u + 1) % 2, i, EI - 1:EI]
                        last = dve.tensor_tensor_scan(run[:, u % 2, i, :], pen[:, half, i, u % 2 * EI:(u % 2 + 1) * EI],
                                                      ps[:, IN + u % 2, :], start, ALU.add, op)
                    last.then_inc(s_scan, 1)
                steps(dve, scan)

            @block.scalar
            def _(act):
                def work(span, turn, u, step):
                    if has_sum(turn, u):
                        n = span * NT + turn * GU + u
                        if not early(n, 2):
                            act.wait_ge(s_sum, n - 1)
                            if isinstance(turn, int) and turn == 0 and u == 0:
                                act.wait_ge(s_sum, n)
                        tile_of_p = dyn_tile(pn, turn * GU + u)
                        act.copy(powers[:, u % 2, 0, :], tile_of_p)
                        act.activation(powers[:, u % 2, 1, :], tile_of_p, ACT.Square).then_inc(s_pow, 1)
                    elif u == 1:
                        act.wait_ge(s_sum, (span + 1) * NT)
                        for i, out in enumerate((sum1, sum2)):
                            act.copy(out[:, bass.ds(span * SPAN, SPAN)], ps[:, SUM + i, 0:SPAN]).then_inc(s_span, 1)
                    if not early(step, 1):
                        rows_out(step - 1, (u - 1) % GU, (span * TURNS + turn) * (GU // 2) + (u - 1) // 2)

                def rows_out(step, u, stores):
                    act.wait_ge(s_back, step + 1)
                    if not early(step, 2):
                        act.wait_ge(s_out[u % 2], stores * 16)
                    for i in range(2):
                        act.copy(rows[:, u % 2, :, i, :], ps[:, BACK + 2 * (u % 2) + i, :].rearrange("p (q f) -> p q f", f=FEAT)).then_inc(s_rows, 1)
                steps(act, work)
                rows_out(GSTEPS - 1, GU - 1, GSTEPS // 2 - 1)

            @block.sync
            def _(sp):
                def store(step, u):
                    sp.wait_ge(s_rows, 2 * (step + 1))
                    sp.dma_start(st["extremes"][bass.ds(step * EI, EI), :].rearrange("(q p) w -> p q w", p=P),
                                 rows[:, u % 2, :, :, :].rearrange("p q i f -> p q (i f)")).then_inc(s_out[u % 2], 16)

                def work(span, turn, u, step):
                    if has_sum(turn, u):
                        if isinstance(turn, int) and turn == 0:
                            if not first(span):
                                sp.wait_ge(s_sum, span * NT if u == 0 else span * NT - GU + u)
                        else:
                            sp.wait_ge(s_sum, span * NT + turn * GU + u - GU + 1)
                        sp.dma_start(counts[:, u, :], st["C"][bass.ds(turn * GU + u, 1), :, bass.ds(span * SPAN, SPAN)].rearrange("a p n -> p (a n)")).then_inc(s_cnt[u], 16)
                    if u % 2 == 0:
                        if not early(step, GU):
                            sp.wait_ge(s_scan, step - GU + 2)
                        sp.dma_start(pen[:, u // 2, :, :], st["pens"][:, bass.ds(step * EI, 2 * EI)].unsqueeze(0).to_broadcast((P, 2, 2 * EI))).then_inc(s_pen[u // 2], 16)
                    if not early(step, LATE):
                        store(step - LATE, (u - LATE) % GU)
                LATE = 2
                steps(sp, work)
                for u in range(GU - LATE, GU):
                    store(GSTEPS - GU + u, u)
                for i in range(2):
                    sp.wait_ge(s_out[i], 16 * GSTEPS // 2)


def extremes_of_nodes(nc, st, layer, mx, mn):
    sig = st["sig"]
    HB = 5
    with nc.sbuf_tensor(f"end_rows{layer}", [P, NT, 2, FEAT], FP32) as rows, nc.semaphore(f"e{layer}_rows") as s_rows:
        turned, copied, fixed = sig["turned"], sig["out"], sig["shared"]
        with nc.Block() as block:
            @block.gpsimd
            def _(pool):
                for t in range(NT):
                    pool.indirect_dma_start(out=rows[:, t, :, :].rearrange("p i f -> p (i f)"), out_offset=None, in_=st["extremes"],
                                            in_offset=bass.IndirectOffsetOnAxis(ap=st["last_edge"][:, t:t + 1], axis=0)).then_inc(s_rows, 16)

            @block.vector
            def _(dve):
                dve.wait_ge(s_rows, 16 * NT)
                for i, op in enumerate((ALU.add, ALU.subtract)):
                    dve.tensor_tensor(rows[:, :, i, :], rows[:, :, i, :], st["no_edge"][:, :].unsqueeze(2).to_broadcast((P, NT, FEAT)), op).then_inc(fixed.sem, 1)

            @block.tensor
            def _(pe):
                n = 0
                for i in range(2):
                    pe.wait_ge(fixed.sem, fixed.at(i + 1))
                    for b in range(-(-NT // 4)):
                        if n >= 8:
                            pe.wait_ge(copied.sem, copied.at(n - 7))
                        for q in range(min(4, NT - 4 * b)):
                            last = pe.transpose(st["ps"][:, n % 8, q * P:(q + 1) * P], rows[:, 4 * b + q, i, :], st["ident"][:, :])
                        last.then_inc(turned.sem, 1)
                        n += 1

            @block.scalar
            def _(act):
                n = 0
                for out in (mx, mn):
                    for b in range(-(-NT // 4)):
                        w = min(4, NT - 4 * b) * P
                        act.wait_ge(turned.sem, turned.at(n + 1))
                        act.copy(out[:, 4 * b * P:4 * b * P + w], st["ps"][:, n % 8, 0:w]).then_inc(copied.sem, 1)
                        n += 1
        turned.passed(2 * -(-NT // 4))
        copied.passed(2 * -(-NT // 4))
        fixed.passed(2)


def principal_layer(nc, io, st, layer, h, ht):
    sig = st["sig"]
    with ExitStack() as ctx:
        def sb(name, shape, dt=FP32):
            return ctx.enter_context(nc.sbuf_tensor(f"{name}{layer}", shape, dt))
        wt = sb("layer_w", [P, WB * P])
        vecs = sb("layer_vecs", [P, 5])
        lnrow = sb("layer_rows", [P, 2, P])
        load_layer(nc, io, st, layer, wt, vecs, lnrow)

        def w(i):
            return wt[:, i * P:(i + 1) * P]
        pt = sb("p_t", [P, NP])
        std = sb("std_t", [P, NP])
        var = sb("var_t", [P, NP])
        with nc.sbuf_tensor(f"p_n{layer}", [P, NP], FP32) as pn:
            linear(nc, st, [(w(0), ht, P)], pt)
            flip(nc, st, pt, pn)
            with nc.Block() as block:
                @block.sync
                def _(sp):
                    sp.dma_start(st["P"].rearrange("(t p) f -> p t f", p=P), over_features(pn)).then_inc(sig["params"].sem, 16)
                    sp.wait_ge(sig["params"].sem, sig["params"].at(16))
            sig["params"].passed(16)
            def clear_rest(dve, link):
                for sums in (std, var):
                    link(dve.memset(sums[:, SPAN * SPANS:NP], 0.0))
            on_vector(nc, st, clear_rest)
            extremes_and_sums(nc, st, layer, pn, std, var)
        mx = sb("max_t", [P, NP])
        mn = sb("min_t", [P, NP])
        extremes_of_nodes(nc, st, layer, mx, mn)
        ready, back = sig["to_act"], sig["from_act"]
        qt = st["norm_work"]
        linear(nc, st, [(w(1), ht, P)], qt, bias=vecs[:, 0:1])
        with nc.sbuf_tensor(f"square{layer}", [P, NP], FP32) as sq:
            with nc.Block() as block:
                @block.vector
                def _(dve):
                    link = Steps(dve, sig["dve"])
                    recip = st["recip_deg"]
                    link(dve.tensor_tensor(std[:, :], std[:, :], pt[:, :], ALU.add))
                    link(dve.tensor_tensor(std[:, :], std[:, :], recip[:, :], ALU.mult))
                    link(dve.tensor_tensor(std[:, :], std[:, :], std[:, :], ALU.mult))
                    link(dve.tensor_tensor(sq[:, :], pt[:, :], pt[:, :], ALU.mult))
                    link(dve.tensor_tensor(var[:, :], var[:, :], sq[:, :], ALU.add))
                    link(dve.tensor_tensor(var[:, :], var[:, :], recip[:, :], ALU.mult))
                    link(dve.tensor_tensor(var[:, :], var[:, :], std[:, :], ALU.subtract))
                    link(dve.tensor_scalar(var[:, :], var[:, :], 0.0, None, ALU.max))
                    dve.tensor_scalar(sq[:, :], var[:, :], 1e-30, None, ALU.add).then_inc(ready.sem, 1)
                    link(dve.tensor_tensor(mx[:, :], mx[:, :], pt[:, :], ALU.max))
                    link(dve.tensor_tensor(mx[:, :], mx[:, :], qt[:, :], ALU.add))
                    link(dve.tensor_tensor(mn[:, :], mn[:, :], pt[:, :], ALU.min))
                    link(dve.tensor_tensor(mn[:, :], mn[:, :], qt[:, :], ALU.add))
                    link.done()

                @block.scalar
                def _(act):
                    act.wait_ge(ready.sem, ready.at(1))
                    act.wait_ge(sig["dve"].sem, sig["dve"].base)
                    act.sqrt(std[:, :], sq[:, :]).then_inc(back.sem, 1)
            ready.passed(1)
            back.passed(1)
            aggs = (mx, mn, std, var)
            u, scaled = sq, pt
            linear(nc, st, [(w(2), ht, P)] + [(w(3 + i), a, P) for i, a in enumerate(aggs)], u, bias=vecs[:, 1:2])
            for s, scaler in enumerate((st["amplify"], st["attenuate"])):
                linear(nc, st, [(w(7 + 4 * s + i), a, P) for i, a in enumerate(aggs)], scaled)

                def add_scaled(dve, link):
                    link(dve.tensor_tensor(scaled[:, :], scaled[:, :], scaler[:, :], ALU.mult))
                    link(dve.tensor_tensor(u[:, :], u[:, :], scaled[:, :], ALU.add))
                on_vector(nc, st, add_scaled)
            on_vector(nc, st, lambda dve, link: link(dve.tensor_scalar(u[:, :], u[:, :], (1.0 / N_NODES) ** 0.5, None, ALU.mult)))
            norm_nodes(nc, st, u, vecs[:, 2:3], vecs[:, 3:4])
            mixed = scaled
            linear(nc, st, [(w(WB - 1), u, P)], mixed, bias=vecs[:, 4:5])

            def residual(dve, link):
                link(dve.scalar_tensor_tensor(mixed[:, :], mixed[:, :], 0.01, mixed[:, :], ALU.mult, ALU.max))
                link(dve.tensor_tensor(ht[:, :], ht[:, :], mixed[:, :], ALU.add))
            on_vector(nc, st, residual)
            flip(nc, st, ht, h)
            norm_rows(nc, st, h, lnrow[:, 0, :], lnrow[:, 1, :])
            with nc.Block() as block:
                @block.vector
                def _(dve):
                    link = Steps(dve, sig["dve"])
                    dve.tensor_scalar(u[:, :], h[:, :], 0.0, None, ALU.min).then_inc(ready.sem, 1)
                    dve.wait_ge(back.sem, back.at(1))
                    link(dve.tensor_scalar(u[:, :], u[:, :], -1.0, None, ALU.add))
                    link(dve.scalar_tensor_tensor(h[:, :], h[:, :], 0.0, u[:, :], ALU.max, ALU.add))
                    link.done()

                @block.scalar
                def _(act):
                    act.wait_ge(ready.sem, ready.at(1))
                    act.activation(u[:, :], u[:, :], ACT.Exp).then_inc(back.sem, 1)
            ready.passed(1)
            back.passed(1)
            if layer < LAYERS - 1:
                flip(nc, st, h, ht)


RING = 3


def program(nc, io, out, kind="Internal"):
    st = {}

    def dram(name, shape, dt=FP32):
        st[name] = nc.dram_tensor(name, shape, dt, kind=kind).ap()
    dram("win_ends", [2 * P], INT32)
    dram("node_ends", [P + NP])
    dram("pens", [2, EP], BF16)
    dram("C", [NT, P, NP])
    dram("AT", [NT, P, NP])
    dram("P", [NP, FEAT])
    dram("extremes", [EP, 2 * FEAT])
    with ExitStack() as ctx:
        def sb(name, shape, dt=FP32):
            st[name] = ctx.enter_context(nc.sbuf_tensor(name, shape, dt))
        sb("ident", [P, P])
        sb("cell_iota", [P, CELLS], FP16)
        sb("last_edge", [P, NT], INT32)
        sb("ends_row", [1, NWIN + 2], INT32)
        sb("big_col", [P, 1])
        with nc.sbuf_tensor("steps", [P, 3, SG * P], FP32) as steps:
            st["steps"] = steps
            windows_and_steps(nc, io, st)
            build_adjacency(nc, st)
        for name, shape in (("x", [P, NP]), ("norm_work", [P, NP]), ("norm_mean", [P, NT]), ("norm_var", [P, NT]), ("node_cols", [P, 5])):
            sb(name, shape)
        sb("stat", [P, RING, P])
        st["ps"] = ctx.enter_context(nc.psum_tensor("ps", [P, 8, 512], FP32))
        sig = st["sig"] = {k: Signal(ctx.enter_context(nc.semaphore("sig_" + k))) for k in
                           ("used", "picked", "out", "turned", "to_act", "from_act", "params", "dve", "act", "pooled", "shared", "scaled", "src_in")}
        sig["loaded"] = [Signal(ctx.enter_context(nc.semaphore(f"sig_loaded{i}"))) for i in range(RING)]
        on_vector(nc, st, lambda dve, link: link(dve.memset(st["big_col"][:, :], BIG)))
        with nc.sbuf_tensor("buf_a", [P, NP], FP32) as a, nc.sbuf_tensor("buf_b", [P, NP], FP32) as b, nc.sbuf_tensor("ring", [P, RING, NP], FP32) as ring:
            st["buf_a"], st["buf_b"], st["ring"] = a, b, ring
            with nc.sbuf_tensor("buf_c", [P, NP], FP32) as c:
                st["buf_c"] = c
                light_hops(nc, io, st)
            attention(nc, io, st)
            isomorphism(nc, io, st)
        for name, shape in (("recip_deg", [P, NP]), ("amplify", [P, NP]), ("attenuate", [P, NP]), ("no_edge", [P, NT]), ("h", [P, NP]), ("h_t", [P, NP])):
            sb(name, shape)
        st["src_cols"] = ctx.enter_context(nc.sbuf_tensor("src_cols", [P, ET], INT32))
        degrees(nc, st)
        h, ht, x = st["h"], st["h_t"], st["x"]
        with nc.Block() as block:
            @block.sync
            def _(sp):
                with nc.allow_non_contiguous_dma(reason="each edge tile's indices become a column"):
                    sp.dma_start(st["src_cols"][:, :], io["src_cols"]).then_inc(sig["src_in"].sem, 16)
                sp.wait_ge(sig["src_in"].sem, 16)
        flip(nc, st, x, ht)
        for layer in range(LAYERS):
            principal_layer(nc, io, st, layer, h, ht)
        on_vector(nc, st, lambda dve, link: link(dve.tensor_tensor(x[:, :], x[:, :], h[:, :], ALU.add)))
        norm_rows(nc, st, x)
        with nc.Block() as block:
            @block.sync
            def _(sp):
                full = N_NODES // P
                sp.dma_start(out[0:full * P, :].rearrange("(t p) f -> p t f", p=P), over_features(x)[:, 0:full, :]).then_inc(sig["params"].sem, 16)
                sp.dma_start(out[full * P:N_NODES, :], x[0:N_NODES - full * P, full * P:NP]).then_inc(sig["params"].sem, 16)
                sp.wait_ge(sig["params"].sem, sig["params"].at(32))


_PARAMS = ["L1_gnn_W", "L1_gnn_b", "L1_gnn_att_src", "L1_gnn_att_dst", "L2_gnn_W1", "L2_gnn_b1", "L2_gnn_gamma", "L2_gnn_beta",
           "L2_gnn_W2", "L2_gnn_b2", "L3_gnn_Mw", "L3_gnn_Mb", "L3_gnn_Uw", "L3_gnn_Ub", "L3_gnn_bn_g", "L3_gnn_bn_b",
           "L3_gnn_mix_w", "L3_gnn_mix_b", "L3_gnn_ln_g", "L3_gnn_ln_b"]


def layouts(inputs):
    import numpy as np
    pad = EP - N_EDGES
    src = np.concatenate([np.asarray(inputs["src"]), np.zeros(pad, np.int32)])
    dst = np.concatenate([np.asarray(inputs["dst"]), np.full(pad, NP, np.int32)])
    weight = np.concatenate([np.asarray(inputs["edge_weight"]), np.zeros(pad, np.float32)])
    x = np.concatenate([np.asarray(inputs["x"]), np.zeros((NP - N_NODES, FEAT), np.float32)])
    arrays = {
        "x_pad": x,
        "dst_pad": np.concatenate([np.full(1, -1, np.int32), dst]),
        "dst_last": np.ascontiguousarray(dst.reshape(ET, P)[:, P - 1:].reshape(1, ET)),
        "dst_tiles": dst.reshape(ET, P),
        "src_tiles": src.reshape(ET, P),
        "src_cols": np.ascontiguousarray(src.reshape(ET, P).T),
        "wgt_tiles": weight.reshape(ET, P),
    }
    for name in _PARAMS:
        arrays[name] = np.ascontiguousarray(inputs[name])
    return arrays


def kernel(**inputs):
    import concourse.bacc as _bacc
    from concourse.bass_utils import run_bass_kernel_spmd as _run

    nc = _bacc.Bacc("TRN2", target_bir_lowering=False, num_devices=1)
    arrays = layouts(inputs)
    io = {name: nc.dram_tensor("in_" + name, list(a.shape), mybir.dt.from_np(a.dtype), kind="ExternalInput").ap() for name, a in arrays.items()}
    out = nc.dram_tensor("out", [N_NODES, FEAT], FP32, kind="ExternalOutput").ap()
    program(nc, io, out)
    r = _run(nc, [{"in_" + name: a for name, a in arrays.items()}], core_ids=[0])
    return r.results[0]["out"]
```

```python
import concourse.bass as bass
from concourse import mybir
from contextlib import ExitStack

FP32 = mybir.dt.float32
BF16 = mybir.dt.bfloat16
FP16 = mybir.dt.float16
INT32 = mybir.dt.int32
ALU = mybir.AluOpType
ACT = mybir.ActivationFunctionType
AX = mybir.AxisListType

P = 128
N_NODES = 3125
FEAT = 128
NT = -(-N_NODES // P)
NP = NT * P
N_EDGES = 100000
EI = 512
EP = -(-N_EDGES // EI) * EI
ET = EP // P
WIN = 16
CELLS = WIN * NT
NWIN = NP // WIN
PER = P // WIN
STEPS = N_EDGES // P + NWIN
SG = -(-STEPS // P)
CHUNK = 400
NC = NP // CHUNK
BIG = 1e30


class Chain:

    def __init__(self, eng, sem, base=0):
        self.eng, self.sem, self.n = eng, sem, base

    def __call__(self, ins):
        ins.then_inc(self.sem, 1)
        self.n = self.n + 1
        self.eng.wait_ge(self.sem, self.n)


def windows_and_steps(nc, io, st):
    with ExitStack() as ctx:
        def sb(name, shape, dt):
            return ctx.enter_context(nc.sbuf_tensor(name, shape, dt))

        def sem(name):
            return ctx.enter_context(nc.semaphore(name))

        last_i = sb("last_i", [P, ET], INT32)
        last_f = sb("last_f", [P, ET], FP32)
        junk = sb("cmp_junk", [P, ET], FP32)
        node_p1_i = sb("node_p1_i", [P, NT], INT32)
        node_p1 = sb("node_p1", [P, NT], FP32)
        step_i = sb("step_i", [P, SG], INT32)
        step_f = sb("step_f", [P, SG], FP32)
        win_thr_i = sb("win_thr_i", [P, 2], INT32)
        win_thr = sb("win_thr", [P, 2], FP32)
        win_tile = sb("win_tile", [P, 2], FP32)
        win_end_i = sb("win_end_i", [P, 2], INT32)
        ends_bi = sb("ends_bi", [P, NWIN], INT32)
        ends_b = sb("ends_b", [P, NWIN], FP32)
        node_tile = sb("node_tile", [P, NT], FP32)
        node_tile_i = sb("node_tile_i", [P, NT], INT32)
        node_rows_i = sb("node_rows_i", [P, NT, P], INT32)
        node_rows = sb("node_rows", [P, P], FP32)
        node_cnt = sb("node_cnt", [P, NT], FP32)
        end_f = sb("end_f", [P, NT], FP32)
        win_of = sb("win_of", [P, SG], FP32)
        tile_of = sb("tile_of", [P, SG], FP32)
        tile_of_i = sb("tile_of_i", [P, SG], INT32)
        src_s = sb("src_s", [P, SG, P], INT32)
        dst_s = sb("dst_s", [P, SG, P], INT32)
        wgt_s = sb("wgt_s", [P, SG, P], FP32)
        shi_i = sb("shi_i", [P, SG, P], INT32)
        slo_i = sb("slo_i", [P, SG, P], INT32)
        key_f = sb("key_f", [P, SG, P], FP32)
        slo_f = sb("slo_f", [P, SG, P], FP32)
        tabs = (key_f, slo_f, wgt_s)
        dst_cur = sb("dst_cur", [P, EP // P], INT32)
        dst_prev = sb("dst_prev", [P, EP // P], INT32)
        differs = sb("differs", [P, EP // P], FP32)
        pens = sb("start_pens", [P, 2, EP // P], BF16)
        zero_row = sb("zero_row", [1, P], FP32)
        psT = [ctx.enter_context(nc.psum_tensor(f"psT{i}", [P, 512], FP32)) for i in range(2)]

        s_const = sem("p0_const")
        s_last = sem("p0_last")
        s_dst = sem("p0_dst")
        s_chain = sem("p0_chain")
        s_wend = sem("p0_wend")
        s_wout = sem("p0_wout")
        s_wback = sem("p0_wback")
        s_nidx = sem("p0_nidx")
        s_ngat = sem("p0_ngat")
        s_sidx = sem("p0_sidx")
        s_sgat = sem("p0_sgat")
        s_end = sem("p0_end")
        s_eout = sem("p0_eout")
        s_pen = sem("p0_pen")
        s_pout = sem("p0_pout")
        s_tabs = sem("p0_tabs")
        s_tr = sem("p0_tr")
        s_ev = sem("p0_ev")
        s_zout = sem("p0_zero_out")

        with nc.Block() as block:
            @block.sync
            def _(sp):
                sp.dma_start(last_i[:, :], io["dst_last"].to_broadcast((P, ET))).then_inc(s_last, 16)
                sp.dma_start(dst_cur[:, :], io["dst_pad"][1:EP + 1].rearrange("(p c) -> p c", p=P)).then_inc(s_dst, 16)
                sp.dma_start(dst_prev[:, :], io["dst_pad"][0:EP].rearrange("(p c) -> p c", p=P)).then_inc(s_dst, 16)
                sp.wait_ge(s_wend, 1)
                with nc.allow_non_contiguous_dma(reason="256 words"):
                    sp.dma_start(st["win_ends"][0:2 * P].rearrange("(j p) -> p j", p=P), win_end_i[:, :]).then_inc(s_wout, 16)
                sp.wait_ge(s_wout, 16)
                sp.dma_start(ends_bi[:, :], st["win_ends"][0:NWIN].rearrange("(a n) -> a n", a=1).to_broadcast((P, NWIN))).then_inc(s_wback, 16)
                sp.dma_start(st["ends_row"][0:1, 1:NWIN + 1], st["win_ends"][0:NWIN].rearrange("(a n) -> a n", a=1)).then_inc(s_wback, 16)
                sp.wait_ge(s_pen, 2)
                for i in range(2):
                    sp.dma_start(st["pens"][i, :].rearrange("(p c) -> p c", p=P), pens[:, i, :]).then_inc(s_pout, 16)
                sp.wait_ge(s_end, 1)
                with nc.allow_non_contiguous_dma(reason="3200 words"):
                    sp.dma_start(st["node_ends"][P:P + NP].rearrange("(g p) -> p g", p=P), end_f[:, :]).then_inc(s_eout, 16)
                sp.wait_ge(s_eout, 16)
                sp.wait_ge(s_pout, 32)
                sp.wait_ge(s_wback, 32)

            @block.gpsimd
            def _(pool):
                pool.iota(node_p1_i[:, :], pattern=[[P, NT]], base=1, channel_multiplier=1).then_inc(s_const, 1)
                pool.iota(step_i[:, :], pattern=[[P, SG]], base=0, channel_multiplier=1).then_inc(s_const, 1)
                pool.iota(win_thr_i[:, :], pattern=[[P * WIN, 2]], base=WIN, channel_multiplier=WIN).then_inc(s_const, 1)
                pool.memset(st["ident"][:, :], 0.0).then_inc(s_const, 1)
                pool.wait_ge(s_const, 4)
                pool.affine_select(out=st["ident"][:, :], in_=st["ident"][:, :], compare_op=ALU.not_equal, fill=1.0,
                                   base=0, pattern=[[-1, P]], channel_multiplier=1).then_inc(s_const, 1)
                pool.iota(st["cell_iota"][:, :], pattern=[[1, CELLS]], base=0, channel_multiplier=0,
                          allow_small_or_imprecise_dtypes=True).then_inc(s_const, 1)
                pool.memset(st["ends_row"][0:1, NWIN + 1:NWIN + 2], 0).then_inc(s_const, 1)
                pool.memset(zero_row[:, :], 0.0).then_inc(s_const, 1)
                pool.wait_ge(s_nidx, 1)
                for g in range(NT):
                    pool.indirect_dma_start(out=node_rows_i[:, g, :], out_offset=None, in_=io["dst_tiles"],
                                            in_offset=bass.IndirectOffsetOnAxis(ap=node_tile_i[:, g:g + 1], axis=0)).then_inc(s_ngat, 16)
                pool.wait_ge(s_sidx, 1)
                for g in range(SG):
                    for table, rows in ((io["src_tiles"], src_s), (io["dst_tiles"], dst_s), (io["wgt_tiles"], wgt_s)):
                        pool.indirect_dma_start(out=rows[:, g, :], out_offset=None, in_=table,
                                                in_offset=bass.IndirectOffsetOnAxis(ap=tile_of_i[:, g:g + 1], axis=0)).then_inc(s_sgat, 16)

            @block.vector
            def _(dve):
                link = Chain(dve, s_chain)
                dve.wait_ge(s_const, 7)
                link(dve.tensor_copy(node_p1[:, :], node_p1_i[:, :]))
                link(dve.tensor_copy(step_f[:, :], step_i[:, :]))
                link(dve.tensor_copy(win_thr[:, :], win_thr_i[:, :]))
                dve.wait_ge(s_last, 16)
                link(dve.tensor_copy(last_f[:, :], last_i[:, :]))
                for j in range(2):
                    link(dve.tensor_scalar(junk[:, :], last_f[:, :], win_thr[:, j:j + 1], 0.0, ALU.is_lt, ALU.add,
                                           accum_out=win_tile[:, j:j + 1]))
                dve.scalar_tensor_tensor(win_end_i[:, :], win_thr[:, :], 1.0 / WIN, win_tile[:, :], ALU.mult, ALU.add).then_inc(s_wend, 1)
                for g in range(NT):
                    link(dve.tensor_scalar(junk[:, :], last_f[:, :], node_p1[:, g:g + 1], 0.0, ALU.is_lt, ALU.add,
                                           accum_out=node_tile[:, g:g + 1]))
                dve.tensor_copy(node_tile_i[:, :], node_tile[:, :]).then_inc(s_nidx, 1)
                dve.wait_ge(s_wback, 32)
                link(dve.tensor_copy(ends_b[:, :], ends_bi[:, :]))
                for g in range(SG):
                    link(dve.tensor_scalar(junk[:, 0:NWIN], ends_b[:, :], step_f[:, g:g + 1], 0.0, ALU.is_le, ALU.add,
                                           accum_out=win_of[:, g:g + 1]))
                link(dve.tensor_tensor(tile_of[:, :], step_f[:, :], win_of[:, :], ALU.subtract))
                dve.tensor_scalar(tile_of_i[:, :], tile_of[:, :], float(ET - 1), None, ALU.min).then_inc(s_sidx, 1)
                dve.wait_ge(s_dst, 32)
                link(dve.tensor_tensor(differs[:, :], dst_cur[:, :], dst_prev[:, :], ALU.not_equal))
                dve.tensor_scalar(pens[:, 0, :], differs[:, :], -BIG, None, ALU.mult).then_inc(s_pen, 1)
                dve.tensor_scalar(pens[:, 1, :], differs[:, :], BIG, None, ALU.mult).then_inc(s_pen, 1)
                for g in range(NT):
                    dve.wait_ge(s_ngat, 16 * NT)
                    link(dve.tensor_copy(node_rows[:, :], node_rows_i[:, g, :]))
                    link(dve.tensor_scalar(junk[:, 0:P], node_rows[:, :], node_p1[:, g:g + 1], 0.0, ALU.is_lt, ALU.add,
                                           accum_out=node_cnt[:, g:g + 1]))
                dve.scalar_tensor_tensor(end_f[:, :], node_tile[:, :], float(P), node_cnt[:, :], ALU.mult, ALU.add).then_inc(s_end, 1)
                dve.wait_ge(s_sgat, 16 * 3 * SG)
                link(dve.tensor_scalar(shi_i[:, :, :], src_s[:, :, :], 7, None, ALU.arith_shift_right))
                link(dve.tensor_scalar(slo_i[:, :, :], src_s[:, :, :], P - 1, None, ALU.bitwise_and))
                link(dve.tensor_copy(slo_f[:, :, :], slo_i[:, :, :]))
                link(dve.scalar_tensor_tensor(key_f[:, :, :], dst_s[:, :, :], float(NT), shi_i[:, :, :], ALU.mult, ALU.add))
                link(dve.tensor_scalar(win_of[:, :], win_of[:, :], -float(CELLS), None, ALU.mult))
                for g in range(SG):
                    last = dve.tensor_scalar(key_f[:, g, :], key_f[:, g, :], win_of[:, g:g + 1], None, ALU.add)
                last.then_inc(s_tabs, 1)

            @block.tensor
            def _(pe):
                pe.wait_ge(s_const, 5)
                pe.wait_ge(s_tabs, 1)
                for n in range(3 * SG // 4):
                    if n >= 2:
                        pe.wait_ge(s_ev, n - 1)
                    for q in range(4):
                        i, g = divmod(4 * n + q, SG)
                        last = pe.transpose(psT[n % 2][:, q * P:(q + 1) * P], tabs[i][:, g, :], st["ident"][:, :])
                    last.then_inc(s_tr, 1)

            @block.scalar
            def _(act):
                act.wait_ge(s_const, 8)
                act.dma_start(st["node_ends"][0:P].rearrange("(a n) -> a n", a=1), zero_row[:, :]).then_inc(s_zout, 16)
                for n in range(3 * SG // 4):
                    i, g = divmod(4 * n, SG)
                    act.wait_ge(s_tr, n + 1)
                    act.copy(st["steps"][:, i, g * P:(g + 4) * P], psT[n % 2][:, :]).then_inc(s_ev, 1)
                act.wait_ge(s_zout, 16)


def build_adjacency(nc, st):
    RING = 8
    with ExitStack() as ctx:
        def sb(name, shape, dt):
            return ctx.enter_context(nc.sbuf_tensor(name, shape, dt))

        def sem(name):
            return ctx.enter_context(nc.semaphore(name))

        cells_c = sb("cells_c", [P, RING, CELLS], BF16)
        cells_a = sb("cells_a", [P, RING, CELLS], FP32)
        rows_c = sb("rows_c", [P, RING, P], BF16)
        rows_a = sb("rows_a", [P, RING, P], FP32)
        now = sb("step_now", [P, 3, RING], FP32)
        now_spare = sb("ahead_spare", [P, 1], FP32)
        now_spare2 = sb("ahead_spare2", [P, 1], FP32)
        stage_c = sb("stage_c", [P, 2, NT, P], FP32)
        stage_a = sb("stage_a", [P, NT, P], FP32)
        stage_t = sb("stage_t", [P, 2, NP], FP32)
        zero_b = sb("zero_b", [P, P], BF16)
        iota_f = sb("cell_iota_f", [P, CELLS], FP32)
        ps = ctx.enter_context(nc.psum_tensor("ps_windows", [P, 4 * 512], FP32))
        ps_t = [ctx.enter_context(nc.psum_tensor(f"ps_t{i}", [P, 512], FP32)) for i in range(2)]
        SUMS = 2 * 512
        s_zero = sem("p1_zero")
        s_made = sem("p1_made")
        s_now = sem("p1_columns")
        s_used = sem("p1_used")
        s_win = sem("p1_window_summed")
        s_free = sem("p1_window_copied")
        s_tr = sem("p1_transposed")
        s_trc = sem("p1_transpose_copied")
        s_cout = [sem(f"p1_c_out{i}") for i in range(2)]
        s_tout = [sem(f"p1_t_out{i}") for i in range(2)]
        TB = -(-NT // 4)
        AHEAD = 2

        def over_tiles(eng, body):
            with eng.Fori(0, NT // 2) as half:
                body(half * 2, 0)
                body(half * 2 + 1, 1)
            body(NT - 1, 0)

        with nc.Block() as block:
            @block.vector
            def _(dve):
                dve.memset(zero_b[:, :], 0.0).then_inc(s_zero, 1)
                dve.tensor_copy(iota_f[:, :], st["cell_iota"][:, :]).then_inc(s_zero, 1)
                dve.wait_ge(s_zero, 2)

                HALF = RING // 2

                def columns(turn, part):
                    dve.tensor_copy(now[:, :, part * HALF:(part + 1) * HALF],
                                    st["steps"][:, :, bass.ds(turn * RING + part * HALF, HALF)]).then_inc(s_now, 1)

                def make(slot):
                    def col(i):
                        return now[:, i, slot:slot + 1]
                    dve.tensor_scalar(cells_c[:, slot, :], st["cell_iota"][:, :], col(0), None, ALU.is_equal)
                    dve.tensor_scalar(cells_a[:, slot, :], iota_f[:, :], col(0), None, ALU.is_equal)
                    dve.tensor_scalar(rows_c[:, slot, :], st["cell_iota"][:, 0:P], col(1), None, ALU.is_equal)
                    dve.tensor_scalar(rows_a[:, slot, :], iota_f[:, 0:P], col(1), col(2), ALU.is_equal, ALU.mult).then_inc(s_made, 1)

                def work(turn, slots, first=False):
                    for slot in range(slots):
                        if slot % HALF == 0:
                            dve.wait_ge(s_now, 2 * turn + slot // HALF + 1)
                        if not first:
                            dve.wait_ge(s_used, (turn - 1) * RING + slot + 1)
                        make(slot)
                        if slot == 0:
                            if not first:
                                dve.wait_ge(s_made, turn * RING)
                            columns(turn, 1)
                        elif slot == HALF and slots == RING:
                            dve.wait_ge(s_made, turn * RING + HALF)
                            columns(turn + 1, 0)

                columns(0, 0)
                work(0, RING, True)
                with dve.Fori(1, STEPS // RING) as turn:
                    work(turn, RING)
                work(STEPS // RING, STEPS % RING)

            @block.tensor
            def _(pe):
                half = pe.alloc_register("window_half")
                window = pe.alloc_register("window")
                left = pe.alloc_register("windows_left_in_tile")
                tile_no = pe.alloc_register("tile_no")
                ends_at = pe.alloc_register("window_ends_at")

                def mark(at, start):
                    for off in (0, SUMS):
                        last = pe.matmul(ps[:, bass.ds(at + (off + CELLS), 1)], zero_b[:, :], zero_b[:, 0:1], start=start, stop=not start, skip_group_check=True)
                    return last

                def transposes():
                    t = pe.snap(tile_no)
                    pe.wait_ge(s_free, (t + 1) * PER * 2 + AHEAD)
                    for b in range(TB):
                        pe.wait_ge(s_trc, t * TB + b + 1)
                        for q in range(min(4, NT - 4 * b)):
                            last = pe.transpose(ps_t[b % 2][:, q * P:(q + 1) * P], stage_a[:, 4 * b + q, :], st["ident"][:, :])
                        last.then_inc(s_tr, 1)
                    pe.reg_add(tile_no, tile_no, 1)
                    pe.reg_mov(left, PER)

                def step(k, slot):
                    pe.wait_ge(s_made, k + 1)
                    at = pe.snap(half, min_val=0, max_val=512)
                    pe.matmul(ps[:, bass.ds(at, CELLS)], rows_c[:, slot, :], cells_c[:, slot, :], start=False, stop=False, skip_group_check=True)
                    pe.matmul(ps[:, bass.ds(at + SUMS, CELLS)], rows_a[:, slot, :], cells_a[:, slot, :],
                              start=False, stop=False, skip_group_check=True).then_inc(s_used, 1)
                    with pe.If_eq(ends_at, k + 1):
                        mark(at, False).then_inc(s_win, 1)
                        pe.reg_add(window, window, 1)
                        pe.reg_alu(half, half, 512, ALU.bitwise_xor)
                        pe.reg_add(left, left, -1)
                        with pe.If_eq(left, 0):
                            transposes()
                        w = pe.snap(window, min_val=1, max_val=NWIN)
                        pe.load(ends_at, st["ends_row"][0:1, bass.ds(w + 1, 1)])
                        pe.wait_ge(s_free, w * 2)
                        mark(pe.snap(half, min_val=0, max_val=512), True)

                pe.wait_ge(s_zero, 1)
                pe.reg_mov(half, 0)
                pe.reg_mov(window, 0)
                pe.reg_mov(left, PER)
                pe.reg_mov(tile_no, 0)
                pe.load(ends_at, st["ends_row"][0:1, 1:2])
                mark(pe.snap(half, min_val=0, max_val=512), True)
                with pe.Fori(0, STEPS // RING) as turn:
                    for slot in range(RING):
                        step(turn * RING + slot, slot)
                for k in range(STEPS // RING * RING, STEPS):
                    step(k, k % RING)

            @block.scalar
            def _(act):
                act.copy(now_spare[:, :], st["cell_iota"][:, 0:1]).then_inc(s_free, AHEAD)
                act.copy(now_spare2[:, :], st["cell_iota"][:, 0:1]).then_inc(s_trc, 2)

                def tile(t, parity, first=False):
                    for j in range(PER):
                        w = t * PER + j
                        act.wait_ge(s_win, w + 1)
                        if j == 0 and not first:
                            act.wait_ge(s_cout[parity], ((t - parity) // 2) * 16)
                        for bank, stage in ((0, stage_c[:, parity, :, j * WIN:(j + 1) * WIN]), (2, stage_a[:, :, j * WIN:(j + 1) * WIN])):
                            at = (bank + j % 2) * 512
                            act.copy(stage, ps[:, at:at + CELLS].rearrange("p (d s) -> p s d", s=NT)).then_inc(s_free, 1)
                    if not first:
                        act.wait_ge(s_tout[parity], ((t - parity) // 2) * 16)
                    for b in range(TB):
                        act.wait_ge(s_tr, t * TB + b + 1)
                        n = min(4, NT - 4 * b) * P
                        act.copy(stage_t[:, parity, 4 * b * P:4 * b * P + n], ps_t[b % 2][:, 0:n]).then_inc(s_trc, 1)

                tile(0, 0, True)
                tile(1, 1, True)
                with act.Fori(1, (NT - 1) // 2) as half:
                    tile(half * 2, 0)
                    tile(half * 2 + 1, 1)
                tile(NT - 1, 0)

            @block.sync
            def _(sp):
                def tile(t, parity):
                    sp.wait_ge(s_free, (t + 1) * PER * 2 + AHEAD)
                    sp.dma_start(st["C"][:, :, bass.ds(t * P, P)].rearrange("s p d -> p s d"), stage_c[:, parity, :, :]).then_inc(s_cout[parity], 16)
                    sp.wait_ge(s_trc, (t + 1) * TB + 2)
                    sp.dma_start(st["AT"][bass.ds(t, 1), :, :].rearrange("a p s -> p (a s)"), stage_t[:, parity, :]).then_inc(s_tout[parity], 16)

                over_tiles(sp, tile)
                for i in range(2):
                    sp.wait_ge(s_cout[i], 16 * ((NT + 1 - i) // 2))
                    sp.wait_ge(s_tout[i], 16 * ((NT + 1 - i) // 2))


class Signal:

    def __init__(self, sem):
        self.sem, self.base = sem, 0

    def at(self, n):
        return n + self.base

    def passed(self, n):
        self.base += n


def signal(nc, st, name):
    if name not in st["signals"]:
        st["signals"][name] = Signal(st["keep"].enter_context(nc.semaphore(name)))
    return st["signals"][name]


class Steps(Chain):

    def __init__(self, eng, kept):
        super().__init__(eng, kept.sem, kept.base)
        self.kept = kept

    def done(self):
        self.kept.base = self.n


def in_ring(eng, ring, body, first_turn=0):
    for slot in range(ring):
        body(slot, slot, 0)
    with eng.Fori(1, NT // ring) as turn:
        for slot in range(ring):
            body(turn * ring + slot, slot, turn)
    for t in range(NT // ring * ring, NT):
        body(t, t % ring, NT // ring)


def banks(st):
    return st["ps"][:, :, 0:CHUNK]


def chunk(buf, c, rows=P):
    return buf[0:rows, c * CHUNK:(c + 1) * CHUNK]


def tile(buf, t, width=P, rows=P):
    return buf[0:rows, t * width:(t + 1) * width]


def dyn_tile(buf, t, width=P, rows=P):
    return buf[0:rows, bass.ds(t * width, width)]


def empty_banks(nc, block, st, out, ready, count):
    sig = st["sig"]

    def half(h):
        return (out[:, h * NP // 2:(h + 1) * NP // 2].rearrange("p (c n) -> p c n", n=CHUNK),
                banks(st)[:, h * NC // 2:(h + 1) * NC // 2, :])

    def scalar(act):
        if count:
            act.wait_ge(ready.sem, ready.at(count))
        act.copy(*half(0)).then_inc(sig["out"].sem, 1)

    @block.vector
    def _(dve):
        if count:
            dve.wait_ge(ready.sem, ready.at(count))
        dve.tensor_copy(*half(1)).then_inc(sig["out"].sem, 1)

    return scalar


def spread(nc, st, matrix, xn, out):
    sig, ring, stat = st["sig"], st["ring"], st["stat"]
    loaded, used, picked = sig["loaded"], sig["used"], sig["picked"]
    with nc.Block() as block:
        @block.sync
        def _(sp):
            def load(t, slot, turn):
                if not isinstance(t, int) or t >= RING:
                    sp.wait_ge(used.sem, used.at(t - RING + 1))
                sp.dma_start(ring[:, slot, :], matrix[bass.ds(t, 1), :, :].rearrange("a p n -> p (a n)")).then_inc(loaded[slot].sem, 16)
            in_ring(sp, RING, load)

        @block.tensor
        def _(pe):
            def multiply(t, slot, turn):
                pe.wait_ge(loaded[slot].sem, loaded[slot].at((turn + 1) * 16))
                pe.wait_ge(picked.sem, picked.at(t + 1))
                for c in range(NC):
                    last = pe.matmul(banks(st)[:, c, :], stat[:, slot, :], ring[:, slot, c * CHUNK:(c + 1) * CHUNK],
                                     start=isinstance(t, int) and t == 0, stop=isinstance(t, int) and t == NT - 1)
                last.then_inc(used.sem, 1)
            in_ring(pe, RING, multiply)

        empty = empty_banks(nc, block, st, out, used, NT)

        @block.scalar
        def _(act):
            def pick(t, slot, turn):
                if not isinstance(t, int) or t >= RING:
                    act.wait_ge(used.sem, used.at(t - RING + 1))
                act.copy(stat[:, slot, :], dyn_tile(xn, t)).then_inc(picked.sem, 1)
            in_ring(act, RING, pick)
            empty(act)
    for slot in range(RING):
        loaded[slot].passed(16 * len(range(slot, NT, RING)))
    used.passed(NT)
    picked.passed(NT)
    sig["out"].passed(2)


def flip(nc, st, source, out, beside=None):
    sig, ident = st["sig"], st["ident"]
    turned, copied = sig["turned"], sig["out"]
    nb = -(-NT // 4)
    with nc.Block() as block:
        @block.tensor
        def _(pe):
            for b in range(nb):
                for q in range(min(4, NT - 4 * b)):
                    last = pe.transpose(st["ps"][:, b, q * P:(q + 1) * P], tile(source, 4 * b + q), ident[:, :])
                last.then_inc(turned.sem, 1)

        def copy_bank(eng, copy, b):
            n = min(4, NT - 4 * b) * P
            eng.wait_ge(turned.sem, turned.at(b + 1))
            copy(out[:, 4 * b * P:4 * b * P + n], st["ps"][:, b, 0:n]).then_inc(copied.sem, 1)

        @block.scalar
        def _(act):
            for b in range(0, nb, 2):
                copy_bank(act, act.copy, b)

        @block.vector
        def _(dve):
            if beside:
                link = Steps(dve, sig["dve"])
                beside(dve, link)
                link.done()
            for b in range(1, nb, 2):
                copy_bank(dve, dve.tensor_copy, b)
    turned.passed(nb)
    copied.passed(nb)


def empty_alone(nc, st, out):
    with nc.Block() as block:
        empty = empty_banks(nc, block, st, out, None, 0)

        @block.scalar
        def _(act):
            empty(act)
    st["sig"]["out"].passed(2)


def linear(nc, st, terms, out, bias=None, func=None, rows=P):
    sig = st["sig"]
    multiplied, copied = sig["used"], sig["out"]
    with nc.Block() as block:
        @block.tensor
        def _(pe):
            for c in range(NC):
                for i, (weight, x, k) in enumerate(terms):
                    last = pe.matmul(banks(st)[0:rows, c, :], weight, chunk(x, c, k), start=i == 0, stop=i == len(terms) - 1)
                last.then_inc(multiplied.sem, 1)

        @block.scalar
        def _(act):
            for c in range(NC):
                act.wait_ge(multiplied.sem, multiplied.at(c + 1))
                if bias is None:
                    act.copy(chunk(out, c, rows), banks(st)[0:rows, c, :]).then_inc(copied.sem, 1)
                else:
                    act.activation(chunk(out, c, rows), banks(st)[0:rows, c, :], func or ACT.Identity, bias=bias).then_inc(copied.sem, 1)
    multiplied.passed(NC)
    copied.passed(NC)


def over_features(buf):
    return buf[:, :].rearrange("p (t f) -> p t f", f=FEAT)


def norm_rows(nc, st, x):
    sig, stats, moments, scale, shift = st["sig"], st["norm_stats"], st["norm_moments"], st["norm_scale"], st["norm_shift"]
    ready, rooted, scaled = sig["to_act"], sig["from_act"], sig["scaled"]

    with nc.Block() as block:
        @block.vector
        def _(dve):
            link = Steps(dve, sig["dve"])
            for t in range(NT):
                last = dve.bn_stats(out=stats[:, t, :], in_=tile(x, t))
            link(last)
            for t in range(NT):
                last = dve.bn_aggr(out=moments[:, t, :], in_=stats[:, t, :])
            last.then_inc(ready.sem, 1)
            dve.wait_ge(rooted.sem, rooted.at(1))
            link(dve.reciprocal(scale[:, :], scale[:, :]))
            dve.scalar_tensor_tensor(shift[:, :], moments[:, :, 0], -1.0, scale[:, :], ALU.mult, ALU.mult).then_inc(scaled.sem, 1)
            dve.wait_ge(scaled.sem, scaled.at(1))
            for t in range(1, NT, 2):
                last = dve.tensor_scalar(tile(x, t), tile(x, t), scale[:, t:t + 1], shift[:, t:t + 1], ALU.mult, ALU.add)
            link(last)
            link.done()

        @block.scalar
        def _(act):
            act.wait_ge(ready.sem, ready.at(1))
            act.activation(scale[:, :], moments[:, :, 1], ACT.Sqrt, bias=st["eps_col"][:, 0:1]).then_inc(rooted.sem, 1)
            act.wait_ge(scaled.sem, scaled.at(1))
            for t in range(0, NT, 2):
                act.activation(tile(x, t), tile(x, t), ACT.Identity, bias=shift[:, t:t + 1], scale=scale[:, t:t + 1])
    ready.passed(1)
    rooted.passed(1)
    scaled.passed(1)


def norm_nodes(nc, st, x, gain, shift):
    sig, work, cols = st["sig"], st["norm_work"], st["node_cols"]
    ready, rooted = sig["to_act"], sig["from_act"]
    real = x[:, 0:N_NODES]
    with nc.Block() as block:
        @block.vector
        def _(dve):
            link = Steps(dve, sig["dve"])
            link(dve.tensor_reduce(cols[:, 0:1], real, AX.X, ALU.add))
            link(dve.tensor_scalar(cols[:, 0:1], cols[:, 0:1], 1.0 / N_NODES, None, ALU.mult))
            dve.tensor_scalar(x[:, :], x[:, :], cols[:, 0:1], None, ALU.subtract).then_inc(ready.sem, 1)
            dve.wait_ge(rooted.sem, rooted.at(1))
            dve.tensor_scalar(cols[:, 2:3], cols[:, 1:2], 1.0 / N_NODES, 1e-5, ALU.mult, ALU.add).then_inc(ready.sem, 1)
            dve.wait_ge(rooted.sem, rooted.at(2))
            link(dve.reciprocal(cols[:, 4:5], cols[:, 3:4]))
            link(dve.tensor_scalar(x[:, :], x[:, :], cols[:, 4:5], gain, ALU.mult, ALU.mult))
            link(dve.tensor_scalar(x[:, :], x[:, :], shift, None, ALU.add))
            link.done()

        @block.scalar
        def _(act):
            act.wait_ge(ready.sem, ready.at(1))
            act.activation(work[:, 0:N_NODES], real, ACT.Square, accum_out=cols[:, 1:2]).then_inc(rooted.sem, 1)
            act.wait_ge(ready.sem, ready.at(2))
            act.sqrt(cols[:, 3:4], cols[:, 2:3]).then_inc(rooted.sem, 1)
    ready.passed(2)
    rooted.passed(2)


def on_vector(nc, st, program):
    with nc.Block() as block:
        @block.vector
        def _(dve):
            link = Steps(dve, st["sig"]["dve"])
            program(dve, link)
            link.done()


def light_hops(nc, io, st):
    sig, x, en, et, acc = st["sig"], st["x"], st["buf_a"], st["buf_b"], st["buf_c"]
    with nc.Block() as block:
        @block.sync
        def _(sp):
            sp.dma_start(over_features(x), io["x_pad"].rearrange("(t p) f -> p t f", p=P)).then_inc(sig["params"].sem, 16)
            sp.wait_ge(sig["params"].sem, sig["params"].at(16))
    sig["params"].passed(16)
    for hop in range(3):
        spread(nc, st, st["AT"], x if hop == 0 else en, et)

        def add_hop(dve, link):
            if hop == 0:
                link(dve.tensor_copy(acc[:, :], et[:, :]))
            else:
                link(dve.tensor_tensor(acc[:, :], acc[:, :], et[:, :], ALU.add))
        if hop < 2:
            flip(nc, st, et, en, add_hop)
        else:
            on_vector(nc, st, add_hop)
    flip(nc, st, acc, en)

    def combine(dve, link):
        link(dve.tensor_tensor(en[:, :], en[:, :], x[:, :], ALU.add))
        link(dve.scalar_tensor_tensor(x[:, :], en[:, :], 0.25, x[:, :], ALU.mult, ALU.add))
    on_vector(nc, st, combine)
    norm_rows(nc, st, x)


HEADS = 4
HD = 32


def attention(nc, io, st):
    sig, x, xt = st["sig"], st["x"], st["buf_a"]
    out = st["buf_b"]
    flip(nc, st, x, xt)
    with ExitStack() as ctx:
        def sb(name, shape, dt=FP32):
            return ctx.enter_context(nc.sbuf_tensor(name, shape, dt))
        w = sb("gat_w", [HD, FEAT])
        att = sb("gat_att", [2 * HEADS, HD])
        bias = sb("gat_b", [HD, 1])
        wt = sb("gat_wt", [P, HD])
        att_t = sb("gat_att_t", [HD, 2 * HEADS])
        att_wide = sb("gat_att_wide", [HD, HEADS, P])
        wh = sb("gat_wh", [P, NT * HD])
        a_src = sb("gat_a_src", [P, NT * HEADS])
        a_dst = sb("gat_a_dst", [P, HEADS, NP])
        best = sb("gat_best", [P, HEADS])
        now = sb("gat_best_now", [P, 2, HEADS])
        best_all = sb("gat_best_all", [P, 4])
        bias_up = sb("gat_bias_up", [P, NT * HEADS])
        bias_down = sb("gat_bias_down", [P, NT * HEADS])
        params, turned, copied, used, ready, back = (sig[k] for k in ("params", "turned", "out", "used", "to_act", "from_act"))
        with nc.Block() as block:
            @block.sync
            def _(sp):
                sp.dma_start(w[:, :], io["L1_gnn_W"]).then_inc(params.sem, 16)
                sp.dma_start(att[0:HEADS, :], io["L1_gnn_att_src"]).then_inc(params.sem, 16)
                sp.dma_start(att[HEADS:2 * HEADS, :], io["L1_gnn_att_dst"]).then_inc(params.sem, 16)
                sp.dma_start(bias[:, :], io["L1_gnn_b"].rearrange("(p a) -> p a", a=1)).then_inc(params.sem, 16)

            @block.tensor
            def _(pe):
                pe.wait_ge(params.sem, params.at(64))
                pe.transpose(st["ps"][0:P, 0, 0:HD], w[:, :], st["ident"][0:HD, 0:HD]).then_inc(turned.sem, 1)
                pe.transpose(st["ps"][0:HD, 1, 0:2 * HEADS], att[:, :], st["ident"][0:2 * HEADS, 0:2 * HEADS]).then_inc(turned.sem, 1)

            @block.vector
            def _(dve):
                link = Steps(dve, sig["dve"])
                dve.wait_ge(turned.sem, turned.at(2))
                link(dve.tensor_copy(wt[:, :], st["ps"][0:P, 0, 0:HD]))
                link(dve.tensor_copy(att_t[:, :], st["ps"][0:HD, 1, 0:2 * HEADS]))
                link(dve.tensor_copy(att_wide[:, :, :], att_t[:, HEADS:2 * HEADS].unsqueeze(2).to_broadcast((HD, HEADS, P))))
                link.done()
        params.passed(64)
        turned.passed(2)
        with nc.sbuf_tensor("gat_wh_t", [HD, NP], FP32) as wh_t:
            linear(nc, st, [(wt[:, :], xt, P)], wh_t, bias=bias[:, 0:1], rows=HD)
            with nc.Block() as block:
                @block.tensor
                def _(pe):
                    for t in range(NT):
                        pe.transpose(st["ps"][:, t // 16, t % 16 * HD:(t % 16 + 1) * HD], tile(wh_t, t, rows=HD), st["ident"][0:HD, 0:HD])
                        last = pe.matmul(st["ps"][:, 2, t * HEADS:(t + 1) * HEADS], tile(wh_t, t, rows=HD), att_t[:, 0:HEADS], start=True, stop=True)
                    last.then_inc(turned.sem, 1)
                    for n in range(HEADS * NC):
                        h, c = divmod(n, NC)
                        if n >= 4:
                            pe.wait_ge(copied.sem, copied.at(n - 3))
                        pe.matmul(st["ps"][:, 4 + n % 4, 0:CHUNK], att_wide[:, h, :], chunk(wh_t, c, HD), start=True, stop=True).then_inc(used.sem, 1)

                @block.scalar
                def _(act):
                    for n in range(HEADS * NC):
                        h, c = divmod(n, NC)
                        act.wait_ge(used.sem, used.at(n + 1))
                        act.copy(a_dst[:, h, c * CHUNK:(c + 1) * CHUNK], st["ps"][:, 4 + n % 4, 0:CHUNK]).then_inc(copied.sem, 1)

                @block.vector
                def _(dve):
                    link = Steps(dve, sig["dve"])
                    dve.wait_ge(turned.sem, turned.at(1))
                    link(dve.tensor_copy(wh[:, 0:16 * HD], st["ps"][:, 0, :]))
                    link(dve.tensor_copy(wh[:, 16 * HD:NT * HD], st["ps"][:, 1, 0:(NT - 16) * HD]))
                    link(dve.tensor_copy(a_src[:, :], st["ps"][:, 2, 0:NT * HEADS]))
                    link.done()
            turned.passed(1)
            used.passed(HEADS * NC)
            copied.passed(HEADS * NC)

        R = 2
        loaded, made, seen = sig["loaded"], sig["picked"], sig["used"]
        with nc.sbuf_tensor("gat_pen", [P, R, NP], FP32) as pen, nc.sbuf_tensor("gat_best_junk", [P, HEADS, NP], BF16) as junk, nc.sbuf_tensor("gat_carrier", [P, 1], FP32) as carrier:
            ring = st["ring"]
            with nc.Block() as block:
                @block.sync
                def _(sp):
                    def load(t, slot, turn):
                        if not isinstance(t, int) or t >= R:
                            sp.wait_ge(made.sem, made.at(t - R + 1))
                        sp.dma_start(ring[:, slot, :], st["C"][bass.ds(t, 1), :, :].rearrange("a p n -> p (a n)")).then_inc(loaded[slot].sem, 16)
                    in_ring(sp, R, load)

                @block.scalar
                def _(act):
                    def penalise(t, slot, turn):
                        act.wait_ge(loaded[slot].sem, loaded[slot].at((turn + 1) * 16))
                        if not isinstance(t, int) or t >= R:
                            act.wait_ge(seen.sem, seen.at((t - R + 1) * HEADS))
                        act.activation(pen[:, slot, :], ring[:, slot, :], ACT.Relu, bias=st["big_col"][:, 0:1], scale=-BIG).then_inc(made.sem, 1)
                    in_ring(act, R, penalise)

                @block.vector
                def _(dve):
                    def add_source(t, slot):
                        dve.wait_ge(seen.sem, seen.at(t * HEADS + HEADS))
                        dve.tensor_tensor(now[:, slot, :], now[:, slot, :], dyn_tile(a_src, t, HEADS), ALU.add).then_inc(sig["dve"].sem, 1)

                    def keep_best(t, slot, before):
                        dve.wait_ge(sig["dve"].sem, sig["dve"].at(before))
                        dve.tensor_tensor(best[:, :], now[:, slot, :], now[:, slot, :] if isinstance(t, int) and t == 0 else best[:, :],
                                          ALU.max).then_inc(sig["dve"].sem, 1)

                    def largest(t, slot, turn):
                        dve.wait_ge(made.sem, made.at(t + 1))
                        has_last = not isinstance(t, int) or t >= 1
                        if has_last:
                            dve.wait_ge(seen.sem, seen.at(t * HEADS))
                            dve.wait_ge(sig["dve"].sem, sig["dve"].at(3 * t - 2))
                        dve.memset(carrier[:, :], 0.0).then_inc(sig["dve"].sem, 1)
                        for h in range(HEADS):
                            dve.tensor_tensor_reduce(out=junk[:, h, :], in0=a_dst[:, h, :], in1=pen[:, slot, :], scale=1.0, scalar=-3e38,
                                                            op0=ALU.subtract, op1=ALU.max, accum_out=now[:, slot, h:h + 1]).then_inc(seen.sem, 1)
                            if has_last and h == 0:
                                add_source(t - 1, 1 - slot)
                            elif has_last and h == 1:
                                keep_best(t - 1, 1 - slot, 3 * t)
                    in_ring(dve, R, largest)
                    add_source(NT - 1, (NT - 1) % R)
                    keep_best(NT - 1, (NT - 1) % R, 3 * NT - 1)
            for slot in range(R):
                loaded[slot].passed(16 * len(range(slot, NT, R)))
            made.passed(NT)
            seen.passed(NT * HEADS)
            sig["dve"].passed(3 * NT)

        pooled = sig["pooled"]
        with nc.Block() as block:
            @block.vector
            def _(dve):
                link = Steps(dve, sig["dve"])
                dve.tensor_reduce(best_all[:, 0:1], best[:, :], AX.X, ALU.max).then_inc(ready.sem, 1)
                dve.wait_ge(pooled.sem, pooled.at(1))
                link(dve.tensor_scalar(best_all[:, 2:3], best_all[:, 1:2], 0.2, None, ALU.mult))
                link(dve.tensor_tensor(best_all[:, 3:4], best_all[:, 1:2], best_all[:, 2:3], ALU.max))
                link(dve.tensor_scalar(bias_up[:, :], a_src[:, :], best_all[:, 3:4], None, ALU.subtract))
                link(dve.tensor_scalar(bias_down[:, :], a_src[:, :], 0.2, best_all[:, 3:4], ALU.mult, ALU.subtract))
                link.done()

            @block.gpsimd
            def _(pool):
                pool.wait_ge(ready.sem, ready.at(1))
                pool.partition_all_reduce(best_all[:, 1:2], best_all[:, 0:1], P, bass.bass_isa.ReduceOp.max).then_inc(pooled.sem, 1)
        ready.passed(1)
        pooled.passed(1)

        R = 3
        down = (xt, st["norm_work"])
        with (nc.sbuf_tensor("gat_exp", [P, 2, NP], FP32) as expd,
              nc.sbuf_tensor("gat_share", [P, 2, NP], FP32) as share, nc.sbuf_tensor("gat_den", [P, 2, 2], FP32) as den,
              nc.sbuf_tensor("gat_message", [P, 2, HD], FP32) as message):
            ring = st["ring"]
            exped, shared, scaled, spent = sig["from_act"], sig["shared"], sig["scaled"], sig["used"]
            with nc.Block() as block:
                @block.sync
                def _(sp):
                    def load(t, slot, turn):
                        if not isinstance(t, int) or t >= R:
                            sp.wait_ge(shared.sem, shared.at((t - R + 1) * HEADS))
                        sp.dma_start(ring[:, slot, :], st["C"][bass.ds(t, 1), :, :].rearrange("a p n -> p (a n)")).then_inc(loaded[slot].sem, 16)
                    in_ring(sp, R, load)

                @block.scalar
                def _(act):
                    def exps(t, slot, turn):
                        for h in range(HEADS):
                            n = t * HEADS + h
                            if not isinstance(n, int) or n >= 2:
                                act.wait_ge(shared.sem, shared.at(n - 1))
                            act.activation(expd[:, h % 2, :], a_dst[:, h, :], ACT.Exp, bias=bias_up[:, bass.ds(n, 1)])
                            act.activation(down[h % 2][:, :], a_dst[:, h, :], ACT.Exp, bias=bias_down[:, bass.ds(n, 1)], scale=0.2).then_inc(exped.sem, 1)
                    in_ring(act, R, exps)

                @block.vector
                def _(dve):
                    def guard_sum(n, par):
                        dve.wait_ge(shared.sem, shared.at(n + 1))
                        dve.tensor_scalar(den[:, par, 0:1], den[:, par, 0:1], 1e-16, None, ALU.add).then_inc(sig["dve"].sem, 1)

                    def scale_message(t, n, par, guarded, inverted):
                        dve.wait_ge(sig["dve"].sem, sig["dve"].at(guarded))
                        dve.reciprocal(den[:, par, 1:2], den[:, par, 0:1]).then_inc(sig["dve"].sem, 1)
                        dve.wait_ge(sig["dve"].sem, sig["dve"].at(inverted))
                        dve.tensor_scalar(message[:, par, :], dyn_tile(wh, t, HD), den[:, par, 1:2], None, ALU.mult).then_inc(scaled.sem, 1)

                    def shares(t, slot, turn):
                        dve.wait_ge(loaded[slot].sem, loaded[slot].at((turn + 1) * 16))
                        for h in range(HEADS):
                            n = t * HEADS + h
                            par = h % 2
                            has_last = not isinstance(n, int) or n >= 1
                            if has_last:
                                guard_sum(n - 1, 1 - par)
                            dve.wait_ge(exped.sem, exped.at(n + 1))
                            dve.tensor_tensor(expd[:, par, :], expd[:, par, :], down[par][:, :], ALU.max).then_inc(sig["dve"].sem, 1)
                            if has_last:
                                scale_message(t if h else t - 1, n - 1, 1 - par, 3 * n - 1, 3 * n + 1)
                            else:
                                dve.wait_ge(sig["dve"].sem, sig["dve"].at(1))
                            if not isinstance(n, int) or n >= 2:
                                dve.wait_ge(spent.sem, spent.at(n - 1))
                            dve.scalar_tensor_tensor(share[:, par, :], expd[:, par, :], 1.0, ring[:, slot, :], ALU.min, ALU.mult,
                                                     accum_out=den[:, par, 0:1]).then_inc(shared.sem, 1)
                    in_ring(dve, R, shares)
                    last_head = NT * HEADS - 1
                    guard_sum(last_head, last_head % 2)
                    scale_message(NT - 1, last_head, last_head % 2, 3 * NT * HEADS - 1, 3 * NT * HEADS)

                @block.tensor
                def _(pe):
                    def sums(t, slot, turn):
                        for h in range(HEADS):
                            n = t * HEADS + h
                            pe.wait_ge(scaled.sem, scaled.at(n + 1))
                            for c in range(NC):
                                last = pe.matmul(banks(st)[h * HD:(h + 1) * HD, c, :], message[:, h % 2, :], share[:, h % 2, c * CHUNK:(c + 1) * CHUNK],
                                                 start=isinstance(t, int) and t == 0, stop=isinstance(t, int) and t == NT - 1)
                            last.then_inc(spent.sem, 1)
                    in_ring(pe, R, sums)

            for slot in range(R):
                loaded[slot].passed(16 * len(range(slot, NT, R)))
            for s, n in ((exped, NT * HEADS), (shared, NT * HEADS), (scaled, NT * HEADS), (spent, NT * HEADS), (sig["dve"], 3 * NT * HEADS)):
                s.passed(n)
    empty_alone(nc, st, out)
    flip(nc, st, out, xt)
    on_vector(nc, st, lambda dve, link: link(dve.tensor_tensor(x[:, :], x[:, :], xt[:, :], ALU.add)))
    norm_rows(nc, st, x)


def isomorphism(nc, io, st):
    sig, x = st["sig"], st["x"]
    agg, ht = st["buf_a"], st["buf_b"]
    with nc.sbuf_tensor("gin_w", [P, 2, P], FP32) as w, nc.sbuf_tensor("gin_vecs", [P, 4], FP32) as vecs:
        params = sig["params"]
        with nc.Block() as block:
            @block.sync
            def _(sp):
                sp.dma_start(w[:, 0, :], io["L2_gnn_W1"]).then_inc(params.sem, 16)
                sp.dma_start(w[:, 1, :], io["L2_gnn_W2"]).then_inc(params.sem, 16)
                for i, name in enumerate(("L2_gnn_b1", "L2_gnn_gamma", "L2_gnn_beta", "L2_gnn_b2")):
                    sp.dma_start(vecs[:, i:i + 1], io[name].rearrange("(p a) -> p a", a=1)).then_inc(params.sem, 16)
                sp.wait_ge(params.sem, params.at(96))
        params.passed(96)
        spread(nc, st, st["C"], x, agg)
        flip(nc, st, x, ht)
        on_vector(nc, st, lambda dve, link: link(dve.tensor_tensor(agg[:, :], agg[:, :], ht[:, :], ALU.add)))
        linear(nc, st, [(w[:, 0, :], agg, P)], ht, bias=vecs[:, 0:1])
        norm_nodes(nc, st, ht, vecs[:, 1:2], vecs[:, 2:3])
        on_vector(nc, st, lambda dve, link: link(dve.tensor_scalar(ht[:, :], ht[:, :], 0.0, None, ALU.max)))
        linear(nc, st, [(w[:, 1, :], ht, P)], agg, bias=vecs[:, 3:4], func=ACT.Relu)
        flip(nc, st, agg, ht)
        on_vector(nc, st, lambda dve, link: link(dve.tensor_tensor(x[:, :], x[:, :], ht[:, :], ALU.add)))
        norm_rows(nc, st, x)


LAYERS = 3
UB = 13
WB = 2 + UB + 1


NAMES = ("Mb", "Ub", "bn_g", "bn_b", "mix_b", "ln_g", "ln_b")


class Layer:

    def __init__(self, wts, vecs, layer):
        self.wts, self.vecs, self.layer = wts, vecs, layer

    def weight(self, i):
        return self.wts[:, self.layer, i * P:(i + 1) * P]

    def vec(self, name):
        i = NAMES.index(name) * LAYERS + self.layer
        return self.vecs[:, i:i + 1]


def prepare_layers(nc, io, st):
    sig = st["sig"]
    GROUPS = LAYERS * WB // 4
    with ExitStack() as ctx:
        def sb(name, shape, dt=FP32):
            return ctx.enter_context(nc.sbuf_tensor(name, shape, dt))

        def sem(name):
            return ctx.enter_context(nc.semaphore("pre_" + name))
        raw = sb("raw_w", [P, LAYERS, WB * P])
        raw_vecs = sb("raw_vecs", [len(NAMES) * LAYERS, P])
        ends = sb("ends_rows", [NT, 2, P])
        scalers = sb("scaler_rows", [NT, 3, P])
        work = sb("ends_work", [NT, 3, P])
        no_edge_row = sb("no_edge_row", [1, 2, FEAT])
        s_ends, s_vecs, s_flat, s_wide, s_rest = (sem(n) for n in ("ends", "vecs", "scalers_stored", "scalers_in", "rest"))
        s_raw = [sem(f"raw{i}") for i in range(LAYERS)]
        s_turn, s_copy, s_chain, s_ready, s_log, s_fill = (sem(n) for n in ("turned", "copied", "chain", "ready", "log", "filled"))
        with nc.Block() as block:
            @block.sync
            def _(sp):
                for i, lo in enumerate((P, P - 1)):
                    sp.dma_start(ends[:, i, :], st["node_ends"][lo:lo + NP].rearrange("(t p) -> t p", p=P)).then_inc(s_ends, 16)
                for i, name in enumerate(NAMES):
                    sp.dma_start(raw_vecs[i * LAYERS:(i + 1) * LAYERS, :], io["L3_gnn_" + name]).then_inc(s_vecs, 16)
                for layer in range(LAYERS):
                    sp.dma_start(raw[:, layer, 0:2 * P], io["L3_gnn_Mw"][layer, :, :]).then_inc(s_raw[layer], 16)
                    sp.dma_start(raw[:, layer, 2 * P:(2 + UB) * P], io["L3_gnn_Uw"][layer, :, :]).then_inc(s_raw[layer], 16)
                    sp.dma_start(raw[:, layer, (2 + UB) * P:WB * P], io["L3_gnn_mix_w"][layer, :, :]).then_inc(s_raw[layer], 16)
                with nc.allow_non_contiguous_dma(reason="each edge tile's indices become a column"):
                    sp.dma_start(st["src_cols"][:, 0:ET], io["src_cols"]).then_inc(sig["src_in"].sem, 16)
                sp.wait_ge(s_ready, 2)
                sp.dma_start(st["scalers"].rearrange("i (t p) -> t i p", p=P), scalers[:, :, :]).then_inc(s_flat, 16)
                sp.wait_ge(s_flat, 16)
                for i, name in enumerate(("recip_deg", "amplify", "attenuate")):
                    sp.dma_start(st[name][:, :], st["scalers"][i:i + 1, :].to_broadcast((P, NP))).then_inc(s_wide, 16)
                sp.wait_ge(s_fill, 2)
                sp.dma_start(st["extremes"][EP:EP + 1, :], no_edge_row[:, :, :].rearrange("a i f -> a (i f)")).then_inc(s_rest, 16)
                sp.wait_ge(sig["src_in"].sem, 16)
                sp.wait_ge(s_wide, 48)
                sp.wait_ge(s_rest, 16)

            @block.gpsimd
            def _(pool):
                pool.memset(st["src_cols"][:, ET:ET + GU * TILES_IN], 0)
                pool.memset(no_edge_row[:, 0, :], -BIG).then_inc(s_fill, 1)
                pool.memset(no_edge_row[:, 1, :], BIG).then_inc(s_fill, 1)

            @block.vector
            def _(dve):
                link = Chain(dve, s_chain)
                dve.wait_ge(s_ends, 32)
                link(dve.tensor_tensor(work[:, 0, :], ends[:, 0, :], ends[:, 1, :], ALU.subtract))
                dve.tensor_scalar(work[:, 0, :], work[:, 0, :], 1.0, None, ALU.add).then_inc(s_ready, 1)
                link(dve.tensor_tensor(work[:, 1, :], ends[:, 0, :], ends[:, 1, :], ALU.is_equal))
                link(dve.tensor_scalar(work[:, 1, :], work[:, 1, :], float(EP), None, ALU.mult))
                link(dve.scalar_tensor_tensor(work[:, 2, :], ends[:, 0, :], -1.0, work[:, 1, :], ALU.add, ALU.max))
                dve.wait_ge(s_ready, 1)
                link(dve.reciprocal(scalers[:, 0, :], work[:, 0, :]))
                dve.wait_ge(s_log, 1)
                link(dve.tensor_scalar(scalers[:, 1, :], scalers[:, 1, :], 0.25, None, ALU.mult))
                dve.reciprocal(scalers[:, 2, :], scalers[:, 1, :]).then_inc(s_ready, 1)
                dve.wait_ge(s_turn, 2)
                link(dve.tensor_copy(st["vecs"][:, :], st["ps"][:, 6, 0:len(NAMES) * LAYERS]))
                link(dve.tensor_copy(st["last_edge"][:, :], st["ps"][:, 7, 0:NT]))

            @block.tensor
            def _(pe):
                pe.wait_ge(s_vecs, 16 * len(NAMES))
                n = len(NAMES) * LAYERS
                pe.transpose(st["ps"][:, 6, 0:n], raw_vecs[:, :], st["ident"][0:n, 0:n]).then_inc(s_turn, 1)
                pe.wait_ge(s_chain, 4)
                pe.transpose(st["ps"][:, 7, 0:NT], work[:, 2, :], st["ident"][0:NT, 0:NT]).then_inc(s_turn, 1)
                for n in range(GROUPS):
                    layer, b = divmod(n, WB // 4)
                    pe.wait_ge(s_raw[layer], 48)
                    if n >= 6:
                        pe.wait_ge(s_copy, n - 5)
                    for q in range(4):
                        last = pe.transpose(st["ps"][:, n % 6, q * P:(q + 1) * P], raw[:, layer, (4 * b + q) * P:(4 * b + q + 1) * P], st["ident"][:, :])
                    last.then_inc(s_turn, 1)

            @block.scalar
            def _(act):
                act.wait_ge(s_ready, 1)
                act.activation(scalers[:, 1, :], work[:, 0, :], ACT.Ln, bias=1.0).then_inc(s_log, 1)
                for n in range(GROUPS):
                    layer, b = divmod(n, WB // 4)
                    act.wait_ge(s_turn, 2 + n + 1)
                    act.copy(st["layer_w"][:, layer, 4 * b * P:4 * (b + 1) * P], st["ps"][:, n % 6, :]).then_inc(s_copy, 1)


GROUP = 4
NG = -(-NT // GROUP)


def group_tiles(k):
    return range(GROUP * k, min(GROUP * (k + 1), NT))


def group(buf, k):
    return buf[:, GROUP * k * P:min(GROUP * (k + 1), NT) * P]


def group_bank(st, bank, k):
    return st["ps"][:, bank, 0:len(group_tiles(k)) * P]


def enter_layer(nc, st, par, pn, pt, qt, update):
    sig, ht = st["sig"], st["h_t"]
    made, from_act, from_dve, stored = sig["used"], sig["from_act"], sig["dve"], sig["params"]
    with nc.Block() as block:
        def target(n):
            i, k = divmod(n, NG)
            return group((pn, pt, qt)[i], k), group_bank(st, n % 8, k)

        def copied(n):
            sem = (from_act, from_dve)[n % 2]
            return sem.sem, sem.at(n // 2 + 1)

        @block.tensor
        def _(pe):
            for n in range(3 * NG):
                i, k = divmod(n, NG)
                if n >= 8:
                    pe.wait_ge(*copied(n - 8))
                if i == 0:
                    for q, t in enumerate(group_tiles(k)):
                        last = pe.matmul(st["ps"][:, n % 8, q * P:(q + 1) * P], tile(ht, t), par.weight(0), start=True, stop=True)
                else:
                    last = pe.matmul(group_bank(st, n % 8, k), par.weight(i - 1), group(ht, k), start=True, stop=True)
                last.then_inc(made.sem, 1)

        @block.scalar
        def _(act):
            for n in range(0, 3 * NG, 2):
                act.wait_ge(made.sem, made.at(n + 1))
                to, bank = target(n)
                if n < 2 * NG:
                    act.copy(to, bank).then_inc(from_act.sem, 1)
                else:
                    act.activation(to, bank, ACT.Identity, bias=par.vec("Mb")).then_inc(from_act.sem, 1)

        @block.vector
        def _(dve):
            for n in range(1, 3 * NG, 2):
                dve.wait_ge(made.sem, made.at(n + 1))
                to, bank = target(n)
                if n < 2 * NG:
                    dve.tensor_copy(to, bank).then_inc(from_dve.sem, 1)
                else:
                    dve.tensor_scalar(to, bank, par.vec("Mb"), None, ALU.add).then_inc(from_dve.sem, 1)

        @block.gpsimd
        def _(pool):
            pool.memset(update[:, SPAN * SPANS:NP], 0.0)

        @block.sync
        def _(sp):
            for k in range(NG):
                sp.wait_ge(*copied(k))
                n = len(group_tiles(k)) * P
                sp.dma_start(st["P"][GROUP * k * P:GROUP * k * P + n, :].rearrange("(t p) f -> p t f", p=P),
                             group(pn, k).rearrange("p (t f) -> p t f", f=FEAT)).then_inc(stored.sem, 16)
            sp.wait_ge(stored.sem, stored.at(16 * NG))
    made.passed(3 * NG)
    from_act.passed(len(range(0, 3 * NG, 2)))
    from_dve.passed(len(range(1, 3 * NG, 2)))
    stored.passed(16 * NG)


TILES_IN = EI // P
GSTEPS = EP // EI
GU = 4
SPANS = 7
SPAN = -(-N_NODES // SPANS // 2) * 2
TURNS = GSTEPS // SPANS // GU
assert TURNS * GU * SPANS == GSTEPS and (TURNS - 1) * GU + 1 == NT and SPAN * SPANS <= NP


def extremes_and_sums(nc, st, layer, par, pn, pt, qt, update):
    with ExitStack() as ctx:
        def sb(name, shape, dt=FP32):
            return ctx.enter_context(nc.sbuf_tensor(f"{name}{layer}", shape, dt))

        def sem(name):
            return signal(nc, st, "g_" + name)
        idx = sb("gather_idx", [P, GU, TILES_IN], INT32)
        got = sb("gathered", [P, GU, TILES_IN, FEAT])
        spare = sb("spare", [P, 1])
        zeros = sb("spare_zeros", [P, 1])
        ahead = sb("spare_ahead", [P, GU])
        pen = sb("pen_rows", [P, 2, 2, 2 * EI], BF16)
        run = sb("running", [P, 2, 2, EI])
        rows = sb("run_rows", [P, GU, TILES_IN, 2, FEAT])
        counts = sb("span_counts", [P, GU, SPAN])
        mean = sb("span_mean", [P, SPAN])
        square = sb("span_square", [P, SPAN])
        var = sb("span_var", [P, SPAN])
        std = sb("span_std", [P, SPAN])
        amplified = sb("span_amplified", [P, SPAN])
        attenuated = sb("span_attenuated", [P, SPAN])
        both = sb("extremes_weights", [P, 3, P])
        powers = sb("powers", [P, 2, 2, FEAT])
        ps = st["ps"]
        IN, BACK, SUM = 0, 2, 6
        s_idx, s_scan, s_turn, s_back, s_rows, s_zero = (sem(n) for n in ("idx", "scanned", "turned", "turned_back", "rows", "zeroed"))
        s_pow, s_sum, s_span, s_std, s_part, s_both = (sem(n) for n in ("powers", "tile_summed", "span_chain", "span_std", "span_product", "weights_added"))
        TAKEN = 12

        def steps_before(span):
            return 0 if first(span) else TAKEN * span - 4
        s_got = [sem(f"gathered{i}") for i in range(GU)]
        s_pen = [sem(f"pen{i}") for i in range(2)]
        s_out = [sem(f"stored{i}") for i in range(GU)]
        s_cnt = [sem(f"counts{i}") for i in range(GU)]

        def first(*xs):
            return all(isinstance(x, int) and x == 0 for x in xs)

        def early(x, n):
            return isinstance(x, int) and x < n

        def steps(eng, body):
            def span(s):
                def turn(t):
                    for u in range(GU):
                        body(s, t, u, s * (TURNS * GU) + t * GU + u)
                turn(0)
                with eng.Fori(1, TURNS - 1) as t:
                    turn(t)
                turn(TURNS - 1)
            span(0)
            with eng.Fori(1, SPANS) as s:
                span(s)

        def has_sum(turn, u):
            return not (isinstance(turn, int) and turn == TURNS - 1 and u > 0)

        def over_span(buf, span):
            return buf[:, bass.ds(span * SPAN, SPAN)]

        def slot_loads(span, turn, u):
            return span * (TURNS if u == 0 else TURNS - 1) + turn + 1

        with nc.Block() as block:
            @block.gpsimd
            def _(pool):
                pool.memset(zeros[:, :], 0.0).then_inc(s_zero.sem, 1)
                pool.wait_ge(s_zero.sem, s_zero.at(1))

                def gather(span, turn, u, step):
                    pool.wait_ge(s_idx.sem, s_idx.at(step + 1))
                    if not early(step, 1):
                        pool.wait_ge(s_zero.sem, s_zero.at(step + 1))
                    pool.tensor_tensor(spare[:, :], zeros[:, :], zeros[:, :], ALU.add).then_inc(s_zero.sem, 1)
                    for q in range(TILES_IN):
                        pool.indirect_dma_start(out=got[:, u, q, :], out_offset=None, in_=st["P"],
                                                in_offset=bass.IndirectOffsetOnAxis(ap=idx[:, u, q:q + 1], axis=0)).then_inc(s_got[u].sem, 16)
                steps(pool, gather)

            @block.tensor
            def _(pe):
                def turn_back(step, parity):
                    pe.wait_ge(s_scan.sem, s_scan.at(step + 1))
                    if not early(step, 2):
                        pe.wait_ge(s_rows.sem, s_rows.at(2 * (step - 1)))
                    for i in range(2):
                        for q in range(TILES_IN):
                            last = pe.transpose(ps[:, BACK + 2 * parity + i, q * P:(q + 1) * P], run[:, parity, i, q * P:(q + 1) * P], st["ident"][:, :])
                    last.then_inc(s_back.sem, 1)

                def products(bank, terms):
                    for i, (weight, x) in enumerate(terms):
                        last = pe.matmul(ps[:, bank, 0:SPAN], weight, x, start=i == 0, stop=i == len(terms) - 1)
                    last.then_inc(s_part.sem, 1)

                def scaled_products(span):
                    q = over_span(qt, span)
                    pe.wait_ge(s_std.sem, s_std.at(span + 1))
                    products(SUM, ((par.weight(9), std[:, :]), (par.weight(10), var[:, :]), (both[:, 1, :], q)))
                    products(SUM + 1, ((par.weight(13), std[:, :]), (par.weight(14), var[:, :]), (both[:, 2, :], q)))

                def plain_products(span):
                    q = over_span(qt, span)
                    products(SUM, ((par.weight(2), over_span(st["h_t"], span)), (par.weight(5), std[:, :]), (par.weight(6), var[:, :]), (both[:, 0, :], q)))

                def work(span, turn, u, step):
                    if has_sum(turn, u):
                        n = span * NT + turn * GU + u
                        pe.wait_ge(s_cnt[u].sem, s_cnt[u].at(slot_loads(span, turn, u) * 16))
                        pe.wait_ge(s_pow.sem, s_pow.at(n + 1))
                        start = isinstance(turn, int) and turn == 0 and u == 0
                        if start and not first(span):
                            pe.wait_ge(s_span.sem, s_span.at(TAKEN * (span - 1) + 3))
                        for i in range(2):
                            last = pe.matmul(ps[:, SUM + i, 0:SPAN], powers[:, u % 2, i, :], counts[:, u, :], start=start,
                                             stop=isinstance(turn, int) and turn == TURNS - 1)
                        last.then_inc(s_sum.sem, 1)
                    pe.wait_ge(s_got[u].sem, s_got[u].at((span * TURNS + turn + 1) * 16 * TILES_IN))
                    if not early(step, 2):
                        pe.wait_ge(s_scan.sem, s_scan.at(step - 1))
                    for q in range(TILES_IN):
                        last = pe.transpose(ps[:, IN + u % 2, q * P:(q + 1) * P], got[:, u, q, :], st["ident"][:, :])
                    last.then_inc(s_turn.sem, 1)
                    if not early(step, 1):
                        turn_back(step - 1, (u - 1) % 2)
                    if not has_sum(turn, u) and not first(span):
                        if u == 2:
                            pe.wait_ge(s_span.sem, s_span.at(TAKEN * span - 1))
                            scaled_products(span - 1)
                        elif u == 3:
                            pe.wait_ge(s_span.sem, s_span.at(TAKEN * span))
                            plain_products(span - 1)
                pe.wait_ge(s_both.sem, s_both.at(3))
                steps(pe, work)
                turn_back(GSTEPS - 1, 1)
                scaled_products(SPANS - 1)
                pe.wait_ge(s_span.sem, s_span.at(TAKEN * SPANS - 3))
                plain_products(SPANS - 1)

            @block.vector
            def _(dve):
                def indices(step, u):
                    dve.tensor_copy(idx[:, u, :], st["src_cols"][:, bass.ds(step * TILES_IN, TILES_IN)]).then_inc(s_idx.sem, 1)

                for u in range(GU):
                    indices(u, u)
                for j in range(3):
                    dve.tensor_tensor(both[:, j, :], par.weight(3 + 4 * j), par.weight(4 + 4 * j), ALU.add).then_inc(s_both.sem, 1)

                def read_sums(span):
                    link = Chain(dve, s_span.sem, s_span.at(steps_before(span)))
                    p = over_span(pt, span)
                    dve.wait_ge(s_sum.sem, s_sum.at((span + 1) * NT))
                    link(dve.tensor_tensor(square[:, :], p, p, ALU.mult))
                    link(dve.tensor_tensor(mean[:, :], ps[:, SUM, 0:SPAN], p, ALU.add))
                    link(dve.tensor_tensor(square[:, :], ps[:, SUM + 1, 0:SPAN], square[:, :], ALU.add))

                def variance(span):
                    recip = over_span(st["recip_deg"], span)
                    link = Chain(dve, s_span.sem, s_span.at(TAKEN * span + 3))
                    link(dve.tensor_tensor(mean[:, :], mean[:, :], recip, ALU.mult))
                    link(dve.tensor_tensor(mean[:, :], mean[:, :], mean[:, :], ALU.mult))
                    link(dve.tensor_tensor(square[:, :], square[:, :], recip, ALU.mult))
                    link(dve.tensor_tensor(square[:, :], square[:, :], mean[:, :], ALU.subtract))
                    link(dve.tensor_scalar(var[:, :], square[:, :], 0.0, None, ALU.max))

                def take_scaled(span, before):
                    link = Chain(dve, s_span.sem, s_span.at(before))
                    dve.wait_ge(s_part.sem, s_part.at(3 * span + 1))
                    link(dve.tensor_tensor(amplified[:, :], ps[:, SUM, 0:SPAN], over_span(st["amplify"], span), ALU.mult))
                    dve.wait_ge(s_part.sem, s_part.at(3 * span + 2))
                    link(dve.tensor_tensor(attenuated[:, :], ps[:, SUM + 1, 0:SPAN], over_span(st["attenuate"], span), ALU.mult))
                    link(dve.tensor_tensor(amplified[:, :], amplified[:, :], attenuated[:, :], ALU.add))

                def take_plain(span, before):
                    link = Chain(dve, s_span.sem, s_span.at(before + 3))
                    dve.wait_ge(s_part.sem, s_part.at(3 * span + 3))
                    link(dve.scalar_tensor_tensor(over_span(update, span), ps[:, SUM, 0:SPAN], par.vec("Ub"), amplified[:, :], ALU.add, ALU.add))

                def scan(span, turn, u, step):
                    half = u // 2
                    if u % 2 == 0:
                        dve.wait_ge(s_pen[half].sem, s_pen[half].at((span * TURNS + turn + 1) * 16))
                    dve.wait_ge(s_turn.sem, s_turn.at(step + 1))
                    indices(step + GU, u)
                    if not early(step, 2):
                        dve.wait_ge(s_back.sem, s_back.at(step - 1))
                    for i, op in ((0, ALU.max), (1, ALU.min)):
                        if first(step):
                            start = 0.0
                        else:
                            dve.wait_ge(s_scan.sem, s_scan.at(step))
                            start = run[:, (u + 1) % 2, i, EI - 1:EI]
                        last = dve.tensor_tensor_scan(run[:, u % 2, i, :], pen[:, half, i, u % 2 * EI:(u % 2 + 1) * EI],
                                                      ps[:, IN + u % 2, :], start, ALU.add, op)
                    last.then_inc(s_scan.sem, 1)
                    if not has_sum(turn, u):
                        if u == 1:
                            read_sums(span)
                        elif u == 2:
                            if not first(span):
                                take_scaled(span - 1, TAKEN * span - 1)
                        else:
                            if not first(span):
                                take_plain(span - 1, TAKEN * span - 1)
                            variance(span)
                steps(dve, scan)
                take_scaled(SPANS - 1, TAKEN * SPANS - 4)
                take_plain(SPANS - 1, TAKEN * SPANS - 4)

            @block.scalar
            def _(act):
                def work(span, turn, u, step):
                    if has_sum(turn, u):
                        n = span * NT + turn * GU + u
                        if not early(n, 2):
                            act.wait_ge(s_sum.sem, s_sum.at(n - 1))
                            if isinstance(turn, int) and turn == 0 and u == 0:
                                act.wait_ge(s_sum.sem, s_sum.at(n))
                        tile_of_p = dyn_tile(pn, turn * GU + u)
                        act.copy(powers[:, u % 2, 0, :], tile_of_p)
                        act.activation(powers[:, u % 2, 1, :], tile_of_p, ACT.Square).then_inc(s_pow.sem, 1)
                    if not early(step, 2):
                        rows_out(step - 2, (u - 2) % GU, span * TURNS + turn + (0 if u >= 2 else -1))
                    if isinstance(turn, int) and turn == 0 and u == 2 and not first(span):
                        deviation(span - 1)

                def deviation(span):
                    act.wait_ge(s_span.sem, s_span.at(TAKEN * span + 8))
                    act.activation(std[:, :], var[:, :], ACT.Sqrt, bias=st["tiny_col"][:, 0:1]).then_inc(s_std.sem, 1)

                for u in range(GU):
                    act.copy(ahead[:, u:u + 1], st["tiny_col"][:, :]).then_inc(s_out[u].sem, 16)

                def rows_out(step, u, stores):
                    act.wait_ge(s_back.sem, s_back.at(step + 1))
                    act.wait_ge(s_out[u].sem, s_out[u].at(16 * (stores + 1)))
                    for i in range(2):
                        act.copy(rows[:, u, :, i, :], ps[:, BACK + 2 * (u % 2) + i, :].rearrange("p (q f) -> p q f", f=FEAT)).then_inc(s_rows.sem, 1)
                steps(act, work)
                for u in (GU - 2, GU - 1):
                    rows_out(GSTEPS - GU + u, u, GSTEPS // GU - 1)
                deviation(SPANS - 1)

            @block.sync
            def _(sp):
                def store(step, u):
                    sp.wait_ge(s_rows.sem, s_rows.at(2 * (step + 1)))
                    sp.dma_start(st["extremes"][bass.ds(step * EI, EI), :].rearrange("(q p) w -> p q w", p=P),
                                 rows[:, u, :, :, :].rearrange("p q i f -> p q (i f)")).then_inc(s_out[u].sem, 16)

                def work(span, turn, u, step):
                    if has_sum(turn, u):
                        if isinstance(turn, int) and turn == 0:
                            if not first(span):
                                sp.wait_ge(s_sum.sem, s_sum.at(span * NT if u == 0 else span * NT - GU + u))
                        else:
                            sp.wait_ge(s_sum.sem, s_sum.at(span * NT + turn * GU + u - GU + 1))
                        sp.dma_start(counts[:, u, :], st["C"][bass.ds(turn * GU + u, 1), :, bass.ds(span * SPAN, SPAN)].rearrange("a p n -> p (a n)")).then_inc(s_cnt[u].sem, 16)
                    if u % 2 == 0:
                        if not early(step, GU):
                            sp.wait_ge(s_scan.sem, s_scan.at(step - GU + 2))
                        sp.dma_start(pen[:, u // 2, :, :], st["pens"][:, bass.ds(step * EI, 2 * EI)].unsqueeze(0).to_broadcast((P, 2, 2 * EI))).then_inc(s_pen[u // 2].sem, 16)
                    if not early(step, LATE):
                        store(step - LATE, (u - LATE) % GU)
                LATE = 3
                steps(sp, work)
                for u in range(GU - LATE, GU):
                    store(GSTEPS - GU + u, u)
                for u in range(GU):
                    sp.wait_ge(s_out[u].sem, s_out[u].at(16 * (GSTEPS // GU + 1)))
        for signals, n in (((s_scan, s_turn, s_back), GSTEPS), ((s_rows,), 2 * GSTEPS), ((s_idx,), GSTEPS + GU), ((s_zero,), GSTEPS + 1), ((s_pow, s_sum), SPANS * NT),
                           ((s_span,), SPANS * TAKEN), ((s_std,), SPANS), ((s_part,), 3 * SPANS), ((s_both,), 3), (s_got, GSTEPS // GU * 16 * TILES_IN),
                           (s_pen, 16 * GSTEPS // GU), (s_out, 16 * (GSTEPS // GU + 1)), (s_cnt[:1], 16 * SPANS * TURNS), (s_cnt[1:], 16 * SPANS * (TURNS - 1))):
            for s in signals:
                s.passed(n)


def leave_layer(nc, st, par, p_rows, pt, update, spare):
    sig, ps, ht, ident = st["sig"], st["ps"], st["h_t"], st["ident"]
    layer = par.layer
    with ExitStack() as ctx:
        def sb(name, shape, dt=FP32):
            return ctx.enter_context(nc.sbuf_tensor(f"{name}{layer}", shape, dt))

        def sem(name):
            return signal(nc, st, "t_" + name)
        ends = sb("end_rows", [P, NT, 2, FEAT])
        extreme = sb("extreme", [P, 2, 2, GROUP * P])
        part = sb("scaled_part", [P, 2, GROUP * P])
        batch_stats = sb("batch_stats", [P, NG, 6])
        cols = sb("batch_cols", [P, 8])
        low = sb("elu_low", [P, 2, GROUP * P])
        power = sb("elu_power", [P, 2, GROUP * P])
        stats, moments, scale, shift = st["norm_stats"], st["norm_moments"], st["norm_scale"], st["norm_shift"]
        s_ends = [sem(f"ends{k}") for k in range(NG)]
        s_turned, s_extreme, s_product, s_taken = (sem(n) for n in ("ends_turned", "extreme", "product", "product_taken"))
        s_chain, s_batch, s_broot, s_affine, s_y, s_mixed, s_out = (sem(n) for n in ("chain", "batch_var", "batch_root", "affine", "y", "mixed", "mix_out"))
        s_res, s_nodes, s_nstat, s_ncopy, s_nvar, s_nroot, s_nscale = (sem(n) for n in ("residual", "node_major", "node_stats", "node_copy", "node_var", "node_root", "node_scale"))
        s_norm_a, s_norm_d, s_back, s_z, s_low, s_pow, s_elu = (sem(n) for n in ("normed_act", "normed_dve", "feature_major", "z", "low", "power", "elu"))

        def width(k):
            return len(group_tiles(k)) * P

        def bank(b, k):
            return group_bank(st, b, k)

        def normed_by(act_side, k):
            return len(range(0 if act_side else 1, group_tiles(k)[-1] + 1, 2))

        with nc.Block() as block:
            @block.gpsimd
            def _(pool):
                for k in range(NG):
                    for t in group_tiles(k):
                        pool.indirect_dma_start(out=ends[:, t, :, :].rearrange("p i f -> p (i f)"), out_offset=None, in_=st["extremes"],
                                                in_offset=bass.IndirectOffsetOnAxis(ap=st["last_edge"][:, t:t + 1], axis=0)).then_inc(s_ends[k].sem, 16)

            @block.tensor
            def _(pe):
                def turn_ends(k):
                    pe.wait_ge(s_ends[k].sem, s_ends[k].at(16 * len(group_tiles(k))))
                    if k >= 1:
                        pe.wait_ge(s_extreme.sem, s_extreme.at(k))
                    for i in range(2):
                        for q, t in enumerate(group_tiles(k)):
                            last = pe.transpose(ps[:, i, q * P:(q + 1) * P], ends[:, t, i, :], ident[:, :])
                    last.then_inc(s_turned.sem, 1)

                def multiply(k):
                    pe.wait_ge(s_extreme.sem, s_extreme.at(k + 1))
                    if k >= 2:
                        pe.wait_ge(s_taken.sem, s_taken.at(k - 1))
                    for j in range(3):
                        for i in range(2):
                            last = pe.matmul(bank(2 + 3 * (k % 2) + j, k), par.weight(3 + 4 * j + i), extreme[:, k % 2, i, 0:width(k)], start=i == 0, stop=i == 1)
                    last.then_inc(s_product.sem, 1)

                turn_ends(0)
                for k in range(NG):
                    if k + 1 < NG:
                        turn_ends(k + 1)
                    multiply(k)

                def mix(k):
                    pe.wait_ge(s_y.sem, s_y.at(k + 1))
                    if k >= 2:
                        pe.wait_ge(s_out.sem, s_out.at(k - 1))
                    pe.matmul(bank(k % 2, k), par.weight(WB - 1), group(pt, k), start=True, stop=True).then_inc(s_mixed.sem, 1)

                def to_nodes(k):
                    pe.wait_ge(s_res.sem, s_res.at(k + 1))
                    if k >= 2:
                        pe.wait_ge(s_ncopy.sem, s_ncopy.at(k - 1))
                    for q, t in enumerate(group_tiles(k)):
                        last = pe.transpose(ps[:, 2 + k % 2, q * P:(q + 1) * P], tile(ht, t), ident[:, :])
                    last.then_inc(s_nodes.sem, 1)

                mix(0)
                for k in range(NG):
                    if k + 1 < NG:
                        mix(k + 1)
                    to_nodes(k)

                for k in range(NG):
                    pe.wait_ge(s_norm_a.sem, s_norm_a.at(normed_by(True, k)))
                    pe.wait_ge(s_norm_d.sem, s_norm_d.at(normed_by(False, k)))
                    if k >= 2:
                        pe.wait_ge(s_z.sem, s_z.at(k - 1))
                    for q, t in enumerate(group_tiles(k)):
                        last = pe.transpose(ps[:, 4 + k % 2, q * P:(q + 1) * P], tile(update, t), ident[:, :])
                    last.then_inc(s_back.sem, 1)

            @block.vector
            def _(dve):
                link = Steps(dve, s_chain)

                def extremes(k):
                    dve.wait_ge(s_turned.sem, s_turned.at(k + 1))
                    if k >= 2:
                        dve.wait_ge(s_product.sem, s_product.at(k - 1))
                    dve.tensor_tensor(extreme[:, k % 2, 0, 0:width(k)], bank(0, k), group(pt, k), ALU.max)
                    dve.tensor_tensor(extreme[:, k % 2, 1, 0:width(k)], bank(1, k), group(pt, k), ALU.min).then_inc(s_extreme.sem, 1)

                def add_parts(k):
                    first_bank = 2 + 3 * (k % 2)
                    dve.wait_ge(s_product.sem, s_product.at(k + 1))
                    dve.tensor_tensor(part[:, 0, 0:width(k)], bank(first_bank + 1, k), group(st["amplify"], k), ALU.mult)
                    dve.tensor_tensor(part[:, 1, 0:width(k)], bank(first_bank + 2, k), group(st["attenuate"], k), ALU.mult)
                    dve.tensor_tensor(group(update, k), group(update, k), bank(first_bank, k), ALU.add).then_inc(s_taken.sem, 1)
                    dve.wait_ge(s_taken.sem, s_taken.at(k + 1))
                    link(dve.tensor_tensor(part[:, 0, 0:width(k)], part[:, 0, 0:width(k)], part[:, 1, 0:width(k)], ALU.add))
                    link(dve.tensor_tensor(group(update, k), group(update, k), part[:, 0, 0:width(k)], ALU.add))
                    link(dve.bn_stats(out=batch_stats[:, k, :], in_=update[:, GROUP * k * P:min(GROUP * (k + 1) * P, N_NODES)]))

                extremes(0)
                for k in range(NG):
                    if k + 1 < NG:
                        extremes(k + 1)
                    add_parts(k)

                mean, var, root, inv, mult, back, add = (cols[:, i:i + 1] for i in range(7))
                link(dve.bn_aggr(out=cols[:, 0:2], in_=batch_stats[:, :, :].rearrange("p k s -> p (k s)")))
                dve.tensor_scalar(root, var, 1.0 / N_NODES, 1e-5, ALU.mult, ALU.add).then_inc(s_batch.sem, 1)
                dve.wait_ge(s_broot.sem, s_broot.at(1))
                link(dve.reciprocal(inv, root))
                link(dve.tensor_scalar(mult, inv, par.vec("bn_g"), (1.0 / N_NODES) ** 0.5, ALU.mult, ALU.mult))
                link(dve.tensor_tensor(back, mean, mult, ALU.mult))
                dve.tensor_tensor(add, par.vec("bn_b"), back, ALU.subtract).then_inc(s_affine.sem, 1)

                def residual(k):
                    dve.wait_ge(s_out.sem, s_out.at(k + 1))
                    link(dve.scalar_tensor_tensor(group(spare, k), group(spare, k), 0.01, group(spare, k), ALU.mult, ALU.max))
                    dve.tensor_tensor(group(ht, k), group(ht, k), group(spare, k), ALU.add).then_inc(s_res.sem, 1)

                def node_stats(k):
                    dve.wait_ge(s_ncopy.sem, s_ncopy.at(k + 1))
                    for t in group_tiles(k):
                        last = dve.bn_stats(out=stats[:, t, :], in_=tile(update, t))
                    last.then_inc(s_nstat.sem, 1)
                    dve.wait_ge(s_nstat.sem, s_nstat.at(k + 1))
                    for t in group_tiles(k):
                        last = dve.bn_aggr(out=moments[:, t, :], in_=stats[:, t, :])
                    return last

                residual(0)
                for k in range(NG):
                    if k + 1 < NG:
                        residual(k + 1)
                    last = node_stats(k)
                last.then_inc(s_nvar.sem, 1)
                dve.wait_ge(s_nroot.sem, s_nroot.at(1))
                link(dve.reciprocal(scale[:, :], scale[:, :]))
                dve.scalar_tensor_tensor(shift[:, :], moments[:, :, 0], -1.0, scale[:, :], ALU.mult, ALU.mult).then_inc(s_nscale.sem, 1)
                dve.wait_ge(s_nscale.sem, s_nscale.at(1))

                def normalise(k):
                    for t in group_tiles(k):
                        if t % 2 == 1:
                            dve.tensor_scalar(tile(update, t), tile(update, t), scale[:, t:t + 1], shift[:, t:t + 1], ALU.mult, ALU.add).then_inc(s_norm_d.sem, 1)

                def lower(k):
                    dve.wait_ge(s_z.sem, s_z.at(k + 1))
                    if k >= 2:
                        dve.wait_ge(s_pow.sem, s_pow.at(k - 1))
                    dve.tensor_scalar(low[:, k % 2, 0:width(k)], group(p_rows, k), 0.0, None, ALU.min).then_inc(s_low.sem, 1)
                    link(dve.tensor_scalar(group(p_rows, k), group(p_rows, k), 0.0, -1.0, ALU.max, ALU.add))

                def elu(k):
                    dve.wait_ge(s_pow.sem, s_pow.at(k + 1))
                    dve.tensor_tensor(group(ht, k), power[:, k % 2, 0:width(k)], group(p_rows, k), ALU.add).then_inc(s_elu.sem, 1)

                normalise(0)
                normalise(1)
                for k in range(NG):
                    if k + 2 < NG:
                        normalise(k + 2)
                    lower(k)
                    if k >= 1:
                        elu(k - 1)
                elu(NG - 1)
                link.done()

            @block.scalar
            def _(act):
                act.wait_ge(s_batch.sem, s_batch.at(1))
                act.activation(cols[:, 2:3], cols[:, 2:3], ACT.Sqrt).then_inc(s_broot.sem, 1)
                act.wait_ge(s_affine.sem, s_affine.at(1))

                def affine(k):
                    act.activation(group(pt, k), group(update, k), ACT.Identity, bias=cols[:, 6:7], scale=cols[:, 4:5]).then_inc(s_y.sem, 1)

                def mix_out(k):
                    act.wait_ge(s_mixed.sem, s_mixed.at(k + 1))
                    act.activation(group(spare, k), bank(k % 2, k), ACT.Identity, bias=par.vec("mix_b")).then_inc(s_out.sem, 1)

                def node_copy(k):
                    act.wait_ge(s_nodes.sem, s_nodes.at(k + 1))
                    act.wait_ge(s_y.sem, s_y.at(k + 1))
                    act.copy(group(update, k), bank(2 + k % 2, k)).then_inc(s_ncopy.sem, 1)

                affine(0)
                affine(1)
                for k in range(NG):
                    if k + 2 < NG:
                        affine(k + 2)
                    mix_out(k)
                    if k >= 1:
                        node_copy(k - 1)
                node_copy(NG - 1)
                act.wait_ge(s_nvar.sem, s_nvar.at(1))
                act.activation(scale[:, :], moments[:, :, 1], ACT.Sqrt, bias=st["eps_col"][:, 0:1]).then_inc(s_nroot.sem, 1)
                act.wait_ge(s_nscale.sem, s_nscale.at(1))
                act.wait_ge(s_ncopy.sem, s_ncopy.at(NG))

                def normalise(k):
                    for t in group_tiles(k):
                        if t % 2 == 0:
                            act.activation(tile(update, t), tile(update, t), ACT.Identity, bias=shift[:, t:t + 1], scale=scale[:, t:t + 1]).then_inc(s_norm_a.sem, 1)

                def gain(k):
                    act.wait_ge(s_back.sem, s_back.at(k + 1))
                    act.activation(group(p_rows, k), bank(4 + k % 2, k), ACT.Identity, bias=par.vec("ln_b"), scale=par.vec("ln_g")).then_inc(s_z.sem, 1)

                def exponential(k):
                    act.wait_ge(s_low.sem, s_low.at(k + 1))
                    if k >= 2:
                        act.wait_ge(s_elu.sem, s_elu.at(k - 1))
                    act.activation(power[:, k % 2, 0:width(k)], low[:, k % 2, 0:width(k)], ACT.Exp).then_inc(s_pow.sem, 1)

                normalise(0)
                normalise(1)
                for k in range(NG):
                    if k + 2 < NG:
                        normalise(k + 2)
                    gain(k)
                    if k >= 1:
                        exponential(k - 1)
                exponential(NG - 1)
        for k in range(NG):
            s_ends[k].passed(16 * len(group_tiles(k)))
        for s in (s_turned, s_extreme, s_product, s_taken, s_y, s_mixed, s_out, s_res, s_nodes, s_nstat, s_ncopy, s_back, s_z, s_low, s_pow, s_elu):
            s.passed(NG)
        for s in (s_batch, s_broot, s_affine, s_nvar, s_nroot, s_nscale):
            s.passed(1)
        s_norm_a.passed(normed_by(True, NG - 1))
        s_norm_d.passed(normed_by(False, NG - 1))


def principal_layer(nc, st, layer):
    par = Layer(st["layer_w"], st["vecs"], layer)
    qt = st["norm_work"]
    with nc.sbuf_tensor(f"p_n{layer}", [P, NP], FP32) as pn, nc.sbuf_tensor(f"p_t{layer}", [P, NP], FP32) as pt, \
            nc.sbuf_tensor(f"update{layer}", [P, NP], FP32) as update:
        enter_layer(nc, st, par, pn, pt, qt, update)
        extremes_and_sums(nc, st, layer, par, pn, pt, qt, update)
        leave_layer(nc, st, par, pn, pt, update, qt)


def finish(nc, st, out):
    x, ht, ps = st["x"], st["h_t"], st["ps"]
    stats, moments, scale, shift = st["norm_stats"], st["norm_moments"], st["norm_scale"], st["norm_shift"]
    with ExitStack() as ctx:
        def sem(name):
            return ctx.enter_context(nc.semaphore("out_" + name))
        s_turned, s_added, s_stat, s_var, s_root, s_inv, s_scale, s_act, s_dve, s_store = (
            sem(n) for n in ("turned", "added", "stats", "var", "root", "inverse", "scale", "normed_act", "normed_dve", "stored"))
        with nc.Block() as block:
            @block.tensor
            def _(pe):
                for k in range(NG):
                    for q, t in enumerate(group_tiles(k)):
                        last = pe.transpose(ps[:, k, q * P:(q + 1) * P], tile(ht, t), st["ident"][:, :])
                    last.then_inc(s_turned, 1)

            @block.vector
            def _(dve):
                for k in range(NG):
                    dve.wait_ge(s_turned, k + 1)
                    dve.tensor_tensor(group(x, k), group(x, k), group_bank(st, k, k), ALU.add).then_inc(s_added, 1)
                    dve.wait_ge(s_added, k + 1)
                    for t in group_tiles(k):
                        last = dve.bn_stats(out=stats[:, t, :], in_=tile(x, t))
                    last.then_inc(s_stat, 1)
                    dve.wait_ge(s_stat, k + 1)
                    for t in group_tiles(k):
                        last = dve.bn_aggr(out=moments[:, t, :], in_=stats[:, t, :])
                last.then_inc(s_var, 1)
                dve.wait_ge(s_root, 1)
                dve.reciprocal(scale[:, :], scale[:, :]).then_inc(s_inv, 1)
                dve.wait_ge(s_inv, 1)
                dve.scalar_tensor_tensor(shift[:, :], moments[:, :, 0], -1.0, scale[:, :], ALU.mult, ALU.mult).then_inc(s_scale, 1)
                dve.wait_ge(s_scale, 1)
                for t in range(1, NT, 2):
                    dve.tensor_scalar(tile(x, t), tile(x, t), scale[:, t:t + 1], shift[:, t:t + 1], ALU.mult, ALU.add).then_inc(s_dve, 1)

            @block.scalar
            def _(act):
                act.wait_ge(s_var, 1)
                act.activation(scale[:, :], moments[:, :, 1], ACT.Sqrt, bias=st["eps_col"][:, 0:1]).then_inc(s_root, 1)
                act.wait_ge(s_scale, 1)
                for t in range(0, NT, 2):
                    act.activation(tile(x, t), tile(x, t), ACT.Identity, bias=shift[:, t:t + 1], scale=scale[:, t:t + 1]).then_inc(s_act, 1)

            @block.sync
            def _(sp):
                full = N_NODES // P
                half = full // 2
                stores = 0
                for lo, hi in ((0, half), (half, full)):
                    sp.wait_ge(s_act, len(range(0, hi, 2)))
                    sp.wait_ge(s_dve, len(range(1, hi, 2)))
                    sp.dma_start(out[lo * P:hi * P, :].rearrange("(t p) f -> p t f", p=P), over_features(x)[:, lo:hi, :]).then_inc(s_store, 16)
                    stores += 1
                if N_NODES > full * P:
                    sp.wait_ge(s_act, len(range(0, NT, 2)))
                    sp.wait_ge(s_dve, len(range(1, NT, 2)))
                    sp.dma_start(out[full * P:N_NODES, :], x[0:N_NODES - full * P, full * P:NP]).then_inc(s_store, 16)
                    stores += 1
                sp.wait_ge(s_store, 16 * stores)


RING = 3


def program(nc, io, out, kind="Internal"):
    st = {"signals": {}}

    def dram(name, shape, dt=FP32):
        st[name] = nc.dram_tensor(name, shape, dt, kind=kind).ap()
    dram("win_ends", [2 * P], INT32)
    dram("node_ends", [P + NP])
    dram("pens", [2, EP], BF16)
    dram("C", [NT, P, NP])
    dram("AT", [NT, P, NP])
    dram("P", [NP, FEAT])
    dram("extremes", [EP + 1, 2 * FEAT])
    dram("scalers", [3, NP])
    with ExitStack() as ctx:
        st["keep"] = ctx
        def sb(name, shape, dt=FP32):
            st[name] = ctx.enter_context(nc.sbuf_tensor(name, shape, dt))
        sb("ident", [P, P])
        sb("cell_iota", [P, CELLS], FP16)
        sb("last_edge", [P, NT], INT32)
        sb("ends_row", [1, NWIN + 2], INT32)
        for name in ("big_col", "tiny_col", "eps_col"):
            sb(name, [P, 1])
        with nc.sbuf_tensor("steps", [P, 3, SG * P], FP32) as steps:
            st["steps"] = steps
            windows_and_steps(nc, io, st)
            build_adjacency(nc, st)
        for name, shape in (("x", [P, NP]), ("norm_work", [P, NP]), ("norm_stats", [P, NT, 6]), ("norm_moments", [P, NT, 2]),
                            ("norm_scale", [P, NT]), ("norm_shift", [P, NT]), ("node_cols", [P, 5])):
            sb(name, shape)
        sb("stat", [P, RING, P])
        st["ps"] = ctx.enter_context(nc.psum_tensor("ps", [P, 8, 512], FP32))
        sig = st["sig"] = {k: Signal(ctx.enter_context(nc.semaphore("sig_" + k))) for k in
                           ("used", "picked", "out", "turned", "to_act", "from_act", "params", "dve", "act", "pooled", "shared", "scaled", "src_in")}
        sig["loaded"] = [Signal(ctx.enter_context(nc.semaphore(f"sig_loaded{i}"))) for i in range(RING)]

        def fill(dve, link):
            for name, value in (("big_col", BIG), ("tiny_col", 1e-30), ("eps_col", 1e-5)):
                link(dve.memset(st[name][:, :], value))
        on_vector(nc, st, fill)
        with nc.sbuf_tensor("buf_a", [P, NP], FP32) as a, nc.sbuf_tensor("buf_b", [P, NP], FP32) as b, nc.sbuf_tensor("ring", [P, RING, NP], FP32) as ring:
            st["buf_a"], st["buf_b"], st["ring"] = a, b, ring
            with nc.sbuf_tensor("buf_c", [P, NP], FP32) as c:
                st["buf_c"] = c
                light_hops(nc, io, st)
            attention(nc, io, st)
            isomorphism(nc, io, st)
        for name, shape in (("recip_deg", [P, NP]), ("amplify", [P, NP]), ("attenuate", [P, NP]), ("h_t", [P, NP]),
                            ("layer_w", [P, LAYERS, WB * P]), ("vecs", [P, len(NAMES) * LAYERS])):
            sb(name, shape)
        sb("src_cols", [P, ET + GU * TILES_IN], INT32)
        prepare_layers(nc, io, st)
        flip(nc, st, st["x"], st["h_t"])
        for layer in range(LAYERS):
            principal_layer(nc, st, layer)
        finish(nc, st, out)


_PARAMS = ["L1_gnn_W", "L1_gnn_b", "L1_gnn_att_src", "L1_gnn_att_dst", "L2_gnn_W1", "L2_gnn_b1", "L2_gnn_gamma", "L2_gnn_beta",
           "L2_gnn_W2", "L2_gnn_b2", "L3_gnn_Mw", "L3_gnn_Mb", "L3_gnn_Uw", "L3_gnn_Ub", "L3_gnn_bn_g", "L3_gnn_bn_b",
           "L3_gnn_mix_w", "L3_gnn_mix_b", "L3_gnn_ln_g", "L3_gnn_ln_b"]


def layouts(inputs):
    import numpy as np
    pad = EP - N_EDGES
    src = np.concatenate([np.asarray(inputs["src"]), np.zeros(pad, np.int32)])
    dst = np.concatenate([np.asarray(inputs["dst"]), np.full(pad, NP, np.int32)])
    weight = np.concatenate([np.asarray(inputs["edge_weight"]), np.zeros(pad, np.float32)])
    x = np.concatenate([np.asarray(inputs["x"]), np.zeros((NP - N_NODES, FEAT), np.float32)])
    arrays = {
        "x_pad": x,
        "dst_pad": np.concatenate([np.full(1, -1, np.int32), dst]),
        "dst_last": np.ascontiguousarray(dst.reshape(ET, P)[:, P - 1:].reshape(1, ET)),
        "dst_tiles": dst.reshape(ET, P),
        "src_tiles": src.reshape(ET, P),
        "src_cols": np.ascontiguousarray(src.reshape(ET, P).T),
        "wgt_tiles": weight.reshape(ET, P),
    }
    for name in _PARAMS:
        arrays[name] = np.ascontiguousarray(inputs[name])
    return arrays


def kernel(**inputs):
    import concourse.bacc as _bacc
    from concourse.bass_utils import run_bass_kernel_spmd as _run

    nc = _bacc.Bacc("TRN2", target_bir_lowering=False, num_devices=1)
    arrays = layouts(inputs)
    io = {name: nc.dram_tensor("in_" + name, list(a.shape), mybir.dt.from_np(a.dtype), kind="ExternalInput").ap() for name, a in arrays.items()}
    out = nc.dram_tensor("out", [N_NODES, FEAT], FP32, kind="ExternalOutput").ap()
    program(nc, io, out)
    r = _run(nc, [{"in_" + name: a for name, a in arrays.items()}], core_ids=[0])
    return r.results[0]["out"]
```
